# Optimizing a Trainium2 kernel written in Bass

```python
import numpy as np
import jax
import jax.numpy as jnp

def _softmax(x, axis=-1):
    return jax.nn.softmax(x, axis=axis)

def _gelu(x):
    return jax.nn.gelu(x, approximate=True)

def _silu(x):
    return jax.nn.silu(x)

def _sigmoid(x):
    return jax.nn.sigmoid(x)

def _layernorm(x, axis=-1, eps=1e-05):
    m = jnp.mean(x, axis=axis, keepdims=True)
    v = jnp.var(x, axis=axis, keepdims=True)
    return (x - m) / jnp.sqrt(v + eps)

def _scatter_add(tgt, idx, src, axis=0):
    return tgt.at[idx].add(src)

def _segment_sum(src, seg, n):
    return jax.ops.segment_sum(src, seg, n)
kernel_name = 'mk_gnn_preln_d4_gnn_r8_138725'

def setup_inputs(seed: int=0):
    np.random.seed(seed)
    _w = jnp.asarray

    def _rec_inputs():
        import jax
        import jax.numpy as jnp
        _gk = jax.random.key(seed)
        x = -0.0005121 + 1.001 * jax.random.normal(jax.random.fold_in(_gk, 1), (6250, 64), jnp.float32)
        src = jax.random.randint(jax.random.fold_in(_gk, 2), (200000,), 0, 6250, jnp.int32)
        dst = jax.random.randint(jax.random.fold_in(_gk, 3), (200000,), 0, 6250, jnp.int32)
        _o = jnp.argsort(dst, stable=True)
        src = src[_o]
        dst = dst[_o]
        edge_attr_5 = -0.000192005 + 0.999979 * jax.random.normal(jax.random.fold_in(_gk, 12), (200000, 5), jnp.float32)
        return (x, src, dst, edge_attr_5)
    x, src, dst, edge_attr_5 = _rec_inputs()

    def _L0_gnn_setup():
        import jax, jax.numpy as jnp
        import numpy as np
        H, C = (3, 64)
        NEG_SLOPE = 0.2
        LN_EPS = 1e-05

        def layer_norm(x, g, b):
            m = jnp.mean(x, axis=-1, keepdims=True)
            v = jnp.mean((x - m) ** 2, axis=-1, keepdims=True)
            return (x - m) * jax.lax.rsqrt(v + LN_EPS) * g + b

        def gat_conv(x, edge_index, edge_attr, lin_w, att_src, att_dst, lin_edge_w, att_edge, gat_bias):
            N = x.shape[0]
            src, dst = (edge_index[0], edge_index[1])
            attr_sum = jax.ops.segment_sum(edge_attr, dst, num_segments=N)
            cnt = jax.ops.segment_sum(jnp.ones((dst.shape[0],), edge_attr.dtype), dst, num_segments=N)
            loop_attr = attr_sum / jnp.maximum(cnt, 1.0)[:, None]
            loop = jnp.arange(N, dtype=src.dtype)
            src = jnp.concatenate([src, loop])
            dst = jnp.concatenate([dst, loop])
            ea = jnp.concatenate([edge_attr, loop_attr], axis=0)
            xs = (x @ lin_w).reshape(N, H, C)
            a_src = jnp.einsum('nhc,hc->nh', xs, att_src)
            a_dst = jnp.einsum('nhc,hc->nh', xs, att_dst)
            e = (ea @ lin_edge_w).reshape(-1, H, C)
            a_edge = jnp.einsum('ehc,hc->eh', e, att_edge)
            logits = a_src[src] + a_dst[dst] + a_edge
            logits = jnp.where(logits >= 0, logits, NEG_SLOPE * logits)
            lmax = jax.ops.segment_max(logits, dst, num_segments=N)
            ex = jnp.exp(logits - lmax[dst])
            denom = jax.ops.segment_sum(ex, dst, num_segments=N)
            alpha = ex / denom[dst]
            msgs = alpha[:, :, None] * xs[src]
            out = jax.ops.segment_sum(msgs, dst, num_segments=N)
            return out.reshape(N, H * C) + gat_bias
        key = jax.random.key(seed)
        ks = jax.random.split(key, 20)
        N, E, D_in, edge_dim = (6250, 100000, 64, 5)
        g = lambda k, shape: jax.random.normal(k, shape, dtype=jnp.float32) * 0.1
        return {'x': jax.random.normal(ks[0], (N, D_in), dtype=jnp.float32), 'edge_attr': jax.random.normal(ks[1], (E, edge_dim), dtype=jnp.float32), 'lin_w': g(ks[2], (D_in, H * C)), 'att_src': g(ks[3], (H, C)), 'att_dst': g(ks[4], (H, C)), 'lin_edge_w': g(ks[5], (edge_dim, H * C)), 'att_edge': g(ks[6], (H, C)), 'gat_bias': jnp.zeros((H * C,), jnp.float32), 'w1': g(ks[7], (H * C, C)), 'b1': jnp.zeros((C,), jnp.float32), 'ln1_g': jnp.ones((C,), jnp.float32), 'ln1_b': jnp.zeros((C,), jnp.float32), 'w2': g(ks[8], (C, C)), 'b2': jnp.zeros((C,), jnp.float32), 'ln2_g': jnp.ones((C,), jnp.float32), 'ln2_b': jnp.zeros((C,), jnp.float32), 'edge_index': jax.random.randint(ks[9], (2, E), 0, N)}
    _L0_gnn_all = _L0_gnn_setup()
    _L0_gnn_in = {k: v for k, v in _L0_gnn_all.items() if k in ('lin_w', 'att_src', 'att_dst', 'lin_edge_w', 'att_edge', 'gat_bias', 'w1', 'b1', 'ln1_g', 'ln1_b', 'w2', 'b2', 'ln2_g', 'ln2_b')}
    del _L0_gnn_all

    def _L1_gnn_setup():
        import jax, jax.numpy as jnp
        import numpy as np
        NUM_LAYERS = 3

        def _lightgcn_layer(x, src, dst, num_nodes):
            msgs = x[src]
            summed = jax.ops.segment_sum(msgs, dst, num_segments=num_nodes)
            counts = jax.ops.segment_sum(jnp.ones((src.shape[0],), x.dtype), dst, num_segments=num_nodes)
            denom = jnp.maximum(counts, 1.0)
            return summed / denom[:, None]
        key = jax.random.key(seed)
        k1, k2, k3 = jax.random.split(key, 3)
        N, D, E = (6250, 64, 100000)
        x = jax.random.normal(k1, (N, D), dtype=jnp.float32)
        src = jax.random.randint(k2, (E,), 0, N)
        dst = jax.random.randint(k3, (E,), 0, N)
        edge_index = jnp.stack([src, dst], axis=0).astype(jnp.int64)
        return {'x': x, 'edge_index': edge_index}
    _L1_gnn_all = _L1_gnn_setup()
    _L1_gnn_in = {k: v for k, v in _L1_gnn_all.items() if k in ()}
    del _L1_gnn_all

    def _L2_gnn_setup():
        import jax, jax.numpy as jnp
        import numpy as np
        N_NODES = 12500
        N_EDGES = 200000
        IN_CH = 64
        OUT_CH = 64
        key = jax.random.key(seed)
        ks = jax.random.split(key, 6)
        x = jax.random.normal(ks[0], (N_NODES, IN_CH), dtype=jnp.float32)
        edge_index = jax.random.randint(ks[1], (2, N_EDGES), 0, N_NODES, dtype=jnp.int64)
        W1 = jax.random.normal(ks[2], (2 * IN_CH, OUT_CH), dtype=jnp.float32) * (1.0 / np.sqrt(2 * IN_CH))
        b1 = jnp.zeros((OUT_CH,), dtype=jnp.float32)
        W2 = jax.random.normal(ks[3], (OUT_CH, OUT_CH), dtype=jnp.float32) * (1.0 / np.sqrt(OUT_CH))
        b2 = jnp.zeros((OUT_CH,), dtype=jnp.float32)
        return {'x': x, 'edge_index': edge_index, 'W1': W1, 'b1': b1, 'W2': W2, 'b2': b2}
    _L2_gnn_all = _L2_gnn_setup()
    _L2_gnn_in = {k: v for k, v in _L2_gnn_all.items() if k in ('W1', 'b1', 'W2', 'b2')}
    del _L2_gnn_all

    def _L3_gnn_setup():
        import jax, jax.numpy as jnp
        import numpy as np
        N_NODES = 12500
        N_EDGES = 200000
        D_IN = 64
        D_OUT = 64
        key = jax.random.key(seed)
        k1, k2, k3, k4 = jax.random.split(key, 4)
        feat = jax.random.normal(k1, (N_NODES, D_IN), dtype=jnp.float32)
        edge_src = jax.random.randint(k2, (N_EDGES,), 0, N_NODES, dtype=jnp.int64)
        edge_dst = jax.random.randint(k3, (N_EDGES,), 0, N_NODES, dtype=jnp.int64)
        gain = float(np.sqrt(2.0))
        limit = gain * float(np.sqrt(6.0 / (D_IN + D_OUT)))
        fc_weight = jax.random.uniform(k4, (D_OUT, D_IN), dtype=jnp.float32, minval=-limit, maxval=limit)
        return {'feat': feat, 'edge_src': edge_src, 'edge_dst': edge_dst, 'fc_weight': fc_weight}
    _L3_gnn_all = _L3_gnn_setup()
    _L3_gnn_in = {k: v for k, v in _L3_gnn_all.items() if k in ('fc_weight',)}
    del _L3_gnn_all
    return {'x': x, 'src': src, 'dst': dst, 'edge_attr_5': edge_attr_5, 'L0_gnn_lin_w': _L0_gnn_in['lin_w'], 'L0_gnn_att_src': _L0_gnn_in['att_src'], 'L0_gnn_att_dst': _L0_gnn_in['att_dst'], 'L0_gnn_lin_edge_w': _L0_gnn_in['lin_edge_w'], 'L0_gnn_att_edge': _L0_gnn_in['att_edge'], 'L0_gnn_gat_bias': _L0_gnn_in['gat_bias'], 'L0_gnn_w1': _L0_gnn_in['w1'], 'L0_gnn_b1': _L0_gnn_in['b1'], 'L0_gnn_ln1_g': _L0_gnn_in['ln1_g'], 'L0_gnn_ln1_b': _L0_gnn_in['ln1_b'], 'L0_gnn_w2': _L0_gnn_in['w2'], 'L0_gnn_b2': _L0_gnn_in['b2'], 'L0_gnn_ln2_g': _L0_gnn_in['ln2_g'], 'L0_gnn_ln2_b': _L0_gnn_in['ln2_b'], 'L2_gnn_W1': _L2_gnn_in['W1'], 'L2_gnn_b1': _L2_gnn_in['b1'], 'L2_gnn_W2': _L2_gnn_in['W2'], 'L2_gnn_b2': _L2_gnn_in['b2'], 'L3_gnn_fc_weight': _L3_gnn_in['fc_weight']}

def reference(x, src, dst, edge_attr_5, L0_gnn_lin_w, L0_gnn_att_src, L0_gnn_att_dst, L0_gnn_lin_edge_w, L0_gnn_att_edge, L0_gnn_gat_bias, L0_gnn_w1, L0_gnn_b1, L0_gnn_ln1_g, L0_gnn_ln1_b, L0_gnn_w2, L0_gnn_b2, L0_gnn_ln2_g, L0_gnn_ln2_b, L2_gnn_W1, L2_gnn_b1, L2_gnn_W2, L2_gnn_b2, L3_gnn_fc_weight):
    import jax
    import jax.numpy as jnp

    def _L0_gnn_ref(x, edge_attr, lin_w, att_src, att_dst, lin_edge_w, att_edge, gat_bias, w1, b1, ln1_g, ln1_b, w2, b2, ln2_g, ln2_b, edge_index):
        import jax, jax.numpy as jnp
        import numpy as np
        H, C = (3, 64)
        NEG_SLOPE = 0.2
        LN_EPS = 1e-05

        def layer_norm(x, g, b):
            m = jnp.mean(x, axis=-1, keepdims=True)
            v = jnp.mean((x - m) ** 2, axis=-1, keepdims=True)
            return (x - m) * jax.lax.rsqrt(v + LN_EPS) * g + b

        def gat_conv(x, edge_index, edge_attr, lin_w, att_src, att_dst, lin_edge_w, att_edge, gat_bias):
            N = x.shape[0]
            src, dst = (edge_index[0], edge_index[1])
            attr_sum = jax.ops.segment_sum(edge_attr, dst, num_segments=N)
            cnt = jax.ops.segment_sum(jnp.ones((dst.shape[0],), edge_attr.dtype), dst, num_segments=N)
            loop_attr = attr_sum / jnp.maximum(cnt, 1.0)[:, None]
            loop = jnp.arange(N, dtype=src.dtype)
            src = jnp.concatenate([src, loop])
            dst = jnp.concatenate([dst, loop])
            ea = jnp.concatenate([edge_attr, loop_attr], axis=0)
            xs = (x @ lin_w).reshape(N, H, C)
            a_src = jnp.einsum('nhc,hc->nh', xs, att_src)
            a_dst = jnp.einsum('nhc,hc->nh', xs, att_dst)
            e = (ea @ lin_edge_w).reshape(-1, H, C)
            a_edge = jnp.einsum('ehc,hc->eh', e, att_edge)
            logits = a_src[src] + a_dst[dst] + a_edge
            logits = jnp.where(logits >= 0, logits, NEG_SLOPE * logits)
            lmax = jax.ops.segment_max(logits, dst, num_segments=N)
            ex = jnp.exp(logits - lmax[dst])
            denom = jax.ops.segment_sum(ex, dst, num_segments=N)
            alpha = ex / denom[dst]
            msgs = alpha[:, :, None] * xs[src]
            out = jax.ops.segment_sum(msgs, dst, num_segments=N)
            return out.reshape(N, H * C) + gat_bias
        x_gat = gat_conv(x, edge_index, edge_attr, lin_w, att_src, att_dst, lin_edge_w, att_edge, gat_bias)
        x_gat = x_gat @ w1 + b1
        x_gat = layer_norm(x + x_gat, ln1_g, ln1_b)
        lin = x_gat @ w2 + b2
        out = layer_norm(lin + x_gat, ln2_g, ln2_b)
        return out

    def _L1_gnn_ref(x, edge_index):
        import jax, jax.numpy as jnp
        import numpy as np
        NUM_LAYERS = 3

        def _lightgcn_layer(x, src, dst, num_nodes):
            msgs = x[src]
            summed = jax.ops.segment_sum(msgs, dst, num_segments=num_nodes)
            counts = jax.ops.segment_sum(jnp.ones((src.shape[0],), x.dtype), dst, num_segments=num_nodes)
            denom = jnp.maximum(counts, 1.0)
            return summed / denom[:, None]
        src = edge_index[0]
        dst = edge_index[1]
        n = x.shape[0]
        for _ in range(NUM_LAYERS):
            x = _lightgcn_layer(x, src, dst, n)
        return x

    def _L2_gnn_ref(x, edge_index, W1, b1, W2, b2):
        import jax, jax.numpy as jnp
        import numpy as np
        N_NODES = 12500
        N_EDGES = 200000
        IN_CH = 64
        OUT_CH = 64
        src = edge_index[0]
        dst = edge_index[1]
        x_i = x[dst]
        x_j = x[src]
        edge_features = jnp.concatenate([x_i, x_j - x_i], axis=-1)
        h = jax.nn.relu(edge_features @ W1 + b1)
        edge_messages = h @ W2 + b2
        out = jax.ops.segment_max(edge_messages, dst, num_segments=x.shape[0])
        return jnp.where(jnp.isfinite(out), out, jnp.zeros_like(out))

    def _L3_gnn_ref(feat, edge_src, edge_dst, fc_weight):
        import jax, jax.numpy as jnp
        import numpy as np
        N_NODES = 12500
        N_EDGES = 200000
        D_IN = 64
        D_OUT = 64
        h_src = feat[edge_src]
        h_dst = feat[edge_dst]
        a = jnp.sum(h_src * h_dst, axis=-1, keepdims=True)
        m = h_src * a
        neigh = jax.ops.segment_sum(m, edge_dst, num_segments=feat.shape[0])
        return neigh @ fc_weight.T
    edge_index = jnp.stack([src, dst])
    h = jnp.maximum(_layernorm(x, axis=-1), 0.0)
    x = x + _L0_gnn_ref(h, edge_attr_5, L0_gnn_lin_w, L0_gnn_att_src, L0_gnn_att_dst, L0_gnn_lin_edge_w, L0_gnn_att_edge, L0_gnn_gat_bias, L0_gnn_w1, L0_gnn_b1, L0_gnn_ln1_g, L0_gnn_ln1_b, L0_gnn_w2, L0_gnn_b2, L0_gnn_ln2_g, L0_gnn_ln2_b, edge_index)
    h = jnp.maximum(_layernorm(x, axis=-1), 0.0)
    x = x + _L1_gnn_ref(h, edge_index)
    h = jnp.maximum(_layernorm(x, axis=-1), 0.0)
    x = x + _L2_gnn_ref(h, edge_index, L2_gnn_W1, L2_gnn_b1, L2_gnn_W2, L2_gnn_b2)
    h = jnp.maximum(_layernorm(x, axis=-1), 0.0)
    x = x + _L3_gnn_ref(h, src, dst, L3_gnn_fc_weight)
    return x

_drawn_inputs = setup_inputs


def setup_inputs(seed=0):
    import zlib

    import numpy as np

    out = dict(_drawn_inputs(seed))
    spreads = {'L0_gnn_gat_bias': (0.0, 0.1),
     'L0_gnn_b1': (0.0, 0.1),
     'L0_gnn_ln1_g': (1.0, 0.2),
     'L0_gnn_ln1_b': (0.0, 0.1),
     'L0_gnn_b2': (0.0, 0.1),
     'L0_gnn_ln2_g': (1.0, 0.2),
     'L0_gnn_ln2_b': (0.0, 0.1),
     'L2_gnn_b1': (0.0, 0.1),
     'L2_gnn_b2': (0.0, 0.1)}
    factors = {'edge_attr_5': 8.0,
     'L0_gnn_att_dst': 64.0,
     'L0_gnn_lin_edge_w': 8.0,
     'L0_gnn_att_edge': 8.0,
     'L0_gnn_att_src': 8.0}
    for name, (base, spread) in spreads.items():
        noise = np.random.default_rng([zlib.crc32(name.encode()), seed]).standard_normal(out[name].shape)
        drawn = base * np.exp(spread * noise) if base else spread * noise
        out[name] = jnp.asarray(drawn.astype(out[name].dtype))
    for name, factor in factors.items():
        out[name] = (out[name] * factor).astype(out[name].dtype)
    return out
```

```python
from contextlib import ExitStack

import concourse.bass as bass
from concourse import mybir

F32, BF16, I32 = mybir.dt.float32, mybir.dt.bfloat16, mybir.dt.int32
ALU, ACT, AX = mybir.AluOpType, mybir.ActivationFunctionType, mybir.AxisListType

P = 128
N, E, D = 6250, 200000, 64
HEADS, EDIM = 3, 5
SLOPE, EPS = 0.2, 1e-5
BIG = 1e38

STREAMS, PER = 2, 4
U = STREAMS * PER
PAIR = 2
BUFS = 4
TILES = -(-E // (P * U * BUFS)) * U * BUFS
CHUNKS = TILES // U
LOOPS = CHUNKS // BUFS
HALF = TILES // STREAMS
ROWP = 98
ROWT = TILES // ROWP
ROWE = ROWT * P

NB = -(-N // P)
LASTP, LASTB = N // NB, N % NB
NPAD = NB * P
RB = NB + 1
RANKS = RB * P
TRASH = RANKS
CROWS = TRASH + NPAD
TW = D + HEADS + 1
CW = HEADS * TW // 2
AW = HEADS + 1
WW = 2 * HEADS


class Norm:

    def __init__(self, s):
        self.stat = s.sb("stat", [P, NB])[:, :]
        self.square = s.sb("square", [P, NB, D])[:, :, :]


class Edges:

    def __init__(self, s):
        self.logit = s.sb("logit", [P, TILES, AW])
        self.dst = s.sb("dst", [P, TILES], I32)


class Memory:

    def __init__(self, s):
        self.src = s.sb("src", [P, TILES], I32)
        self.local = s.sb("local", [P, TILES])
        self.last = s.sb("last", [P, TILES])
        self.starts = s.sb("starts", [1, TILES], I32)
        self.x = s.sb("x", [P, NB, D])
        self.h = s.sb("h", [P, NB, D])
        self.rank_of = s.sb("rank_of", [P, NB], I32)
        self.inv_count = s.sb("inv_count", [P, NB])
        self.logit = s.sb("logit", [P, NB, WW])
        self.self_w = s.sb("self_w", [P, NB, HEADS])
        self.iota = s.sb("iota", [P, P])
        self.lane = s.sb("lane", [P, 1])
        self.ident = s.sb("ident", [P, P])


def loop_steps(eng, body, skew):
    for j in range(BUFS):
        body(0, j)
    with eng.Fori(1, LOOPS) as k:
        for j in range(BUFS):
            body(k, j)
    for step in range(CHUNKS, CHUNKS + skew):
        body(step // BUFS, step % BUFS)


def stage(k, j, skew):
    if j < skew:
        k = k - 1
    b = (j - skew) % BUFS
    c = k * BUFS + b
    if isinstance(k, int) and not 0 <= c < CHUNKS:
        return None
    return c, k, b


def chunk_row(row, c, st, parts):
    return row[bass.ds(c * (PER * P) + st * HALF * P, PER * P)].unsqueeze(0).broadcast_to([parts, PER * P])


def window_starts(nc, engine, starts, c):
    _, regs = nc.values_load_multi_w_load_instructions(
        starts[0:1, bass.ds(c * U, U)], engines=[engine], min_val=0, max_val=RANKS - P,
        skip_runtime_bounds_check_because="a rank is at most the number of nodes")
    return regs


def gather_pass(pool, rows, index, table, width, index_ready, rows_in, layer=0):
    def step(k, j):
        c, k, b = stage(k, j, 0)
        pool.wait_ge(index_ready, layer * CHUNKS + c + 1)
        pool.nop(nofuse=True)
        for u in range(U):
            pool.indirect_dma_start(rows[:, b, u * width:(u + 1) * width], None, table,
                                    bass.IndirectOffsetOnAxis(index[:, b, u:u + 1], 0)).then_inc(rows_in[b], 16)
    loop_steps(pool, step, 0)


def one_hot(nc, out, iota, local):
    return nc.vector.tensor_tensor(out, iota.unsqueeze(1).broadcast_to([P, U, P]),
                                   local.unsqueeze(2).broadcast_to([P, U, P]), ALU.is_equal)


class Scope:

    def __init__(self, nc, ctx, tag):
        self.nc, self.ctx, self.tag, self.sems = nc, ctx, tag, []

    def sb(self, name, shape, dt=F32):
        return self.ctx.enter_context(self.nc.sbuf_tensor(f"{self.tag}_{name}", shape, dt))

    def ps(self, name, shape, dt=F32):
        return self.ctx.enter_context(self.nc.psum_tensor(f"{self.tag}_{name}", shape, dt))

    def sem(self, name):
        if not self.sems:
            self.ctx.callback(self.clear)
        self.sems.append(self.nc.alloc_semaphore(f"{self.tag}_{name}"))
        return self.sems[-1]

    def clear(self):
        self.nc.clear_and_free_semaphores(self.sems)
        self.nc.all_engine_barrier()


def linker(eng, sem):
    count = [0]

    def link(ins):
        count[0] += 1
        ins.then_inc(sem, 1)
        eng.wait_ge(sem, count[0])
        return count[0]

    return link


def bcast(v, n):
    return v.unsqueeze(2).broadcast_to([P, NB, n])


def layer_norm(nc, link, dve, out, x, t, sem_var, sem_std, turn):
    link(nc.vector.tensor_reduce(out=t.stat, in_=x, axis=AX.X, op=ALU.add))
    link(nc.vector.tensor_scalar(t.stat, t.stat, 1.0 / D, None, ALU.mult))
    link(nc.vector.tensor_tensor(out, x, bcast(t.stat, D), ALU.subtract))
    link(nc.vector.tensor_tensor(t.square, out, out, ALU.mult))
    link(nc.vector.tensor_reduce(out=t.stat, in_=t.square, axis=AX.X, op=ALU.add))
    nc.vector.tensor_scalar(t.stat, t.stat, 1.0 / D, EPS, ALU.mult, ALU.add).then_inc(sem_var, 1)
    dve.wait_ge(sem_std, turn)
    link(nc.vector.reciprocal(t.stat, t.stat))
    link(nc.vector.tensor_tensor(out, out, bcast(t.stat, D), ALU.mult))


def root(nc, act, t, sem_var, sem_std, turn):
    act.wait_ge(sem_var, turn)
    nc.scalar.activation(t.stat, t.stat, ACT.Sqrt).then_inc(sem_std, 1)


def phase_ranks(nc, m, d):
    with ExitStack() as ctx:
        s = Scope(nc, ctx, "rk")
        prev, cur, nxt = (s.sb(n, [ROWP, ROWE]) for n in ("prev", "cur", "next"))
        raw = s.sb("raw", [ROWP, 3, ROWE], I32)
        ones = s.sb("ones", [ROWP, ROWE])
        rank = s.sb("rank", [ROWP, ROWE])
        local16 = s.sb("local16", [ROWP, ROWE], BF16)
        before = s.sb("before", [ROWP, ROWP])
        offset = s.sb("offset", [ROWP, 1])
        base = s.sb("base", [ROWP, ROWT])
        base_i = s.sb("base_i", [ROWP, ROWT], I32)
        starts_t = s.sb("starts_t", [1, TILES], I32)
        zeros = s.sb("zeros", [P, NB * HEADS * TW])
        init = s.sb("init", [P, NB], I32)
        ps_off = s.ps("ps_off", [ROWP, 512])
        ps_t = s.ps("ps_t", [P, 4, 512])
        loaded, made, chain = s.sem("loaded"), s.sem("made"), s.sem("chain")
        counted, offset_ready, transposed, taken = (s.sem(n) for n in ("counted", "offset_ready", "transposed", "taken"))
        stored, zeroed, base_ready, rows_ready = (s.sem(n) for n in ("stored", "zeroed", "base_ready", "rows_ready"))
        starts_in, zero_made, src_in, last_ready = (s.sem(n) for n in ("starts_in", "zero_made", "src_in", "last_ready"))
        block = ctx.enter_context(nc.Block())

        @block.sync
        def _(sp):
            for i in range(3):
                sp.dma_start(raw[:, i, :], d["dst_rows"][i:i + TILES * P].rearrange("(p e) -> p e", p=ROWP)).then_inc(loaded, 16)
            sp.dma_start(m.src[:, :], d["src_cols"]).then_inc(src_in, 16)
            sp.wait_ge(base_ready, 1)
            sp.dma_start(d["starts"].rearrange("(p t) -> p t", p=ROWP), base_i[:, :]).then_inc(stored, 16)
            sp.wait_ge(stored, 16)
            sp.dma_start(starts_t[:, :], d["starts"].rearrange("(o t) -> o t", o=1)).then_inc(starts_in, 16)
            sp.wait_ge(rows_ready, 1)
            sp.dma_start(d["local_rows"].rearrange("(p e) -> p e", p=ROWP), local16[:, :]).then_inc(stored, 16)
            sp.wait_ge(rows_ready, 2)
            sp.dma_start(d["reset_rows"].rearrange("(p e) -> p e", p=ROWP), nxt[:, :]).then_inc(stored, 16)
            sp.wait_ge(src_in, 16)
            sp.wait_ge(stored, 48)

        @block.scalar
        def _(act):
            act.wait_ge(zero_made, 1)
            for table, w in ((d["rank8"], 8), (d["rank_heads"], HEADS * TW), (d["rank_feat"], D)):
                act.dma_start(table[TRASH:CROWS, :].rearrange("(p b) w -> p (b w)", b=NB),
                              zeros[:, 0:NB * w]).then_inc(zeroed, 16)
            for table, w in ((d["win8"], 8), (d["win"], D)):
                act.dma_start(table[0:RANKS, :].rearrange("(p r) w -> p (r w)", r=RB), zeros[:, 0:RB * w]).then_inc(zeroed, 16)
            act.wait_ge(made, 3)
            act.dma_start(d["rank_of"][0:NPAD, :].rearrange("(p b) o -> p (b o)", b=NB), init[:, :]).then_inc(zeroed, 16)
            act.wait_ge(zeroed, 96)

        @block.gpsimd
        def _(pool):
            nc.gpsimd.iota(m.iota[:, :], pattern=[[1, P]], base=0, channel_multiplier=0,
                           allow_small_or_imprecise_dtypes=True).then_inc(made, 1)
            nc.gpsimd.iota(m.lane[:, :], pattern=[[0, 1]], base=0, channel_multiplier=1,
                           allow_small_or_imprecise_dtypes=True).then_inc(made, 1)
            nc.gpsimd.iota(init[:, :], pattern=[[1, NB]], base=TRASH, channel_multiplier=NB).then_inc(made, 1)

        @block.vector
        def _(dve):
            link = linker(dve, chain)
            nc.vector.memset(zeros[:, :], 0.0).then_inc(zero_made, 1)
            link(nc.vector.memset(ones[:, :], 1.0))
            dve.wait_ge(made, 2)
            link(nc.vector.tensor_scalar(m.ident[:, :], m.iota[:, :], m.lane[:, :], None, ALU.is_equal))
            link(nc.vector.tensor_scalar(before[:, :], m.iota[0:ROWP, 0:ROWP], m.lane[0:ROWP, :], None, ALU.is_gt))
            dve.wait_ge(loaded, 48)
            for i, t in enumerate((prev, cur, nxt)):
                link(nc.vector.tensor_copy(t[:, :], raw[:, i, :]))
            link(nc.vector.tensor_tensor(prev[:, :], prev[:, :], cur[:, :], ALU.not_equal))
            link(nc.vector.tensor_tensor(nxt[:, :], nxt[:, :], cur[:, :], ALU.not_equal))
            nc.vector.tensor_tensor_scan(rank[:, :], ones[:, :], prev[:, :], 0.0, ALU.mult, ALU.add).then_inc(counted, 1)
            dve.wait_ge(offset_ready, 1)
            link(nc.vector.tensor_scalar(offset[:, :], ps_off[:, 0:1], 1.0, None, ALU.subtract))
            link(nc.vector.tensor_scalar(rank[:, :], rank[:, :], offset[:, :], None, ALU.add))
            rank_t = rank[:, :].rearrange("p (t e) -> p t e", e=P)
            link(nc.vector.tensor_copy(base[:, :], rank_t[:, :, 0]))
            nc.vector.tensor_copy(base_i[:, :], base[:, :]).then_inc(base_ready, 1)
            link(nc.vector.tensor_tensor(rank_t, rank_t, base[:, :].unsqueeze(2).broadcast_to([ROWP, ROWT, P]), ALU.subtract))
            link(nc.vector.scalar_tensor_tensor(cur[:, :], rank[:, :], 1.0, nxt[:, :], ALU.add, ALU.mult))
            nc.vector.tensor_scalar(cur[:, :], cur[:, :], 1.0, None, ALU.subtract).then_inc(last_ready, 1)
            nc.vector.tensor_copy(local16[:, :], rank[:, :]).then_inc(rows_ready, 1)
            nc.vector.tensor_scalar(nxt[:, :], prev[:, :], -BIG, None, ALU.mult).then_inc(rows_ready, 1)
            for n in range(2 * ROWT):
                dve.wait_ge(transposed, n + 1)
                out = (m.local, m.last)[n // ROWT]
                j = n % ROWT
                view = out[:, :].rearrange("p (k a s i) -> p k a s i", a=ROWT // PER, s=STREAMS, i=PER)[:, :, j // PER, :, j % PER]
                nc.vector.tensor_copy(view, ps_t[:, n % 4, 0:ROWP].rearrange("p (s k) -> p k s", s=STREAMS)).then_inc(taken, 1)
            dve.wait_ge(starts_in, 16)
            for st in range(STREAMS):
                nc.vector.tensor_copy(m.starts[:, :].rearrange("o (c s i) -> o c s i", s=STREAMS, i=PER)[:, :, st, :],
                                      starts_t[:, st * HALF:(st + 1) * HALF].rearrange("o (c i) -> o c i", i=PER))

        @block.tensor
        def _(pe):
            pe.wait_ge(counted, 1)
            pe.wait_ge(chain, 3)
            nc.tensor.matmul(ps_off[:, 0:1], before[:, :], rank[:, ROWE - 1:ROWE], start=True, stop=True).then_inc(offset_ready, 1)
            pe.wait_ge(last_ready, 1)
            for n in range(2 * ROWT):
                if n >= 4:
                    pe.wait_ge(taken, n - 3)
                j = n % ROWT
                nc.tensor.transpose(ps_t[:, n % 4, 0:ROWP], (rank, cur)[n // ROWT][:, j * P:(j + 1) * P],
                                    m.ident[0:ROWP, 0:ROWP]).then_inc(transposed, 1)


def load_features(nc, sp, m, d, sem):
    sp.dma_start(m.x[0:LASTP, :, :], d["x"][0:LASTP * NB, :].rearrange("(p b) w -> p b w", b=NB)).then_inc(sem, 16)
    sp.dma_start(m.x[LASTP:LASTP + 1, 0:LASTB, :], d["x"][LASTP * NB:N, :].rearrange("(p b) w -> p b w", b=LASTB)).then_inc(sem, 16)


def phase_table(nc, m, d, edge):
    with ExitStack() as ctx:
        s = Scope(nc, ctx, "tb")
        t = Norm(s)
        lin_w = s.sb("lin_w", [D, HEADS * D])
        att = s.sb("att", [D, 2, HEADS * D])
        prod = s.sb("prod", [D, HEADS * D])
        folded = s.sb("folded", [D, 2 * HEADS])
        edge_w = s.sb("edge_w", [P, EDIM, HEADS * D])
        att_e = s.sb("att_e", [P, HEADS * D])
        v = s.sb("v", [P, EDIM * HEADS])
        attr = s.sb("attr", [P, TILES * EDIM])
        h_t = s.sb("h_t", [D, 2, P])
        table = s.sb("table", [P, NB, TW])
        ps_t = s.ps("ps_t", [D, 2, 512])
        ps_a = s.ps("ps_a", [P, 512])
        loaded, weights_in, attr_in, chain = (s.sem(n) for n in ("loaded", "weights_in", "attr_in", "chain"))
        var, std, h_ready, folded_ready = (s.sem(n) for n in ("var", "std", "h_ready", "folded_ready"))
        transposed, taken, logits_ready, table_ready, stored = (s.sem(n) for n in ("transposed", "taken", "logits_ready", "table_ready", "stored"))
        cleared = s.sem("cleared")
        block = ctx.enter_context(nc.Block())

        @block.sync
        def _(sp):
            sp.wait_ge(cleared, 1)
            load_features(nc, sp, m, d, loaded)
            sp.dma_start(lin_w[:, :], d["lin_w"]).then_inc(weights_in, 16)
            sp.dma_start(att[:, 0, :], d["att_src"].rearrange("h c -> (h c)").unsqueeze(0).broadcast_to([D, HEADS * D])).then_inc(weights_in, 16)
            sp.dma_start(att[:, 1, :], d["att_dst"].rearrange("h c -> (h c)").unsqueeze(0).broadcast_to([D, HEADS * D])).then_inc(weights_in, 16)
            sp.dma_start(edge_w[:, :, :].rearrange("p a b -> p (a b)"), d["lin_edge_w"].rearrange("h c -> (h c)").unsqueeze(0).broadcast_to([P, EDIM * HEADS * D])).then_inc(weights_in, 16)
            sp.dma_start(att_e[:, :], d["att_edge"].rearrange("h c -> (h c)").unsqueeze(0).broadcast_to([P, HEADS * D])).then_inc(weights_in, 16)
            sp.dma_start(attr[:, :], d["attr_cols"]).then_inc(attr_in, 16)
            sp.dma_start(edge.dst[:, :], d["dst_cols"]).then_inc(attr_in, 16)
            sp.wait_ge(table_ready, 1)
            sp.dma_start(d["table0"].rearrange("(p b) w -> p b w", b=NB), table[:, :, :]).then_inc(stored, 16)
            sp.wait_ge(stored, 16)

        @block.scalar
        def _(act):
            root(nc, act, t, var, std, 1)
            for b in range(NB):
                act.wait_ge(transposed, b + 1)
                if b >= 2:
                    act.wait_ge(logits_ready, b - 1)
                nc.scalar.copy(h_t[:, b % 2, :], ps_t[:, b % 2, 0:P]).then_inc(taken, 1)

        @block.tensor
        def _(pe):
            pe.wait_ge(h_ready, 1)
            pe.wait_ge(folded_ready, 1)
            for b in range(NB + 1):
                if b < NB:
                    if b >= 2:
                        pe.wait_ge(taken, b - 1)
                    nc.tensor.transpose(ps_t[:, b % 2, 0:P], m.h[:, b, :], m.ident[:, :]).then_inc(transposed, 1)
                if b >= 1:
                    pe.wait_ge(taken, b)
                    nc.tensor.matmul(ps_a[:, (b - 1) * WW:b * WW], h_t[:, (b - 1) % 2, :], folded[:, :],
                                     start=True, stop=True).then_inc(logits_ready, 1)

        @block.vector
        def _(dve):
            link = linker(dve, chain)
            nc.vector.memset(m.x[:, :, :], 0.0).then_inc(cleared, 1)
            dve.wait_ge(weights_in, 80)
            for a in range(2):
                link(nc.vector.tensor_tensor(prod[:, :], lin_w[:, :], att[:, a, :], ALU.mult))
                ins = nc.vector.tensor_reduce(out=folded[:, a * HEADS:(a + 1) * HEADS], in_=prod[:, :].rearrange("p (h c) -> p h c", h=HEADS), axis=AX.X, op=ALU.add)
                if a == 0:
                    link(ins)
                else:
                    ins.then_inc(folded_ready, 1)
            link(nc.vector.tensor_tensor(edge_w[:, :, :], edge_w[:, :, :], att_e[:, :].unsqueeze(1).broadcast_to([P, EDIM, HEADS * D]), ALU.mult))
            link(nc.vector.tensor_reduce(out=v[:, :], in_=edge_w[:, :, :].rearrange("p a (h c) -> p (a h) c", h=HEADS), axis=AX.X, op=ALU.add))
            dve.wait_ge(loaded, 32)
            layer_norm(nc, link, dve, m.h[:, :, :], m.x[:, :, :], t, var, std, 1)
            link(nc.vector.tensor_scalar(m.h[:, :, :], m.h[:, :, :], 0.0, None, ALU.max))
            nc.vector.tensor_copy(table[:, :, 0:D], m.h[:, :, :]).then_inc(h_ready, 1)
            dve.wait_ge(attr_in, 32)
            at = attr[:, :].rearrange("p (t c) -> p t c", c=EDIM)
            for hd in range(HEADS):
                link(nc.vector.tensor_scalar(edge.logit[:, :, hd], at[:, :, 0], v[:, hd:hd + 1], None, ALU.mult))
                for c in range(1, EDIM):
                    link(nc.vector.scalar_tensor_tensor(edge.logit[:, :, hd], at[:, :, c], v[:, c * HEADS + hd:c * HEADS + hd + 1],
                                                        edge.logit[:, :, hd], ALU.mult, ALU.add))
            link(nc.vector.memset(edge.logit[:, :, HEADS], 1.0))
            dve.wait_ge(logits_ready, NB)
            link(nc.vector.tensor_copy(m.logit[:, :, :], ps_a[:, 0:NB * WW].rearrange("p (b w) -> p b w", w=WW)))
            nc.vector.memset(table[:, :, D + HEADS:TW], 1.0)
            nc.vector.tensor_copy(table[:, :, D:D + HEADS], m.logit[:, :, 0:HEADS]).then_inc(table_ready, 1)


def add_windows(nc, dve, acc, ps_o, starts, product, added, c, per_bank, layer=0):
    banks = U // per_bank
    regs = window_starts(nc, mybir.EngineType.DVE, starts, c)
    for u in range(U):
        if u % per_bank == 0:
            dve.wait_ge(product, layer * ((CHUNKS + BUFS) * banks) + c * banks + (BUFS * banks + u // per_bank + 1))
        dve.wait_ge(added, layer * (TILES + U) + c * U + (U + u))
        where = acc[..., bass.ds(regs[u], P)] if len(acc.shape) == 2 else acc[:, :, bass.ds(regs[u], P)]
        nc.vector.tensor_tensor(where, where, ps_o(u), ALU.add).then_inc(added, 1)


def phase_gat_max(nc, m, d, edge, acc):
    with ExitStack() as ctx:
        s = Scope(nc, ctx, "gm")
        rows = s.sb("rows", [P, BUFS, U * TW])
        index = s.sb("index", [P, BUFS, U], I32)
        hot = s.sb("hot", [P, BUFS, U, P])
        hot_last = s.sb("hot_last", [P, BUFS, U, P])
        part = s.sb("part", [P, BUFS, U, AW])
        cand = s.sb("cand", [P, 2, PER, STREAMS * AW])
        reset = s.sb("reset", [STREAMS * AW, BUFS, PER * P])
        run = s.sb("run", [STREAMS * AW, 2, PER * P])
        back = s.sb("back", [P, 2, PER, STREAMS * AW])
        border = s.sb("border", [AW, 1])
        ps_c = s.ps("ps_c", [STREAMS * AW, 2, PER * P])
        ps_b = s.ps("ps_b", [P, 512])
        ps_o = s.ps("ps_o", [AW, U, 2, P])
        index_ready = s.sem("index_ready")
        rows_in = [s.sem(f"rows_in{b}") for b in range(BUFS)]
        saved = [s.sem(f"saved{b}") for b in range(BUFS)]
        reset_in = [s.sem(f"reset_in{b}") for b in range(BUFS)]
        hot_ready, cand_ready, cand_t, run_ready = (s.sem(n) for n in ("hot_ready", "cand_ready", "cand_t", "run_ready"))
        back_t, back_ready, product, added = (s.sem(n) for n in ("back_t", "back_ready", "product", "added"))
        part_ready, border_in, chain = s.sem("part_ready"), s.sem("border_in"), s.sem("chain")
        BANKS = U // PAIR
        block = ctx.enter_context(nc.Block())

        @block.gpsimd
        def _(pool):
            gather_pass(pool, rows, index, d["table0"], TW, index_ready, rows_in)

        @block.sync
        def _(sp):
            sp.dma_start(border[:, :], d["reset_rows"][HALF * P:HALF * P + 1].unsqueeze(0).broadcast_to([AW, 1])).then_inc(border_in, 16)

            def step(k, j):
                if now := stage(k, j, 0):
                    c, _, b = now
                    sp.wait_ge(run_ready, c + 1)
                    sp.nop(nofuse=True)
                    for st in range(STREAMS):
                        sp.dma_start(reset[st * AW:(st + 1) * AW, b, :], chunk_row(d["reset_rows"], c, st, AW)).then_inc(reset_in[b], 16)
                if now := stage(k, j, 1):
                    c, r, b = now
                    sp.wait_ge(rows_in[b], (r + 1) * (16 * U))
                    sp.nop(nofuse=True)
                    sp.dma_start(d["saved"][bass.ds(c * P, P), :], rows[:, b, :]).then_inc(saved[b], 16)
            loop_steps(sp, step, 1)
            for b in range(BUFS):
                sp.wait_ge(saved[b], 16 * (LOOPS + 1))
            sp.wait_ge(border_in, 16)

        @block.scalar
        def _(act):
            for b in range(BUFS):
                act.sem_inc(saved[b], 16)
            act.sem_inc(back_ready, 1)

            def step(k, j):
                if now := stage(k, j, 0):
                    c, r, b = now
                    act.wait_ge(cand_ready, c * 2 + 2)
                    act.wait_ge(saved[b], (r + 1) * 16)
                    nc.scalar.copy(index[:, b, :], m.src[:, bass.ds(c * U, U)]).then_inc(index_ready, 1)
                    act.wait_ge(product, c * BANKS + BANKS)
                    nc.scalar.copy(part[:, b, :, :], edge.logit[:, bass.ds(c * U, U), :]).then_inc(part_ready, 1)
                if now := stage(k, j, 2):
                    c, r, b = now
                    act.wait_ge(back_t, c + 3)
                    act.wait_ge(product, c * BANKS + 3 * BANKS)
                    nc.scalar.copy(back[:, b % 2, :, :], ps_b[:, 0:U * AW].rearrange("p (i a) -> p i a", i=PER)).then_inc(back_ready, 1)
            loop_steps(act, step, 2)

        @block.tensor
        def _(pe):
            pe.sem_inc(product, BUFS * BANKS)
            pe.sem_inc(cand_t, 2)
            pe.sem_inc(back_t, 2)

            def step(k, j):
                if now := stage(k, j, 1):
                    c, r, b = now
                    pe.wait_ge(cand_ready, c * 2 + 2 * BUFS + 2)
                    pe.wait_ge(run_ready, c + BUFS - 1)
                    for i in range(PER):
                        last = nc.tensor.transpose(ps_c[:, b % 2, i * P:(i + 1) * P], cand[:, b % 2, i, :], m.ident[:, :])
                    last.then_inc(cand_t, 1)
                if now := stage(k, j, 2):
                    c, r, b = now
                    pe.wait_ge(run_ready, c + BUFS + 1)
                    pe.wait_ge(back_ready, c + 1)
                    pe.nop(nofuse=True)
                    w = STREAMS * AW
                    for i in range(PER):
                        last = nc.tensor.transpose(ps_b[:, i * w:(i + 1) * w], run[:, b % 2, i * P:(i + 1) * P], m.ident[0:w, 0:w])
                    last.then_inc(back_t, 1)
                    pe.wait_ge(part_ready, c + 1)
                    pe.wait_ge(hot_ready, c * 2 + 2)
                    pe.wait_ge(back_ready, c + 2)
                    for u in range(U):
                        st, i = divmod(u, PER)
                        if u % PAIR == 0:
                            pe.wait_ge(added, c * U + (u + PAIR))
                        nc.tensor.matmul(ps_o[:, u, 0, :], part[:, b, u, :], hot[:, b, u, :], start=True, stop=True)
                        last = nc.tensor.matmul(ps_o[:, u, 1, :], back[:, b % 2, i, st * AW:(st + 1) * AW], hot_last[:, b, u, :],
                                         start=True, stop=True)
                        if u % PAIR == PAIR - 1:
                            last.then_inc(product, 1)
            loop_steps(pe, step, 2)

        @block.vector
        def _(dve):
            link = linker(dve, chain)
            nc.vector.memset(acc[0:AW, :, :], 0.0).then_inc(added, U)
            nc.vector.memset(run[:, :, :], -BIG).then_inc(run_ready, BUFS)
            dve.sem_inc(cand_ready, 2 * BUFS)

            def step(k, j):
                if now := stage(k, j, 0):
                    c, r, b = now
                    dve.wait_ge(product, c * BANKS + BANKS)
                    one_hot(nc, hot[:, b], m.iota[:, :], m.local[:, bass.ds(c * U, U)]).then_inc(hot_ready, 1)
                    one_hot(nc, hot_last[:, b], m.iota[:, :], m.last[:, bass.ds(c * U, U)]).then_inc(hot_ready, 1)
                if now := stage(k, j, 1):
                    c, r, b = now
                    dve.wait_ge(cand_t, c + 3)
                    dve.wait_ge(reset_in[b], (r + 1) * (16 * STREAMS))
                    dve.wait_ge(back_t, c + 1)
                    dve.wait_ge(run_ready, c + BUFS)
                    nc.vector.tensor_tensor_scan(run[:, b % 2, :], reset[:, b, :], ps_c[:, b % 2, :],
                                                 run[:, (b + 1) % 2, PER * P - 1:PER * P], ALU.add, ALU.max).then_inc(run_ready, 1)
                if now := stage(k, j, 2):
                    add_windows(nc, dve, acc[0:AW, :, :], lambda u: ps_o[:, u, :, :], m.starts, product, added, now[0], PAIR)
                if now := stage(k, j, 0):
                    c, r, b = now
                    dve.wait_ge(rows_in[b], (r + 1) * (16 * U))
                    dve.wait_ge(cand_t, c + 1)
                    tile4 = lambda ap: ap.rearrange("p (s i) a -> p s i a", s=STREAMS)
                    to = cand[:, b % 2, :, :].rearrange("p i (s a) -> p s i a", s=STREAMS)
                    nc.vector.tensor_tensor(to[:, :, :, 0:HEADS],
                                            tile4(rows[:, b, :].rearrange("p (u w) -> p u w", w=TW)[:, :, D:D + HEADS]),
                                            tile4(edge.logit[:, bass.ds(c * U, U), 0:HEADS]), ALU.add).then_inc(cand_ready, 1)
                    nc.vector.tensor_copy(to[:, :, :, HEADS],
                                          edge.dst[:, bass.ds(c * U, U)].rearrange("p (s i) -> p s i", s=STREAMS)).then_inc(cand_ready, 1)
            loop_steps(dve, step, 2)
            dve.wait_ge(border_in, 16)
            dve.wait_ge(run_ready, CHUNKS + BUFS)
            link(nc.vector.tensor_tensor(border[:, :], border[:, :], run[0:AW, (CHUNKS - 1) % 2, PER * P - 1:PER * P], ALU.add))
            dve.wait_ge(added, TILES + U)
            first = nc.vector.value_load(m.starts[0:1, PER:PER + 1], min_val=0, max_val=RANKS - P)
            link(nc.vector.tensor_tensor(acc[0:AW, 1, bass.ds(first, 1)], acc[0:AW, 1, bass.ds(first, 1)], border[:, :], ALU.max))


def phase_gat_nodes(nc, m, d, acc):
    with ExitStack() as ctx:
        s = Scope(nc, ctx, "gn")
        table = s.sb("table", [P, RB, 2 * AW])
        slot_f = s.sb("slot_f", [P, RB])
        slot = s.sb("slot", [P, RB], I32)
        number = s.sb("number", [P, RB], I32)
        number_f = s.sb("number_f", [P, RB])
        node = s.sb("node", [P, NB, 2 * AW])
        win = s.sb("win", [P, NB, 2 * AW])
        mean = s.sb("mean", [P, NB, HEADS])
        own = s.sb("own", [P, NB, HEADS])
        tmp = s.sb("tmp", [P, NB, HEADS])
        empty = s.sb("empty", [P, NB])
        ps = s.ps("ps", [P, 512])
        rows_t, table_ready, stored, numbered, slot_ready = (s.sem(n) for n in ("rows_t", "table_ready", "stored", "numbered", "slot_ready"))
        scattered, rank_in, gathered, win_ready, win_out = (s.sem(n) for n in ("scattered", "rank_in", "gathered", "win_ready", "win_out"))
        chain, arg_ready, exp_ready = s.sem("chain"), s.sem("arg_ready"), s.sem("exp_ready")
        block = ctx.enter_context(nc.Block())

        @block.tensor
        def _(pe):
            for r in range(RB):
                for a in range(2):
                    last = nc.tensor.transpose(ps[:, (2 * r + a) * AW:(2 * r + a + 1) * AW], acc[0:AW, a, r * P:(r + 1) * P], m.ident[0:AW, 0:AW])
            last.then_inc(rows_t, 1)

        @block.sync
        def _(sp):
            sp.wait_ge(table_ready, 1)
            sp.dma_start(d["rank8"][0:RANKS, :].rearrange("(r p) w -> p r w", p=P), table[:, :, :]).then_inc(stored, 16)
            sp.wait_ge(scattered, 16 * RB)
            sp.dma_start(m.rank_of[:, :], d["rank_of"][0:NPAD, :].rearrange("(p b) o -> p (b o)", b=NB)).then_inc(rank_in, 16)
            sp.wait_ge(rank_in, 16)

        @block.gpsimd
        def _(pool):
            nc.gpsimd.iota(number[:, :], pattern=[[P, RB]], base=0, channel_multiplier=1).then_inc(numbered, 1)
            pool.wait_ge(numbered, 1)
            pool.wait_ge(slot_ready, 1)
            for r in range(RB):
                pool.indirect_dma_start(d["rank_of"], bass.IndirectOffsetOnAxis(slot[:, r:r + 1], 0), number[:, r:r + 1], None).then_inc(scattered, 16)
            pool.wait_ge(rank_in, 16)
            pool.wait_ge(stored, 16)
            for b in range(NB):
                pool.indirect_dma_start(node[:, b, :], None, d["rank8"], bass.IndirectOffsetOnAxis(m.rank_of[:, b:b + 1], 0)).then_inc(gathered, 16)
            pool.wait_ge(win_ready, 1)
            for b in range(NB):
                pool.indirect_dma_start(d["win8"], bass.IndirectOffsetOnAxis(m.rank_of[:, b:b + 1], 0), win[:, b, :], None).then_inc(win_out, 16)
            pool.wait_ge(win_out, 16 * NB)

        @block.scalar
        def _(act):
            act.wait_ge(arg_ready, 1)
            nc.scalar.activation(m.self_w[:, :, :], tmp[:, :, :], ACT.Exp).then_inc(exp_ready, 1)

        @block.vector
        def _(dve):
            link = linker(dve, chain)
            dve.wait_ge(rows_t, 1)
            link(nc.vector.tensor_copy(table[:, :, :], ps[:, 0:RB * 2 * AW].rearrange("p (r w) -> p r w", r=RB)))
            dve.wait_ge(numbered, 1)
            link(nc.vector.tensor_copy(number_f[:, :], number[:, :]))
            link(nc.vector.tensor_scalar(slot_f[:, :], number_f[:, :], float(TRASH), None, ALU.add))
            link(nc.vector.tensor_scalar(number_f[:, :], table[:, :, HEADS], 0.0, None, ALU.is_equal))
            link(nc.vector.tensor_tensor(slot_f[:, :], slot_f[:, :], number_f[:, :], ALU.mult))
            link(nc.vector.tensor_tensor(slot_f[:, :], slot_f[:, :], table[:, :, 2 * AW - 1], ALU.add))
            nc.vector.tensor_copy(slot[:, :], slot_f[:, :]).then_inc(slot_ready, 1)
            dve.sem_inc(table_ready, 1)
            link(nc.vector.memset(win[:, :, :], 0.0))
            dve.wait_ge(gathered, 16 * NB)
            link(nc.vector.tensor_scalar(empty[:, :], node[:, :, HEADS], 0.0, -BIG, ALU.is_equal, ALU.mult))
            link(nc.vector.tensor_scalar(m.inv_count[:, :], node[:, :, HEADS], 1.0, None, ALU.max))
            link(nc.vector.reciprocal(m.inv_count[:, :], m.inv_count[:, :]))
            link(nc.vector.tensor_tensor(mean[:, :, :], node[:, :, 0:HEADS], bcast(m.inv_count[:, :], HEADS), ALU.mult))
            link(nc.vector.tensor_tensor(own[:, :, :], m.logit[:, :, 0:HEADS], mean[:, :, :], ALU.add))
            link(nc.vector.tensor_tensor(tmp[:, :, :], node[:, :, AW:AW + HEADS], bcast(empty[:, :], HEADS), ALU.add))
            link(nc.vector.tensor_tensor(tmp[:, :, :], tmp[:, :, :], own[:, :, :], ALU.max))
            link(nc.vector.tensor_tensor(tmp[:, :, :], tmp[:, :, :], m.logit[:, :, HEADS:WW], ALU.add))
            link(nc.vector.tensor_tensor(own[:, :, :], own[:, :, :], m.logit[:, :, HEADS:WW], ALU.add))
            link(nc.vector.scalar_tensor_tensor(win[:, :, HEADS:WW], tmp[:, :, :], SLOPE, tmp[:, :, :], ALU.mult, ALU.max))
            link(nc.vector.scalar_tensor_tensor(mean[:, :, :], own[:, :, :], SLOPE, own[:, :, :], ALU.mult, ALU.max))
            link(nc.vector.tensor_copy(win[:, :, 0:HEADS], m.logit[:, :, HEADS:WW]))
            nc.vector.tensor_tensor(tmp[:, :, :], mean[:, :, :], win[:, :, HEADS:WW], ALU.subtract).then_inc(arg_ready, 1)
            dve.sem_inc(win_ready, 1)


def local_chunk(row, c):
    return row.rearrange("(s e) -> s e", s=STREAMS)[:, bass.ds(c * (PER * P), PER * P)].unsqueeze(0).broadcast_to([P, STREAMS, PER * P])


def load_windows(nc, sp, win, wide, table, starts, c, b, win_in, spread, local_in):
    sp.nop(nofuse=True)
    for u, first in enumerate(window_starts(nc, mybir.EngineType.SP, starts, c)):
        sp.dma_start(win[:, b, u, :], table[bass.ds(first, P), :]).then_inc(win_in, 16)
    sp.dma_start(wide[:, b, :, :], local_chunk(spread, c)).then_inc(local_in, 16)


def phase_gat_sum(nc, m, d, edge, acc):
    with ExitStack() as ctx:
        s = Scope(nc, ctx, "gs")
        rows = s.sb("rows", [P, BUFS, U, TW])
        wide = s.sb("wide", [P, BUFS, STREAMS, PER * P], BF16)
        win = s.sb("win", [P, BUFS, U, 2 * AW])
        hot = s.sb("hot", [P, BUFS, U, P])
        hot_t = s.sb("hot_t", [P, 2, U, P])
        logit = s.sb("logit", [P, 2, U, HEADS])
        steep = s.sb("steep", [P, 2, U, HEADS])
        weight = s.sb("weight", [P, 2, U, HEADS])
        scaled = s.sb("scaled", [P, 2, U, HEADS * TW])
        ps_w = s.ps("ps_w", [P, 2, 512])
        ps_o = s.ps("ps_o", [CW, U, 2, P])
        rows_in = [s.sem(f"rows_in{b}") for b in range(BUFS)]
        win_in = [s.sem(f"win_in{b}") for b in range(BUFS)]
        local_in = [s.sem(f"local_in{b}") for b in range(BUFS)]
        hot_ready, hot_t_ready, spread, chain = (s.sem(n) for n in ("hot_ready", "hot_t_ready", "spread", "chain"))
        logit_ready, weight_ready, scaled_ready, product, added = (s.sem(n) for n in ("logit_ready", "weight_ready", "scaled_ready", "product", "added"))
        BANKS = U // PAIR
        block = ctx.enter_context(nc.Block())

        @block.sync
        def _(sp):
            def step(k, j):
                c, r, b = stage(k, j, 0)
                sp.wait_ge(scaled_ready, c + 1)
                sp.wait_ge(spread, c + 1)
                sp.nop(nofuse=True)
                sp.dma_start(rows[:, b, :, :].rearrange("p u w -> p (u w)"), d["saved"][bass.ds(c * P, P), :]).then_inc(rows_in[b], 16)
                load_windows(nc, sp, win, wide, d["win8"], m.starts, c, b, win_in[b], d["local_rows"], local_in[b])
            loop_steps(sp, step, 0)

        @block.scalar
        def _(act):
            def step(k, j):
                if now := stage(k, j, 1):
                    c, r, b = now
                    act.wait_ge(logit_ready, c + 1)
                    act.wait_ge(scaled_ready, c + BUFS - 1)
                    nc.scalar.activation(weight[:, b % 2, :, :], logit[:, b % 2, :, :], ACT.Exp).then_inc(weight_ready, 1)
            loop_steps(act, step, 1)

        @block.tensor
        def _(pe):
            pe.sem_inc(spread, BUFS)
            pe.sem_inc(product, BUFS * BANKS)

            def step(k, j):
                if now := stage(k, j, 0):
                    c, r, b = now
                    pe.wait_ge(hot_t_ready, c + 1)
                    pe.wait_ge(win_in[b], (r + 1) * (16 * U))
                    if not isinstance(c, int) or c >= 2:
                        pe.wait_ge(logit_ready, c - 1)
                    for u in range(U):
                        last = nc.tensor.matmul(ps_w[:, b % 2, u * WW:(u + 1) * WW], hot_t[:, b % 2, u, :], win[:, b, u, 0:WW], start=True, stop=True)
                    last.then_inc(spread, 1)
                if now := stage(k, j, 3):
                    c, r, b = now
                    pe.wait_ge(scaled_ready, c + BUFS + 1)
                    pe.wait_ge(hot_ready, c + 1)
                    for u in range(U):
                        if u % PAIR == 0:
                            pe.wait_ge(added, c * U + (u + PAIR))
                        for a in range(2):
                            last = nc.tensor.matmul(ps_o[:, u, a, :], scaled[:, b % 2, u, a * CW:(a + 1) * CW], hot[:, b, u, :], start=True, stop=True)
                        if u % PAIR == PAIR - 1:
                            last.then_inc(product, 1)
            loop_steps(pe, step, 3)

        @block.vector
        def _(dve):
            nc.vector.memset(acc[0:CW, :, :], 0.0).then_inc(added, U)
            dve.sem_inc(scaled_ready, BUFS)

            def step(k, j):
                if now := stage(k, j, 0):
                    c, r, b = now
                    dve.wait_ge(spread, c + BUFS - 1)
                    dve.wait_ge(local_in[b], (r + 1) * 16)
                    nc.vector.tensor_scalar(hot_t[:, b % 2, :, :].rearrange("p u e -> p (u e)"), wide[:, b, :, :].rearrange("p s e -> p (s e)"),
                                            m.lane[:, :], None, ALU.is_equal).then_inc(hot_t_ready, 1)
                    dve.wait_ge(product, c * BANKS + BANKS)
                    one_hot(nc, hot[:, b], m.iota[:, :], m.local[:, bass.ds(c * U, U)]).then_inc(hot_ready, 1)
                if now := stage(k, j, 1):
                    c, r, b = now
                    dve.wait_ge(rows_in[b], (r + 1) * 16)
                    if not isinstance(c, int) or c >= 2:
                        dve.wait_ge(weight_ready, c - 1)
                    z, t = logit[:, b % 2, :, :], steep[:, b % 2, :, :]
                    nc.vector.tensor_tensor(z, rows[:, b, :, D:D + HEADS], edge.logit[:, bass.ds(c * U, U), 0:HEADS], ALU.add).then_inc(chain, 1)
                    dve.wait_ge(chain, c * 3 + 1)
                    dve.wait_ge(spread, c + BUFS + 1)
                    at_dst = ps_w[:, b % 2, 0:U * WW].rearrange("p (u w) -> p u w", w=WW)
                    nc.vector.tensor_tensor(t, z, at_dst[:, :, 0:HEADS], ALU.add).then_inc(chain, 1)
                    dve.wait_ge(chain, c * 3 + 2)
                    nc.vector.scalar_tensor_tensor(z, t, SLOPE, t, ALU.mult, ALU.max).then_inc(chain, 1)
                    dve.wait_ge(chain, c * 3 + 3)
                    nc.vector.tensor_tensor(z, z, at_dst[:, :, HEADS:WW], ALU.subtract).then_inc(logit_ready, 1)
                if now := stage(k, j, 2):
                    c, r, b = now
                    dve.wait_ge(weight_ready, c + 1)
                    dve.wait_ge(product, c * BANKS + 3 * BANKS)
                    nc.vector.tensor_tensor(scaled[:, b % 2, :, :].rearrange("p u (h w) -> p u h w", h=HEADS),
                                            rows[:, b, :, :].unsqueeze(2).broadcast_to([P, U, HEADS, TW]),
                                            weight[:, b % 2, :, :].unsqueeze(3).broadcast_to([P, U, HEADS, TW]), ALU.mult).then_inc(scaled_ready, 1)
                if now := stage(k, j, 3):
                    add_windows(nc, dve, acc[0:CW, :, :], lambda u: ps_o[:, u, :, :], m.starts, product, added, now[0], PAIR)
            loop_steps(dve, step, 3)
            dve.wait_ge(added, TILES + U)


def rows_by_rank(nc, pe, acc, ps, ident, rows_t, rows_taken, width, parts, per_bank, base=0):
    for g in range(-(-RB // per_bank)):
        if g >= 2:
            pe.wait_ge(rows_taken, base + g - 1)
            pe.nop(nofuse=True)
        for r in range(g * per_bank, min((g + 1) * per_bank, RB)):
            o = (r - g * per_bank) * width
            for a in range(width // parts):
                block = acc[0:parts, a, r * P:(r + 1) * P] if width > parts else acc[0:parts, r * P:(r + 1) * P]
                last = nc.tensor.transpose(ps[:, g % 2, o + a * parts:o + (a + 1) * parts], block, ident[0:parts, 0:parts])
        last.then_inc(rows_t, 1)


def take_rows(nc, act, ps, rows, rows_t, rows_taken, width, per_bank, base=0):
    for g in range(-(-RB // per_bank)):
        act.wait_ge(rows_t, base + g + 1)
        lo, hi = g * per_bank, min((g + 1) * per_bank, RB)
        nc.scalar.copy(rows[:, lo:hi, :], ps[:, g % 2, 0:(hi - lo) * width].rearrange("p (r w) -> p r w", w=width)).then_inc(rows_taken, 1)


def gather_nodes(nc, pool, m, out, table, gathered):
    for b in range(NB):
        pool.indirect_dma_start(out[:, b, :], None, table, bass.IndirectOffsetOnAxis(m.rank_of[:, b:b + 1], 0)).then_inc(gathered, 16)


def scatter_nodes(nc, pool, m, table, rows, scattered):
    for b in range(NB):
        pool.indirect_dma_start(table, bass.IndirectOffsetOnAxis(m.rank_of[:, b:b + 1], 0), rows[:, b, :], None).then_inc(scattered, 16)


def phase_gat_rows(nc, m, d, acc):
    with ExitStack() as ctx:
        s = Scope(nc, ctx, "gr")
        rows = s.sb("rows", [P, RB, HEADS * TW])
        ps = s.ps("ps", [P, 2, 512])
        rows_t, rows_taken, stored = s.sem("rows_t"), s.sem("rows_taken"), s.sem("stored")
        block = ctx.enter_context(nc.Block())

        @block.tensor
        def _(pe):
            rows_by_rank(nc, pe, acc, ps, m.ident, rows_t, rows_taken, HEADS * TW, CW, 2)

        @block.scalar
        def _(act):
            take_rows(nc, act, ps, rows, rows_t, rows_taken, HEADS * TW, 2)

        @block.sync
        def _(sp):
            sp.wait_ge(rows_taken, RB // 2)
            sp.dma_start(d["rank_heads"][0:RANKS, :].rearrange("(r p) w -> p r w", p=P), rows[:, :, :]).then_inc(stored, 16)
            sp.wait_ge(stored, 16)


def phase_gat_out(nc, m, d):
    with ExitStack() as ctx:
        s = Scope(nc, ctx, "go")
        t = Norm(s)
        sums = s.sb("sums", [P, NB, HEADS * TW])
        den = s.sb("den", [P, NB, HEADS])
        norm = s.sb("norm", [P, NB, HEADS * D])
        y = s.sb("y", [P, NB, D])
        z = s.sb("z", [P, NB, D])
        lin_wt = s.sb("lin_wt", [D, HEADS, D])
        split = s.sb("split", [D, 2, 2 * D])
        w1 = s.sb("w1", [D, HEADS, D])
        w1_01, w1_2 = s.sb("w1_01", [P, D]), s.sb("w1_2", [D, D])
        bias_01, bias_2 = s.sb("bias_01", [P, 1]), s.sb("bias_2", [D, 1])
        fold_01, fold_2 = s.sb("fold_01", [P, D]), s.sb("fold_2", [D, D])
        w2 = s.sb("w2", [D, D])
        vec = s.sb("vec", [P, 6, D])
        bias = s.sb("bias", [P, D])
        left = s.sb("left", [P, 2, P])
        right = s.sb("right", [D, 2, P])
        ps_w = s.ps("ps_w", [P, 3, D])
        ps_l, ps_r = s.ps("ps_l", [P, 2, 512]), s.ps("ps_r", [D, 2, 512])
        ps_y = s.ps("ps_y", [P, 2, 512])
        gathered, loaded, padded, folded, fold_taken = (s.sem(n) for n in ("gathered", "loaded", "padded", "folded", "fold_taken"))
        sums_ready, block_t, block_taken, done, drained = (s.sem(n) for n in ("sums_ready", "block_t", "block_taken", "done", "drained"))
        var, std, chain, y_ready = (s.sem(n) for n in ("var", "std", "chain", "y_ready"))
        sums_h = sums[:, :, :].rearrange("p b (h w) -> p b h w", h=HEADS)
        block = ctx.enter_context(nc.Block())

        @block.gpsimd
        def _(pool):
            gather_nodes(nc, pool, m, sums, d["rank_heads"], gathered)
            pool.wait_ge(gathered, 16 * NB)

        @block.sync
        def _(sp):
            sp.dma_start(lin_wt[:, :, :], d["lin_wt"].rearrange("(h c) i -> c h i", h=HEADS)).then_inc(loaded, 16)
            sp.dma_start(w1[:, :, :], d["w1"].rearrange("(h c) i -> c h i", h=HEADS)).then_inc(loaded, 16)
            sp.dma_start(w1_01[:, :], d["w1"][0:P, :]).then_inc(loaded, 16)
            sp.dma_start(w1_2[:, :], d["w1"][P:HEADS * D, :]).then_inc(loaded, 16)
            sp.dma_start(bias_01[:, :], d["gat_bias"][0:P].unsqueeze(1)).then_inc(loaded, 16)
            sp.dma_start(bias_2[:, :], d["gat_bias"][P:HEADS * D].unsqueeze(1)).then_inc(loaded, 16)
            sp.dma_start(w2[:, :], d["w2"]).then_inc(loaded, 16)
            for i, v in enumerate((d["b1"], d["ln1_g"], d["ln1_b"], d["b2"], d["ln2_g"], d["ln2_b"])):
                sp.dma_start(vec[:, i, :], v.unsqueeze(0).broadcast_to([P, D])).then_inc(loaded, 16)
            sp.wait_ge(loaded, 16 * 13)

        @block.tensor
        def _(pe):
            pe.wait_ge(loaded, 16 * 13)
            pe.wait_ge(padded, 1)
            nc.tensor.matmul(ps_w[:, 0, :], split[:, 0, :], w1[:, 0, :], start=True, stop=False)
            nc.tensor.matmul(ps_w[:, 0, :], split[:, 1, :], w1[:, 1, :], start=False, stop=True)
            nc.tensor.matmul(ps_w[0:D, 1, :], lin_wt[:, 2, :], w1[:, 2, :], start=True, stop=True)
            nc.tensor.matmul(ps_w[:, 2, :], bias_01[:, 0:1].broadcast_to([P, P]), w1_01[:, :], start=True, stop=False)
            nc.tensor.matmul(ps_w[:, 2, :], bias_2[:, 0:1].broadcast_to([D, P]), w1_2[:, :], start=False, stop=True).then_inc(folded, 1)
            pe.wait_ge(fold_taken, 2)
            pe.wait_ge(sums_ready, 1)
            for b in range(NB + 1):
                if b < NB:
                    if b >= 2:
                        pe.wait_ge(block_taken, 2 * (b - 1))
                    nc.tensor.transpose(ps_l[:, b % 2, 0:P], norm[:, b, 0:2 * D], m.ident[:, :])
                    nc.tensor.transpose(ps_r[:, b % 2, 0:P], norm[:, b, 2 * D:HEADS * D], m.ident[:, :]).then_inc(block_t, 1)
                if b >= 1:
                    q = b - 1
                    pe.wait_ge(block_taken, 2 * b)
                    if q >= 16 and q % 8 == 0:
                        pe.wait_ge(drained, q // 8 - 1)
                    o = ps_y[:, q // 8 % 2, q % 8 * D:(q % 8 + 1) * D]
                    nc.tensor.matmul(o, left[:, q % 2, :], fold_01[:, :], start=True, stop=False)
                    nc.tensor.matmul(o, right[:, q % 2, :], fold_2[:, :], start=False, stop=True).then_inc(done, 1)
            pe.wait_ge(y_ready, 1)
            for b in range(NB + 1):
                if b < NB:
                    pe.wait_ge(block_taken, 2 * NB + max(b - 1, 0))
                    nc.tensor.transpose(ps_r[:, b % 2, 0:P], y[:, b, :], m.ident[:, :]).then_inc(block_t, 1)
                if b >= 1:
                    q = b - 1
                    pe.wait_ge(block_taken, 2 * NB + b)
                    g = q // 8
                    if q % 8 == 0:
                        pe.wait_ge(drained, 7 + max(g - 1, 0))
                    nc.tensor.matmul(ps_y[:, g % 2, q % 8 * D:(q % 8 + 1) * D], right[:, q % 2, :], w2[:, :], start=True, stop=True).then_inc(done, 1)

        @block.scalar
        def _(act):
            for b in range(NB):
                act.wait_ge(block_t, b + 1)
                if b >= 2:
                    act.wait_ge(done, b - 1)
                nc.scalar.copy(left[:, b % 2, :], ps_l[:, b % 2, 0:P]).then_inc(block_taken, 1)
                nc.scalar.copy(right[:, b % 2, :], ps_r[:, b % 2, 0:P]).then_inc(block_taken, 1)
            root(nc, act, t, var, std, 1)
            for b in range(NB):
                act.wait_ge(block_t, NB + b + 1)
                act.wait_ge(done, NB + max(b - 1, 0))
                nc.scalar.copy(right[:, b % 2, :], ps_r[:, b % 2, 0:P]).then_inc(block_taken, 1)
            root(nc, act, t, var, std, 2)
            root(nc, act, t, var, std, 3)

        @block.vector
        def _(dve):
            link = linker(dve, chain)
            link(nc.vector.memset(split[:, :, :], 0.0))
            dve.wait_ge(loaded, 16 * 13)
            link(nc.vector.tensor_copy(split[:, 0, 0:D], lin_wt[:, 0, :]))
            nc.vector.tensor_copy(split[:, 1, D:2 * D], lin_wt[:, 1, :]).then_inc(padded, 1)
            dve.wait_ge(folded, 1)
            nc.vector.tensor_copy(fold_01[:, :], ps_w[:, 0, :]).then_inc(fold_taken, 1)
            nc.vector.tensor_copy(fold_2[:, :], ps_w[0:D, 1, :]).then_inc(fold_taken, 1)
            link(nc.vector.tensor_tensor(bias[:, :], vec[:, 0, :], ps_w[:, 2, :], ALU.add))
            dve.wait_ge(gathered, 16 * NB)
            link(nc.vector.tensor_tensor(den[:, :, :], sums_h[:, :, :, TW - 1], m.self_w[:, :, :], ALU.add))
            link(nc.vector.reciprocal(den[:, :, :], den[:, :, :]))
            for hd in range(HEADS):
                part = sums_h[:, :, hd, 0:D]
                link(nc.vector.tensor_tensor(z[:, :, :], m.h[:, :, :], bcast(m.self_w[:, :, hd], D), ALU.mult))
                link(nc.vector.tensor_tensor(part, part, z[:, :, :], ALU.add))
                ins = nc.vector.tensor_tensor(norm[:, :, hd * D:(hd + 1) * D], part, bcast(den[:, :, hd], D), ALU.mult)
                if hd < HEADS - 1:
                    link(ins)
                else:
                    ins.then_inc(sums_ready, 1)
            wide = lambda i, n=NB: (vec[:, i, :] if isinstance(i, int) else i).unsqueeze(1).broadcast_to([P, n, D])

            def drain(first, add):
                for g in range(7):
                    lo, hi = g * 8, min(g * 8 + 8, NB)
                    dve.wait_ge(done, first + hi)
                    nc.vector.tensor_tensor(z[:, lo:hi, :], ps_y[:, g % 2, 0:(hi - lo) * D].rearrange("p (b w) -> p b w", w=D),
                                            wide(add, hi - lo), ALU.add).then_inc(drained, 1)

            drain(0, bias[:, :])
            dve.wait_ge(drained, 7)
            link(nc.vector.tensor_tensor(z[:, :, :], z[:, :, :], m.h[:, :, :], ALU.add))
            layer_norm(nc, link, dve, y[:, :, :], z[:, :, :], t, var, std, 1)
            link(nc.vector.tensor_tensor(y[:, :, :], y[:, :, :], wide(1), ALU.mult))
            nc.vector.tensor_tensor(y[:, :, :], y[:, :, :], wide(2), ALU.add).then_inc(y_ready, 1)
            dve.wait_ge(y_ready, 1)
            drain(NB, 3)
            dve.wait_ge(drained, 14)
            link(nc.vector.tensor_tensor(z[:, :, :], z[:, :, :], y[:, :, :], ALU.add))
            layer_norm(nc, link, dve, y[:, :, :], z[:, :, :], t, var, std, 2)
            link(nc.vector.tensor_tensor(y[:, :, :], y[:, :, :], wide(4), ALU.mult))
            link(nc.vector.tensor_tensor(y[:, :, :], y[:, :, :], wide(5), ALU.add))
            link(nc.vector.tensor_tensor(m.x[:, :, :], m.x[:, :, :], y[:, :, :], ALU.add))
            layer_norm(nc, link, dve, m.h[:, :, :], m.x[:, :, :], t, var, std, 3)
            link(nc.vector.tensor_scalar(m.h[:, :, :], m.h[:, :, :], 0.0, None, ALU.max))


LAYERS = 3


def phase_light(nc, m, d, acc):
    with ExitStack() as ctx:
        s = Scope(nc, ctx, "li")
        rows = s.sb("rows", [P, BUFS, U * D])
        index = s.sb("index", [P, BUFS, U], I32)
        hot = s.sb("hot", [P, BUFS, U, P])
        by_rank = s.sb("by_rank", [P, RB, D])
        node = s.sb("node", [P, NB, D])
        ps_o = s.ps("ps_o", [D, 2, PER, P])
        ps_r = s.ps("ps_r", [P, 2, 512])
        index_ready, hot_ready, product, added = (s.sem(n) for n in ("index_ready", "hot_ready", "product", "added"))
        rows_in = [s.sem(f"rows_in{b}") for b in range(BUFS)]
        table_out, rows_t, rows_taken, stored, gathered, mean_ready = (s.sem(n) for n in ("table_out", "rows_t", "rows_taken", "stored", "gathered", "mean_ready"))
        G = 7
        BANKS = U // PER
        block = ctx.enter_context(nc.Block())

        @block.gpsimd
        def _(pool):
            with pool.Fori(0, LAYERS) as n:
                pool.wait_ge(table_out, n * 16 + 16)
                gather_pass(pool, rows, index, d["table"], D, index_ready, rows_in, n)
                pool.wait_ge(stored, n * 16 + 16)
                pool.nop(nofuse=True)
                gather_nodes(nc, pool, m, node, d["rank_feat"], gathered)

        @block.sync
        def _(sp):
            sp.dma_start(d["table"].rearrange("(p b) w -> p b w", b=NB), m.h[:, :, :]).then_inc(table_out, 16)
            with sp.Fori(0, LAYERS) as n:
                sp.wait_ge(rows_taken, n * G + G)
                sp.dma_start(d["rank_feat"][0:RANKS, :].rearrange("(r p) w -> p r w", p=P), by_rank[:, :, :]).then_inc(stored, 16)
                sp.wait_ge(mean_ready, n + 1)
                sp.dma_start(d["table"].rearrange("(p b) w -> p b w", b=NB), node[:, :, :]).then_inc(table_out, 16)
            sp.wait_ge(table_out, 16 * (LAYERS + 1))

        @block.scalar
        def _(act):
            with act.Fori(0, LAYERS) as n:
                def step(k, j):
                    c, r, b = stage(k, j, 0)
                    act.wait_ge(product, n * ((CHUNKS + BUFS) * BANKS) + c * BANKS + BANKS)
                    nc.scalar.copy(index[:, b, :], m.src[:, bass.ds(c * U, U)]).then_inc(index_ready, 1)
                loop_steps(act, step, 0)
                take_rows(nc, act, ps_r, by_rank, rows_t, rows_taken, D, 8, n * G)

        @block.tensor
        def _(pe):
            with pe.Fori(0, LAYERS) as n:
                pe.sem_inc(product, BUFS * BANKS)

                def step(k, j):
                    c, r, b = stage(k, j, 0)
                    pe.wait_ge(rows_in[b], n * (16 * U * LOOPS) + (r + 1) * (16 * U))
                    pe.wait_ge(hot_ready, n * CHUNKS + c + 1)
                    for u in range(U):
                        if u % PER == 0:
                            pe.wait_ge(added, n * (TILES + U) + c * U + (u + PER))
                        last = nc.tensor.matmul(ps_o[:, u // PER, u % PER, :], rows[:, b, u * D:(u + 1) * D], hot[:, b, u, :], start=True, stop=True)
                        if u % PER == PER - 1:
                            last.then_inc(product, 1)
                loop_steps(pe, step, 0)
                pe.wait_ge(added, n * (TILES + U) + TILES + U)
                pe.nop(nofuse=True)
                rows_by_rank(nc, pe, acc, ps_r, m.ident, rows_t, rows_taken, D, D, 8, n * G)

        @block.vector
        def _(dve):
            with dve.Fori(0, LAYERS) as n:
                nc.vector.memset(acc[:, :], 0.0).then_inc(added, U)

                def step(k, j):
                    if now := stage(k, j, 0):
                        c, r, b = now
                        dve.wait_ge(product, n * ((CHUNKS + BUFS) * BANKS) + c * BANKS + BANKS)
                        one_hot(nc, hot[:, b], m.iota[:, :], m.local[:, bass.ds(c * U, U)]).then_inc(hot_ready, 1)
                    if now := stage(k, j, 1):
                        add_windows(nc, dve, acc[:, :], lambda u: ps_o[:, u // PER, u % PER, :], m.starts, product, added, now[0], PER, n)
                loop_steps(dve, step, 1)
                dve.wait_ge(gathered, n * (16 * NB) + 16 * NB)
                nc.vector.tensor_tensor(node[:, :, :], node[:, :, :], bcast(m.inv_count[:, :], D), ALU.mult).then_inc(mean_ready, 1)
            dve.wait_ge(mean_ready, LAYERS)
            nc.vector.tensor_tensor(m.x[:, :, :], m.x[:, :, :], node[:, :, :], ALU.add)


def phase_edge_tables(nc, m, d):
    with ExitStack() as ctx:
        s = Scope(nc, ctx, "et")
        t = Norm(s)
        w = s.sb("w", [D, 2, D])
        b1 = s.sb("b1", [P, D])
        h_t = s.sb("h_t", [D, 2, P])
        at_dst, at_src = s.sb("at_dst", [P, NB, D]), s.sb("at_src", [P, NB, D])
        ps_t = s.ps("ps_t", [D, 2, 512])
        ps_y = s.ps("ps_y", [P, 2, 4, 2, D])
        loaded, var, std, chain, h_ready, w_ready = (s.sem(n) for n in ("loaded", "var", "std", "chain", "h_ready", "w_ready"))
        transposed, taken, done, src_ready, dst_ready, stored, scattered = (s.sem(n) for n in ("transposed", "taken", "done", "src_ready", "dst_ready", "stored", "scattered"))
        G = -(-NB // 4)
        block = ctx.enter_context(nc.Block())

        @block.sync
        def _(sp):
            sp.dma_start(w[:, :, :], d["w1e"].rearrange("(a i) o -> i a o", a=2)).then_inc(loaded, 16)
            sp.dma_start(b1[:, :], d["b1e"].unsqueeze(0).broadcast_to([P, D])).then_inc(loaded, 16)
            sp.wait_ge(src_ready, G)
            sp.dma_start(d["table"].rearrange("(p b) w -> p b w", b=NB), at_src[:, :, :]).then_inc(stored, 16)
            sp.wait_ge(stored, 16)
            sp.wait_ge(loaded, 32)

        @block.gpsimd
        def _(pool):
            pool.wait_ge(dst_ready, G)
            scatter_nodes(nc, pool, m, d["win"], at_dst, scattered)
            pool.wait_ge(scattered, 16 * NB)

        @block.scalar
        def _(act):
            root(nc, act, t, var, std, 1)
            for b in range(NB):
                act.wait_ge(transposed, b + 1)
                if b >= 2:
                    act.wait_ge(done, b - 1)
                nc.scalar.copy(h_t[:, b % 2, :], ps_t[:, b % 2, 0:P]).then_inc(taken, 1)

        @block.tensor
        def _(pe):
            pe.wait_ge(h_ready, 1)
            pe.wait_ge(w_ready, 1)
            for b in range(NB + 1):
                if b < NB:
                    if b >= 2:
                        pe.wait_ge(taken, b - 1)
                    nc.tensor.transpose(ps_t[:, b % 2, 0:P], m.h[:, b, :], m.ident[:, :]).then_inc(transposed, 1)
                if b >= 1:
                    q = b - 1
                    pe.wait_ge(taken, b)
                    if q >= 8 and q % 4 == 0:
                        pe.wait_ge(src_ready, q // 4 - 1)
                        pe.wait_ge(dst_ready, q // 4 - 1)
                    nc.tensor.matmul(ps_y[:, q // 4 % 2, q % 4, :, :], h_t[:, q % 2, :], w[:, :, :], start=True, stop=True).then_inc(done, 1)

        @block.vector
        def _(dve):
            link = linker(dve, chain)
            dve.wait_ge(loaded, 32)
            nc.vector.tensor_tensor(w[:, 0, :], w[:, 0, :], w[:, 1, :], ALU.subtract).then_inc(w_ready, 1)
            layer_norm(nc, link, dve, m.h[:, :, :], m.x[:, :, :], t, var, std, 1)
            nc.vector.tensor_scalar(m.h[:, :, :], m.h[:, :, :], 0.0, None, ALU.max).then_inc(h_ready, 1)
            for g in range(G):
                lo, hi = g * 4, min(g * 4 + 4, NB)
                dve.wait_ge(done, hi)
                nc.vector.tensor_tensor(at_dst[:, lo:hi, :], ps_y[:, g % 2, 0:hi - lo, 0, :], b1[:, :].unsqueeze(1).broadcast_to([P, hi - lo, D]),
                                        ALU.add).then_inc(dst_ready, 1)
                nc.vector.tensor_copy(at_src[:, lo:hi, :], ps_y[:, g % 2, 0:hi - lo, 1, :]).then_inc(src_ready, 1)


def phase_edge_max(nc, m, d, acc):
    with ExitStack() as ctx:
        s = Scope(nc, ctx, "em")
        rows = s.sb("rows", [P, BUFS, STREAMS, PER, D])
        index = s.sb("index", [P, BUFS, U], I32)
        wide = s.sb("wide", [P, BUFS, STREAMS, PER * P], BF16)
        win = s.sb("win", [P, BUFS, U, D])
        reset = s.sb("reset", [STREAMS * D, BUFS, PER * P])
        hot_t = s.sb("hot_t", [P, 2, U, P])
        hot_last = s.sb("hot_last", [P, BUFS, U, P])
        both = s.sb("both", [P, 2, PER, STREAMS * D])
        hidden = s.sb("hidden", [STREAMS * D, 2, PER * P])
        run = s.sb("run", [STREAMS * D, 2, PER * P])
        back = s.sb("back", [P, 2, PER, STREAMS * D])
        w2 = s.sb("w2", [STREAMS * D, STREAMS * D])
        border = s.sb("border", [D, 1])
        ps_z = s.ps("ps_z", [P, U, D])
        ps_h = s.ps("ps_h", [STREAMS * D, PER * P])
        ps_m = s.ps("ps_m", [STREAMS * D, 2, PER * P])
        ps_b = s.ps("ps_b", [P, PER, STREAMS * D])
        ps_o = s.ps("ps_o", [D, 2, PER, P])
        rows_in, win_in, local_in, reset_in = ([s.sem(f"{n}{b}") for b in range(BUFS)] for n in ("rows_in", "win_in", "local_in", "reset_in"))
        index_ready, hot_t_ready, hot_ready, spread, both_ready = (s.sem(n) for n in ("index_ready", "hot_t_ready", "hot_ready", "spread", "both_ready"))
        both_t, hidden_ready, message, run_ready, back_t, back_ready = (s.sem(n) for n in ("both_t", "hidden_ready", "message", "run_ready", "back_t", "back_ready"))
        product, added, w_in, w_clear, chain = (s.sem(n) for n in ("product", "added", "w_in", "w_clear", "chain"))
        BANKS = U // PER
        block = ctx.enter_context(nc.Block())

        @block.gpsimd
        def _(pool):
            flat = rows[:, :, :, :, :].rearrange("p b s i w -> p b (s i w)")
            gather_pass(pool, flat, index, d["table"], D, index_ready, rows_in)

        @block.sync
        def _(sp):
            sp.wait_ge(w_clear, 1)
            for st in range(STREAMS):
                sp.dma_start(w2[st * D:(st + 1) * D, st * D:(st + 1) * D], d["w2e"]).then_inc(w_in, 16)
            sp.dma_start(border[:, :], d["reset_rows"][HALF * P:HALF * P + 1].unsqueeze(0).broadcast_to([D, 1])).then_inc(w_in, 16)

            def step(k, j):
                c, r, b = stage(k, j, 0)
                sp.wait_ge(spread, c + 1)
                load_windows(nc, sp, win, wide, d["win"], m.starts, c, b, win_in[b], d["local_rows"], local_in[b])
                sp.wait_ge(run_ready, c + 1)
                sp.nop(nofuse=True)
                for st in range(STREAMS):
                    sp.dma_start(reset[st * D:(st + 1) * D, b, :], chunk_row(d["reset_rows"], c, st, D)).then_inc(reset_in[b], 16)
            loop_steps(sp, step, 0)
            sp.wait_ge(w_in, 48)

        @block.scalar
        def _(act):
            act.sem_inc(back_ready, 2)
            act.sem_inc(hidden_ready, 2)

            def step(k, j):
                if now := stage(k, j, 0):
                    c, r, b = now
                    act.wait_ge(both_ready, c + 1)
                    nc.scalar.copy(index[:, b, :], m.src[:, bass.ds(c * U, U)]).then_inc(index_ready, 1)
                if now := stage(k, j, 2):
                    c, r, b = now
                    act.wait_ge(both_t, c + 3)
                    act.wait_ge(message, c + 1)
                    nc.scalar.activation(hidden[:, b % 2, :], ps_h[:, :], ACT.Relu).then_inc(hidden_ready, 1)
                if now := stage(k, j, 3):
                    c, r, b = now
                    act.wait_ge(back_t, c + 3)
                    act.wait_ge(product, c * BANKS + 3 * BANKS)
                    nc.scalar.copy(back[:, b % 2, :, :], ps_b[:, :, :]).then_inc(back_ready, 1)
            loop_steps(act, step, 3)

        @block.tensor
        def _(pe):
            pe.sem_inc(spread, BUFS)
            pe.sem_inc(both_t, 2)
            pe.sem_inc(message, 2)
            pe.sem_inc(back_t, 2)
            pe.sem_inc(product, BUFS * BANKS)
            pe.wait_ge(w_in, 48)

            def step(k, j):
                if now := stage(k, j, 0):
                    c, r, b = now
                    pe.wait_ge(hot_t_ready, c + 1)
                    pe.wait_ge(win_in[b], (r + 1) * (16 * U))
                    pe.wait_ge(both_ready, c + BUFS)
                    for u in range(U):
                        last = nc.tensor.matmul(ps_z[:, u, :], hot_t[:, b % 2, u, :], win[:, b, u, :], start=True, stop=True)
                    last.then_inc(spread, 1)
                if now := stage(k, j, 2):
                    c, r, b = now
                    pe.wait_ge(both_ready, c + BUFS + 1)
                    pe.wait_ge(hidden_ready, c + 2)
                    for i in range(PER):
                        last = nc.tensor.transpose(ps_h[:, i * P:(i + 1) * P], both[:, b % 2, i, :], m.ident[:, :])
                    last.then_inc(both_t, 1)
                if now := stage(k, j, 3):
                    c, r, b = now
                    pe.wait_ge(run_ready, c + BUFS + 1)
                    pe.wait_ge(back_ready, c + 2)
                    for i in range(PER):
                        last = nc.tensor.transpose(ps_b[:, i, :], run[:, b % 2, i * P:(i + 1) * P], m.ident[:, :])
                    last.then_inc(back_t, 1)
                if now := stage(k, j, 2):
                    c, r, b = now
                    pe.wait_ge(hidden_ready, c + 3)
                    pe.wait_ge(run_ready, c + BUFS - 1)
                    nc.tensor.matmul(ps_m[:, b % 2, :], w2[:, :], hidden[:, b % 2, :], start=True, stop=True).then_inc(message, 1)
                if now := stage(k, j, 3):
                    c, r, b = now
                    pe.wait_ge(back_ready, c + 3)
                    pe.wait_ge(hot_ready, c + 1)
                    for u in range(U):
                        st, i = divmod(u, PER)
                        if u % PER == 0:
                            pe.wait_ge(added, c * U + (u + PER))
                        last = nc.tensor.matmul(ps_o[:, st, i, :], back[:, b % 2, i, st * D:(st + 1) * D], hot_last[:, b, u, :],
                                         start=True, stop=True)
                        if u % PER == PER - 1:
                            last.then_inc(product, 1)
            loop_steps(pe, step, 3)

        @block.vector
        def _(dve):
            link = linker(dve, chain)
            nc.vector.memset(w2[:, :], 0.0).then_inc(w_clear, 1)
            nc.vector.memset(acc[:, :], 0.0).then_inc(added, U)
            nc.vector.memset(run[:, :, :], -BIG).then_inc(run_ready, BUFS)
            dve.sem_inc(both_ready, BUFS)

            def step(k, j):
                if now := stage(k, j, 0):
                    c, r, b = now
                    dve.wait_ge(spread, c + BUFS - 1)
                    dve.wait_ge(local_in[b], (r + 1) * 16)
                    nc.vector.tensor_scalar(hot_t[:, b % 2, :, :].rearrange("p u e -> p (u e)"), wide[:, b, :, :].rearrange("p s e -> p (s e)"),
                                            m.lane[:, :], None, ALU.is_equal).then_inc(hot_t_ready, 1)
                    dve.wait_ge(product, c * BANKS + BANKS)
                    one_hot(nc, hot_last[:, b], m.iota[:, :], m.last[:, bass.ds(c * U, U)]).then_inc(hot_ready, 1)
                if now := stage(k, j, 2):
                    c, r, b = now
                    dve.wait_ge(message, c + 3)
                    dve.wait_ge(reset_in[b], (r + 1) * (16 * STREAMS))
                    dve.wait_ge(back_t, c + 1)
                    dve.wait_ge(run_ready, c + BUFS)
                    nc.vector.tensor_tensor_scan(run[:, b % 2, :], reset[:, b, :], ps_m[:, b % 2, :],
                                                 run[:, (b + 1) % 2, PER * P - 1:PER * P], ALU.add, ALU.max).then_inc(run_ready, 1)
                if now := stage(k, j, 3):
                    add_windows(nc, dve, acc[:, :], lambda u: ps_o[:, u // PER, u % PER, :], m.starts, product, added, now[0], PER)
                if now := stage(k, j, 0):
                    c, r, b = now
                    dve.wait_ge(spread, c + BUFS + 1)
                    dve.wait_ge(rows_in[b], (r + 1) * (16 * U))
                    dve.wait_ge(both_t, c + 1)
                    nc.vector.tensor_tensor(both[:, b % 2, :, :].rearrange("p i (s w) -> p s i w", s=STREAMS), rows[:, b, :, :, :],
                                            ps_z[:, :, :].rearrange("p (s i) w -> p s i w", s=STREAMS), ALU.add).then_inc(both_ready, 1)
            loop_steps(dve, step, 3)
            dve.wait_ge(w_in, 48)
            dve.wait_ge(run_ready, CHUNKS + BUFS)
            link(nc.vector.tensor_tensor(border[:, :], border[:, :], run[0:D, (CHUNKS - 1) % 2, PER * P - 1:PER * P], ALU.add))
            dve.wait_ge(added, TILES + U)
            first = nc.vector.value_load(m.starts[0:1, PER:PER + 1], min_val=0, max_val=RANKS - P)
            link(nc.vector.tensor_tensor(acc[:, bass.ds(first, 1)], acc[:, bass.ds(first, 1)], border[:, :], ALU.max))


def phase_edge_out(nc, m, d, acc):
    with ExitStack() as ctx:
        s = Scope(nc, ctx, "eo")
        t = Norm(s)
        by_rank = s.sb("by_rank", [P, RB, D])
        node = s.sb("node", [P, NB, D])
        b2 = s.sb("b2", [P, D])
        has = s.sb("has", [P, NB])
        rank_f = s.sb("rank_f", [P, NB])
        ps = s.ps("ps", [P, 2, 512])
        rows_t, rows_taken, stored, gathered, loaded = (s.sem(n) for n in ("rows_t", "rows_taken", "stored", "gathered", "loaded"))
        chain, var, std, h_ready, scattered = (s.sem(n) for n in ("chain", "var", "std", "h_ready", "scattered"))
        block = ctx.enter_context(nc.Block())

        @block.tensor
        def _(pe):
            rows_by_rank(nc, pe, acc, ps, m.ident, rows_t, rows_taken, D, D, 8)

        @block.scalar
        def _(act):
            take_rows(nc, act, ps, by_rank, rows_t, rows_taken, D, 8)
            root(nc, act, t, var, std, 1)

        @block.sync
        def _(sp):
            sp.dma_start(b2[:, :], d["b2e"].unsqueeze(0).broadcast_to([P, D])).then_inc(loaded, 16)
            sp.wait_ge(rows_taken, 7)
            sp.dma_start(d["rank_feat"][0:RANKS, :].rearrange("(r p) w -> p r w", p=P), by_rank[:, :, :]).then_inc(stored, 16)
            sp.wait_ge(h_ready, 1)
            sp.dma_start(d["table"].rearrange("(p b) w -> p b w", b=NB), m.h[:, :, :]).then_inc(stored, 16)
            sp.wait_ge(stored, 32)
            sp.wait_ge(loaded, 16)

        @block.gpsimd
        def _(pool):
            pool.wait_ge(stored, 16)
            gather_nodes(nc, pool, m, node, d["rank_feat"], gathered)
            pool.wait_ge(h_ready, 1)
            scatter_nodes(nc, pool, m, d["win"], m.h, scattered)
            pool.wait_ge(scattered, 16 * NB)

        @block.vector
        def _(dve):
            link = linker(dve, chain)
            link(nc.vector.tensor_copy(rank_f[:, :], m.rank_of[:, :]))
            link(nc.vector.tensor_scalar(has[:, :], rank_f[:, :], float(TRASH), None, ALU.is_lt))
            dve.wait_ge(loaded, 16)
            dve.wait_ge(gathered, 16 * NB)
            link(nc.vector.tensor_tensor(node[:, :, :], node[:, :, :], b2[:, :].unsqueeze(1).broadcast_to([P, NB, D]), ALU.add))
            link(nc.vector.tensor_tensor(node[:, :, :], node[:, :, :], bcast(has[:, :], D), ALU.mult))
            link(nc.vector.tensor_tensor(m.x[:, :, :], m.x[:, :, :], node[:, :, :], ALU.add))
            layer_norm(nc, link, dve, m.h[:, :, :], m.x[:, :, :], t, var, std, 1)
            nc.vector.tensor_scalar(m.h[:, :, :], m.h[:, :, :], 0.0, None, ALU.max).then_inc(h_ready, 1)


def phase_dot(nc, m, d, acc):
    with ExitStack() as ctx:
        s = Scope(nc, ctx, "dt")
        rows = s.sb("rows", [P, BUFS, U, D])
        index = s.sb("index", [P, BUFS, U], I32)
        wide = s.sb("wide", [P, BUFS, STREAMS, PER * P], BF16)
        win = s.sb("win", [P, BUFS, U, D])
        hot = s.sb("hot", [P, BUFS, U, P])
        hot_t = s.sb("hot_t", [P, 2, U, P])
        prod = s.sb("prod", [P, 2, U, D])
        dot = s.sb("dot", [P, 2, U])
        scaled = s.sb("scaled", [P, 2, U, D])
        ps_z = s.ps("ps_z", [P, 2, U, D])
        ps_o = s.ps("ps_o", [D, 2, PER, P])
        rows_in, win_in, local_in = ([s.sem(f"{n}{b}") for b in range(BUFS)] for n in ("rows_in", "win_in", "local_in"))
        index_ready, hot_ready, hot_t_ready, spread = (s.sem(n) for n in ("index_ready", "hot_ready", "hot_t_ready", "spread"))
        prod_ready, dot_ready, scaled_ready, product, added = (s.sem(n) for n in ("prod_ready", "dot_ready", "scaled_ready", "product", "added"))
        BANKS = U // PER
        block = ctx.enter_context(nc.Block())

        @block.gpsimd
        def _(pool):
            gather_pass(pool, rows[:, :, :, :].rearrange("p b u w -> p b (u w)"), index, d["table"], D, index_ready, rows_in)

        @block.sync
        def _(sp):
            def step(k, j):
                c, r, b = stage(k, j, 0)
                sp.wait_ge(spread, c + 1)
                load_windows(nc, sp, win, wide, d["win"], m.starts, c, b, win_in[b], d["local_rows"], local_in[b])
            loop_steps(sp, step, 0)

        @block.scalar
        def _(act):
            def step(k, j):
                c, r, b = stage(k, j, 0)
                act.wait_ge(scaled_ready, c + 1)
                nc.scalar.copy(index[:, b, :], m.src[:, bass.ds(c * U, U)]).then_inc(index_ready, 1)
            loop_steps(act, step, 0)

        @block.tensor
        def _(pe):
            pe.sem_inc(spread, BUFS)
            pe.sem_inc(product, BUFS * BANKS)

            def step(k, j):
                if now := stage(k, j, 0):
                    c, r, b = now
                    pe.wait_ge(hot_t_ready, c + 1)
                    pe.wait_ge(win_in[b], (r + 1) * (16 * U))
                    pe.wait_ge(prod_ready, c + 1)
                    for u in range(U):
                        last = nc.tensor.matmul(ps_z[:, b % 2, u, :], hot_t[:, b % 2, u, :], win[:, b, u, :], start=True, stop=True)
                    last.then_inc(spread, 1)
                if now := stage(k, j, 1):
                    c, r, b = now
                    pe.wait_ge(scaled_ready, c + BUFS + 1)
                    pe.wait_ge(hot_ready, c + 1)
                    for u in range(U):
                        if u % PER == 0:
                            pe.wait_ge(added, c * U + (u + PER))
                        last = nc.tensor.matmul(ps_o[:, u // PER, u % PER, :], scaled[:, b % 2, u, :], hot[:, b, u, :], start=True, stop=True)
                        if u % PER == PER - 1:
                            last.then_inc(product, 1)
            loop_steps(pe, step, 1)

        @block.vector
        def _(dve):
            nc.vector.memset(acc[:, :], 0.0).then_inc(added, U)
            dve.sem_inc(scaled_ready, BUFS)
            dve.sem_inc(prod_ready, 2)

            def step(k, j):
                if now := stage(k, j, 0):
                    c, r, b = now
                    dve.wait_ge(spread, c + BUFS - 1)
                    dve.wait_ge(local_in[b], (r + 1) * 16)
                    nc.vector.tensor_scalar(hot_t[:, b % 2, :, :].rearrange("p u e -> p (u e)"), wide[:, b, :, :].rearrange("p s e -> p (s e)"),
                                            m.lane[:, :], None, ALU.is_equal).then_inc(hot_t_ready, 1)
                    dve.wait_ge(product, c * BANKS + BANKS)
                    one_hot(nc, hot[:, b], m.iota[:, :], m.local[:, bass.ds(c * U, U)]).then_inc(hot_ready, 1)
                if now := stage(k, j, 1):
                    add_windows(nc, dve, acc[:, :], lambda u: ps_o[:, u // PER, u % PER, :], m.starts, product, added, now[0], PER)
                if now := stage(k, j, 0):
                    c, r, b = now
                    dve.wait_ge(spread, c + BUFS + 1)
                    dve.wait_ge(rows_in[b], (r + 1) * (16 * U))
                    nc.vector.tensor_tensor(prod[:, b % 2, :, :], rows[:, b, :, :], ps_z[:, b % 2, :, :], ALU.mult).then_inc(prod_ready, 1)
                    dve.wait_ge(prod_ready, c + 3)
                    nc.vector.tensor_reduce(out=dot[:, b % 2, :], in_=prod[:, b % 2, :, :], axis=AX.X, op=ALU.add).then_inc(dot_ready, 1)
                    dve.wait_ge(dot_ready, c + 1)
                    dve.wait_ge(product, c * BANKS + 3 * BANKS)
                    nc.vector.tensor_tensor(scaled[:, b % 2, :, :], rows[:, b, :, :], dot[:, b % 2, :].unsqueeze(2).broadcast_to([P, U, D]),
                                            ALU.mult).then_inc(scaled_ready, 1)
            loop_steps(dve, step, 1)
            dve.wait_ge(added, TILES + U)


def phase_dot_out(nc, m, d, acc):
    with ExitStack() as ctx:
        s = Scope(nc, ctx, "do")
        by_rank = s.sb("by_rank", [P, RB, D])
        node = s.sb("node", [P, NB, D])
        fc = s.sb("fc", [D, D])
        ps = s.ps("ps", [P, 2, 512])
        rows_t, rows_taken, stored, gathered, loaded, x_ready, out_done = (s.sem(n) for n in ("rows_t", "rows_taken", "stored", "gathered", "loaded", "x_ready", "out_done"))
        block = ctx.enter_context(nc.Block())

        @block.tensor
        def _(pe):
            pe.wait_ge(loaded, 16)
            for r in range(RB):
                g = r // 8
                if g >= 2 and r % 8 == 0:
                    pe.wait_ge(rows_taken, g - 1)
                last = nc.tensor.matmul(ps[:, g % 2, r % 8 * D:(r % 8 + 1) * D], acc[:, r * P:(r + 1) * P], fc[:, :], start=True, stop=True)
                if r % 8 == 7 or r == RB - 1:
                    last.then_inc(rows_t, 1)

        @block.scalar
        def _(act):
            take_rows(nc, act, ps, by_rank, rows_t, rows_taken, D, 8)

        @block.sync
        def _(sp):
            sp.dma_start(fc[:, :], d["fc_t"]).then_inc(loaded, 16)
            sp.wait_ge(rows_taken, 7)
            sp.dma_start(d["rank_feat"][0:RANKS, :].rearrange("(r p) w -> p r w", p=P), by_rank[:, :, :]).then_inc(stored, 16)
            sp.wait_ge(x_ready, 1)
            sp.dma_start(d["out"][0:LASTP * NB, :].rearrange("(p b) w -> p b w", b=NB), m.x[0:LASTP, :, :]).then_inc(out_done, 16)
            sp.dma_start(d["out"][LASTP * NB:N, :].rearrange("(p b) w -> p b w", b=LASTB), m.x[LASTP:LASTP + 1, 0:LASTB, :]).then_inc(out_done, 16)
            sp.wait_ge(out_done, 32)

        @block.gpsimd
        def _(pool):
            pool.wait_ge(stored, 16)
            gather_nodes(nc, pool, m, node, d["rank_feat"], gathered)

        @block.vector
        def _(dve):
            dve.wait_ge(gathered, 16 * NB)
            nc.vector.tensor_tensor(m.x[:, :, :], m.x[:, :, :], node[:, :, :], ALU.add).then_inc(x_ready, 1)


def build(nc, d):
    def dram(name, shape, dt=F32):
        return nc.dram_tensor(name, shape, dt, kind="Internal").ap()

    d["starts"] = dram("starts", [TILES], I32)
    d["local_rows"] = dram("local_rows", [TILES * P], BF16)
    d["reset_rows"] = dram("reset_rows", [TILES * P])
    d["table0"] = dram("table0", [NPAD, TW])
    d["table"] = dram("table", [NPAD, D])
    d["saved"] = dram("saved", [CHUNKS * P, U * TW])
    d["rank8"] = dram("rank8", [CROWS, 2 * AW])
    d["rank_heads"] = dram("rank_heads", [CROWS, HEADS * TW])
    d["rank_feat"] = dram("rank_feat", [CROWS, D])
    d["rank_of"] = dram("rank_of", [TRASH + RANKS, 1], I32)
    d["win8"] = dram("win8", [CROWS, 2 * AW])
    d["win"] = dram("win", [CROWS, D])
    with ExitStack() as ctx:
        s = Scope(nc, ctx, "all")
        m = Memory(s)
        phase_ranks(nc, m, d)
        with ExitStack() as gat:
            g = Scope(nc, gat, "gat")
            edge = Edges(g)
            phase_table(nc, m, d, edge)
            with ExitStack() as c:
                acc = Scope(nc, c, "g1").sb("acc", [P, 2, RANKS])
                phase_gat_max(nc, m, d, edge, acc)
                phase_gat_nodes(nc, m, d, acc)
                phase_gat_sum(nc, m, d, edge, acc)
                phase_gat_rows(nc, m, d, acc)
        phase_gat_out(nc, m, d)
        acc = s.sb("acc", [D, RANKS])
        phase_light(nc, m, d, acc)
        phase_edge_tables(nc, m, d)
        phase_edge_max(nc, m, d, acc)
        phase_edge_out(nc, m, d, acc)
        phase_dot(nc, m, d, acc)
        phase_dot_out(nc, m, d, acc)


def kernel(**inputs):
    import concourse.bacc as bacc
    import numpy as np
    from concourse.bass_utils import run_bass_kernel_spmd

    a = {k: np.asarray(v) for k, v in inputs.items()}
    pad = TILES * P - E
    dst = np.concatenate([a["dst"], np.full(pad, N, np.int32)])

    def columns(v):
        t = v.reshape(STREAMS, CHUNKS, PER, P, *v.shape[1:])
        return np.ascontiguousarray(np.moveaxis(t, (3, 1, 0, 2), (0, 1, 2, 3)).reshape(P, -1))

    arrays = {
        "x": a["x"],
        "dst_rows": np.concatenate([np.full(1, -1, np.int32), dst, np.full(1, N + 1, np.int32)]),
        "dst_cols": columns(dst),
        "src_cols": columns(np.concatenate([a["src"], np.zeros(pad, np.int32)])),
        "attr_cols": columns(np.concatenate([a["edge_attr_5"], np.zeros((pad, EDIM), np.float32)])),
        "lin_w": a["L0_gnn_lin_w"], "lin_wt": np.ascontiguousarray(a["L0_gnn_lin_w"].T),
        "att_src": a["L0_gnn_att_src"], "att_dst": a["L0_gnn_att_dst"], "att_edge": a["L0_gnn_att_edge"],
        "lin_edge_w": a["L0_gnn_lin_edge_w"], "gat_bias": a["L0_gnn_gat_bias"],
        "w1": a["L0_gnn_w1"], "b1": a["L0_gnn_b1"], "ln1_g": a["L0_gnn_ln1_g"], "ln1_b": a["L0_gnn_ln1_b"],
        "w2": a["L0_gnn_w2"], "b2": a["L0_gnn_b2"], "ln2_g": a["L0_gnn_ln2_g"], "ln2_b": a["L0_gnn_ln2_b"],
        "w1e": a["L2_gnn_W1"], "b1e": a["L2_gnn_b1"], "w2e": a["L2_gnn_W2"], "b2e": a["L2_gnn_b2"],
        "fc_t": np.ascontiguousarray(a["L3_gnn_fc_weight"].T),
    }
    nc = bacc.Bacc("TRN2", target_bir_lowering=False, num_devices=1)
    d = {}
    for name, v in arrays.items():
        d[name] = nc.dram_tensor(f"in_{name}", v.shape, mybir.dt.from_np(v.dtype), kind="ExternalInput").ap()
    d["out"] = nc.dram_tensor("out", (N, D), F32, kind="ExternalOutput").ap()
    build(nc, d)
    got = run_bass_kernel_spmd(nc, [{f"in_{k}": v for k, v in arrays.items()}], core_ids=[0])
    return got.results[0]["out"]
```

```python
from contextlib import ExitStack

import concourse.bass as bass
from concourse import mybir

F32, BF16, I32 = mybir.dt.float32, mybir.dt.bfloat16, mybir.dt.int32
ALU, ACT, AX = mybir.AluOpType, mybir.ActivationFunctionType, mybir.AxisListType

P = 128
N, E, D = 6250, 200000, 64
HEADS, EDIM = 3, 5
SLOPE, EPS = 0.2, 1e-5
BIG = 1e38

STREAMS, PER = 2, 4
U = STREAMS * PER
PAIR = 2
BUFS = 4
TILES = -(-E // (P * U * BUFS)) * U * BUFS
CHUNKS = TILES // U
LOOPS = CHUNKS // BUFS
HALF = TILES // STREAMS
ROWP = 98
ROWT = TILES // ROWP
ROWE = ROWT * P

NB = -(-N // P)
LASTP, LASTB = N // NB, N % NB
NPAD = NB * P
RB = NB + 1
RANKS = RB * P
TRASH = RANKS
CROWS = TRASH + NPAD
ROWS = TILES * P
ENDROW = ((HALF // PER - 1) * P + P - 1) * U + (PER - 1) * STREAMS
BORDER = 1
TW = D + HEADS + 1
AW = HEADS + 1
WW = 2 * HEADS


class Norm:

    def __init__(self, s):
        self.stat = s.sb("stat", [P, NB])[:, :]
        self.square = s.sb("square", [P, NB, D])[:, :, :]


class Edges:

    def __init__(self, s):
        self.logit = s.sb("logit", [P, TILES, AW])


class Ranks:

    def __init__(self, s):
        self.dst = s.sb("dst", [P, TILES], I32)
        self.local = s.sb("local", [P, TILES])
        self.last = s.sb("last", [P, TILES])
        self.starts = s.sb("starts", [1, TILES], I32)


class Memory:

    def __init__(self, s):
        self.src = s.sb("src", [P, TILES], I32)
        self.x = s.sb("x", [P, NB, D])
        self.h = s.sb("h", [P, NB, D])
        self.node_no = s.sb("node_no", [P, NB])
        self.end_row = s.sb("end_row", [P, NB], I32)
        self.start_row = s.sb("start_row", [P, NB], I32)
        self.end_pos = s.sb("end_pos", [P, NB], I32)
        self.start_pos = s.sb("start_pos", [P, NB], I32)
        self.has = s.sb("has", [P, NB])
        self.first = s.sb("first", [1, 1], I32)
        self.join = s.sb("join", [P, NB])
        self.inv_count = s.sb("inv_count", [P, NB])
        self.logit = s.sb("logit", [P, NB, WW])
        self.self_w = s.sb("self_w", [P, NB, HEADS])
        self.iota = s.sb("iota", [P, P])
        self.lane = s.sb("lane", [P, 1])
        self.ident = s.sb("ident", [P, P])


def loop_steps(eng, body, skew):
    for j in range(BUFS):
        body(0, j)
    with eng.Fori(1, LOOPS) as k:
        for j in range(BUFS):
            body(k, j)
    for step in range(CHUNKS, CHUNKS + skew):
        body(step // BUFS, step % BUFS)


def stage(k, j, skew):
    if j < skew:
        k = k - 1
    b = (j - skew) % BUFS
    c = k * BUFS + b
    if isinstance(k, int) and not 0 <= c < CHUNKS:
        return None
    return c, k, b


def upto(c, back=0, layer=0):
    return layer * CHUNKS + c + (BUFS + 1 - back)


def flags_row(flags, kind, c, st, parts):
    part = flags[kind, bass.ds(c * (PER * P) + st * HALF * P, PER * P)]
    return part.unsqueeze(0).broadcast_to([parts, *part.shape])


def window_starts(nc, engine, starts, c):
    _, regs = nc.values_load_multi_w_load_instructions(
        starts[0:1, bass.ds(c * U, U)], engines=[engine], min_val=0, max_val=RANKS - P,
        skip_runtime_bounds_check_because="a rank is at most the number of nodes")
    return regs


def gather_pass(pool, rows, index, table, width, index_ready, rows_in, layer=0):
    def step(k, j):
        c, k, b = stage(k, j, 0)
        pool.wait_ge(index_ready, layer * CHUNKS + c + 1)
        pool.nop(nofuse=True)
        for u in range(U):
            pool.indirect_dma_start(rows[:, b, u * width:(u + 1) * width], None, table,
                                    bass.IndirectOffsetOnAxis(index[:, b, u:u + 1], 0)).then_inc(rows_in[b], 16)
    loop_steps(pool, step, 0)


def one_hot(nc, out, iota, local):
    return nc.vector.tensor_tensor(out, iota.unsqueeze(1).broadcast_to([P, U, P]),
                                   local.unsqueeze(2).broadcast_to([P, U, P]), ALU.is_equal)


class Scope:

    def __init__(self, nc, ctx, tag):
        self.nc, self.ctx, self.tag, self.sems = nc, ctx, tag, []

    def sb(self, name, shape, dt=F32):
        return self.ctx.enter_context(self.nc.sbuf_tensor(f"{self.tag}_{name}", shape, dt))

    def ps(self, name, shape, dt=F32):
        return self.ctx.enter_context(self.nc.psum_tensor(f"{self.tag}_{name}", shape, dt))

    def sem(self, name):
        if not self.sems:
            self.ctx.callback(self.clear)
        self.sems.append(self.nc.alloc_semaphore(f"{self.tag}_{name}"))
        return self.sems[-1]

    def clear(self):
        self.nc.clear_and_free_semaphores(self.sems)
        self.nc.all_engine_barrier()


def linker(eng, sem):
    count = [0]

    def link(ins):
        count[0] += 1
        ins.then_inc(sem, 1)
        eng.wait_ge(sem, count[0])
        return count[0]

    return link


def bcast(v, n):
    return v.unsqueeze(2).broadcast_to([P, NB, n])


def layer_norm(nc, link, dve, out, x, t, sem_var, sem_std, turn):
    link(nc.vector.tensor_reduce(out=t.stat, in_=x, axis=AX.X, op=ALU.add))
    link(nc.vector.tensor_scalar(t.stat, t.stat, 1.0 / D, None, ALU.mult))
    link(nc.vector.tensor_tensor(out, x, bcast(t.stat, D), ALU.subtract))
    link(nc.vector.tensor_tensor(t.square, out, out, ALU.mult))
    link(nc.vector.tensor_reduce(out=t.stat, in_=t.square, axis=AX.X, op=ALU.add))
    nc.vector.tensor_scalar(t.stat, t.stat, 1.0 / D, EPS, ALU.mult, ALU.add).then_inc(sem_var, 1)
    dve.wait_ge(sem_std, turn)
    link(nc.vector.reciprocal(t.stat, t.stat))
    link(nc.vector.tensor_tensor(out, out, bcast(t.stat, D), ALU.mult))


def root(nc, act, t, sem_var, sem_std, turn):
    act.wait_ge(sem_var, turn)
    nc.scalar.activation(t.stat, t.stat, ACT.Sqrt).then_inc(sem_std, 1)


def phase_ranks(nc, m, rk, d):
    with ExitStack() as ctx:
        s = Scope(nc, ctx, "rk")
        prev, cur, nxt = (s.sb(n, [ROWP, ROWE]) for n in ("prev", "cur", "next"))
        raw = s.sb("raw", [ROWP, 3, ROWE], I32)
        ones = s.sb("ones", [ROWP, ROWE])
        rank = s.sb("rank", [ROWP, ROWE])
        keep16 = s.sb("keep16", [ROWP, ROWE], BF16)
        reset16 = s.sb("reset16", [ROWP, ROWE], BF16)
        before = s.sb("before", [ROWP, ROWP])
        offset = s.sb("offset", [ROWP, 1])
        base = s.sb("base", [ROWP, ROWT])
        base_i = s.sb("base_i", [ROWP, ROWT], I32)
        starts_t = s.sb("starts_t", [1, TILES], I32)
        zeros = s.sb("zeros", [P, NB * HEADS * D])
        init = s.sb("init", [P, NB], I32)
        ps_off = s.ps("ps_off", [ROWP, 512])
        ps_t = s.ps("ps_t", [P, 4, 512])
        loaded, made, chain = s.sem("loaded"), s.sem("made"), s.sem("chain")
        counted, offset_ready, transposed, taken = (s.sem(n) for n in ("counted", "offset_ready", "transposed", "taken"))
        stored, zeroed, base_ready, rows_ready = (s.sem(n) for n in ("stored", "zeroed", "base_ready", "rows_ready"))
        starts_in, zero_made, src_in, last_ready = (s.sem(n) for n in ("starts_in", "zero_made", "src_in", "last_ready"))
        block = ctx.enter_context(nc.Block())

        @block.sync
        def _(sp):
            for i in range(3):
                sp.dma_start(raw[:, i, :], d["dst_rows"][i:i + TILES * P].rearrange("(p e) -> p e", p=ROWP)).then_inc(loaded, 16)
            sp.dma_start(m.src[:, :], d["src_cols"]).then_inc(src_in, 16)
            sp.wait_ge(base_ready, 1)
            sp.dma_start(d["starts"].rearrange("(p t) -> p t", p=ROWP), base_i[:, :]).then_inc(stored, 16)
            sp.wait_ge(stored, 16)
            sp.dma_start(starts_t[:, :], d["starts"].rearrange("(o t) -> o t", o=1)).then_inc(starts_in, 16)
            for kind, t in enumerate((keep16, reset16)):
                sp.wait_ge(rows_ready, kind + 1)
                sp.dma_start(d["flags"][kind, :].rearrange("(p e) -> p e", p=ROWP), t[:, :]).then_inc(stored, 16)
            sp.wait_ge(src_in, 16)
            sp.wait_ge(stored, 48)

        @block.scalar
        def _(act):
            act.wait_ge(zero_made, 1)
            act.dma_start(d["sums"][ROWS:ROWS + NPAD, :].rearrange("(p b) w -> p (b w)", b=NB), zeros[:, 0:NB * D]).then_inc(zeroed, 16)
            for table, first, w in ((d["rank8"], TRASH, 8), (d["sums_heads"], ROWS, HEADS * D)):
                act.dma_start(table[first:first + NPAD, :].rearrange("(p b) w -> p (b w)", b=NB),
                              zeros[:, 0:NB * w]).then_inc(zeroed, 16)
            act.wait_ge(made, 3)
            act.dma_start(d["rank_of"][0:NPAD, :].rearrange("(p b) o -> p (b o)", b=NB), init[:, :]).then_inc(zeroed, 16)
            act.wait_ge(zeroed, 64)

        @block.gpsimd
        def _(pool):
            nc.gpsimd.iota(m.iota[:, :], pattern=[[1, P]], base=0, channel_multiplier=0,
                           allow_small_or_imprecise_dtypes=True).then_inc(made, 1)
            nc.gpsimd.iota(m.lane[:, :], pattern=[[0, 1]], base=0, channel_multiplier=1,
                           allow_small_or_imprecise_dtypes=True).then_inc(made, 1)
            nc.gpsimd.iota(init[:, :], pattern=[[1, NB]], base=TRASH, channel_multiplier=NB).then_inc(made, 1)

        @block.vector
        def _(dve):
            link = linker(dve, chain)
            nc.vector.memset(zeros[:, :], 0.0).then_inc(zero_made, 1)
            link(nc.vector.memset(ones[:, :], 1.0))
            dve.wait_ge(made, 2)
            link(nc.vector.tensor_scalar(m.ident[:, :], m.iota[:, :], m.lane[:, :], None, ALU.is_equal))
            link(nc.vector.tensor_scalar(before[:, :], m.iota[0:ROWP, 0:ROWP], m.lane[0:ROWP, :], None, ALU.is_gt))
            dve.wait_ge(loaded, 48)
            for i, t in enumerate((prev, cur, nxt)):
                link(nc.vector.tensor_copy(t[:, :], raw[:, i, :]))
            link(nc.vector.tensor_tensor(prev[:, :], prev[:, :], cur[:, :], ALU.not_equal))
            link(nc.vector.tensor_tensor(nxt[:, :], nxt[:, :], cur[:, :], ALU.not_equal))
            nc.vector.tensor_tensor_scan(rank[:, :], ones[:, :], prev[:, :], 0.0, ALU.mult, ALU.add).then_inc(counted, 1)
            dve.wait_ge(offset_ready, 1)
            link(nc.vector.tensor_scalar(offset[:, :], ps_off[:, 0:1], 1.0, None, ALU.subtract))
            link(nc.vector.tensor_scalar(rank[:, :], rank[:, :], offset[:, :], None, ALU.add))
            rank_t = rank[:, :].rearrange("p (t e) -> p t e", e=P)
            link(nc.vector.tensor_copy(base[:, :], rank_t[:, :, 0]))
            nc.vector.tensor_copy(base_i[:, :], base[:, :]).then_inc(base_ready, 1)
            link(nc.vector.tensor_tensor(rank_t, rank_t, base[:, :].unsqueeze(2).broadcast_to([ROWP, ROWT, P]), ALU.subtract))
            link(nc.vector.scalar_tensor_tensor(cur[:, :], rank[:, :], 1.0, nxt[:, :], ALU.add, ALU.mult))
            nc.vector.tensor_scalar(cur[:, :], cur[:, :], 1.0, None, ALU.subtract).then_inc(last_ready, 1)
            nc.vector.tensor_scalar(keep16[:, :], prev[:, :], 0.0, None, ALU.is_equal).then_inc(rows_ready, 1)
            nc.vector.tensor_scalar(reset16[:, :], prev[:, :], -BIG, None, ALU.mult).then_inc(rows_ready, 1)
            for n in range(2 * ROWT):
                dve.wait_ge(transposed, n + 1)
                out = (rk.local, rk.last)[n // ROWT]
                j = n % ROWT
                view = out[:, :].rearrange("p (k a s i) -> p k a s i", a=ROWT // PER, s=STREAMS, i=PER)[:, :, j // PER, :, j % PER]
                nc.vector.tensor_copy(view, ps_t[:, n % 4, 0:ROWP].rearrange("p (s k) -> p k s", s=STREAMS)).then_inc(taken, 1)
            dve.wait_ge(starts_in, 16)
            for st in range(STREAMS):
                nc.vector.tensor_copy(rk.starts[:, :].rearrange("o (c s i) -> o c s i", s=STREAMS, i=PER)[:, :, st, :],
                                      starts_t[:, st * HALF:(st + 1) * HALF].rearrange("o (c i) -> o c i", i=PER))

        @block.tensor
        def _(pe):
            pe.wait_ge(counted, 1)
            pe.wait_ge(chain, 3)
            nc.tensor.matmul(ps_off[:, 0:1], before[:, :], rank[:, ROWE - 1:ROWE], start=True, stop=True).then_inc(offset_ready, 1)
            pe.wait_ge(last_ready, 1)
            for n in range(2 * ROWT):
                if n >= 4:
                    pe.wait_ge(taken, n - 3)
                j = n % ROWT
                nc.tensor.transpose(ps_t[:, n % 4, 0:ROWP], (rank, cur)[n // ROWT][:, j * P:(j + 1) * P],
                                    m.ident[0:ROWP, 0:ROWP]).then_inc(transposed, 1)


def load_features(nc, sp, m, d, sem):
    sp.dma_start(m.x[0:LASTP, :, :], d["x"][0:LASTP * NB, :].rearrange("(p b) w -> p b w", b=NB)).then_inc(sem, 16)
    sp.dma_start(m.x[LASTP:LASTP + 1, 0:LASTB, :], d["x"][LASTP * NB:N, :].rearrange("(p b) w -> p b w", b=LASTB)).then_inc(sem, 16)


def phase_table(nc, m, rk, d, edge):
    with ExitStack() as ctx:
        s = Scope(nc, ctx, "tb")
        t = Norm(s)
        lin_w = s.sb("lin_w", [D, HEADS * D])
        att = s.sb("att", [D, 2, HEADS * D])
        prod = s.sb("prod", [D, HEADS * D])
        folded = s.sb("folded", [D, 2 * HEADS])
        edge_w = s.sb("edge_w", [P, EDIM, HEADS * D])
        att_e = s.sb("att_e", [P, HEADS * D])
        v = s.sb("v", [P, EDIM * HEADS])
        attr = s.sb("attr", [P, TILES * EDIM])
        h_t = s.sb("h_t", [D, 2, P])
        table = s.sb("table", [P, NB, TW])
        ps_t = s.ps("ps_t", [D, 2, 512])
        ps_a = s.ps("ps_a", [P, 512])
        loaded, weights_in, attr_in, chain = (s.sem(n) for n in ("loaded", "weights_in", "attr_in", "chain"))
        var, std, h_ready, folded_ready = (s.sem(n) for n in ("var", "std", "h_ready", "folded_ready"))
        transposed, taken, logits_ready, table_ready, stored = (s.sem(n) for n in ("transposed", "taken", "logits_ready", "table_ready", "stored"))
        cleared = s.sem("cleared")
        block = ctx.enter_context(nc.Block())

        @block.sync
        def _(sp):
            sp.wait_ge(cleared, 1)
            load_features(nc, sp, m, d, loaded)
            sp.dma_start(lin_w[:, :], d["lin_w"]).then_inc(weights_in, 16)
            sp.dma_start(att[:, 0, :], d["att_src"].rearrange("h c -> (h c)").unsqueeze(0).broadcast_to([D, HEADS * D])).then_inc(weights_in, 16)
            sp.dma_start(att[:, 1, :], d["att_dst"].rearrange("h c -> (h c)").unsqueeze(0).broadcast_to([D, HEADS * D])).then_inc(weights_in, 16)
            sp.dma_start(edge_w[:, :, :].rearrange("p a b -> p (a b)"), d["lin_edge_w"].rearrange("h c -> (h c)").unsqueeze(0).broadcast_to([P, EDIM * HEADS * D])).then_inc(weights_in, 16)
            sp.dma_start(att_e[:, :], d["att_edge"].rearrange("h c -> (h c)").unsqueeze(0).broadcast_to([P, HEADS * D])).then_inc(weights_in, 16)
            sp.dma_start(attr[:, :], d["attr_cols"]).then_inc(attr_in, 16)
            sp.dma_start(rk.dst[:, :], d["dst_cols"]).then_inc(attr_in, 16)
            sp.wait_ge(table_ready, 1)
            sp.dma_start(d["table0"].rearrange("(p b) w -> p b w", b=NB), table[:, :, :]).then_inc(stored, 16)
            sp.wait_ge(stored, 16)

        @block.scalar
        def _(act):
            root(nc, act, t, var, std, 1)
            for b in range(NB):
                act.wait_ge(transposed, b + 1)
                if b >= 2:
                    act.wait_ge(logits_ready, b - 1)
                nc.scalar.copy(h_t[:, b % 2, :], ps_t[:, b % 2, 0:P]).then_inc(taken, 1)

        @block.tensor
        def _(pe):
            pe.wait_ge(h_ready, 1)
            pe.wait_ge(folded_ready, 1)
            for b in range(NB + 1):
                if b < NB:
                    if b >= 2:
                        pe.wait_ge(taken, b - 1)
                    nc.tensor.transpose(ps_t[:, b % 2, 0:P], m.h[:, b, :], m.ident[:, :]).then_inc(transposed, 1)
                if b >= 1:
                    pe.wait_ge(taken, b)
                    nc.tensor.matmul(ps_a[:, (b - 1) * WW:b * WW], h_t[:, (b - 1) % 2, :], folded[:, :],
                                     start=True, stop=True).then_inc(logits_ready, 1)

        @block.vector
        def _(dve):
            link = linker(dve, chain)
            nc.vector.memset(m.x[:, :, :], 0.0).then_inc(cleared, 1)
            dve.wait_ge(weights_in, 80)
            for a in range(2):
                link(nc.vector.tensor_tensor(prod[:, :], lin_w[:, :], att[:, a, :], ALU.mult))
                ins = nc.vector.tensor_reduce(out=folded[:, a * HEADS:(a + 1) * HEADS], in_=prod[:, :].rearrange("p (h c) -> p h c", h=HEADS), axis=AX.X, op=ALU.add)
                if a == 0:
                    link(ins)
                else:
                    ins.then_inc(folded_ready, 1)
            link(nc.vector.tensor_tensor(edge_w[:, :, :], edge_w[:, :, :], att_e[:, :].unsqueeze(1).broadcast_to([P, EDIM, HEADS * D]), ALU.mult))
            link(nc.vector.tensor_reduce(out=v[:, :], in_=edge_w[:, :, :].rearrange("p a (h c) -> p (a h) c", h=HEADS), axis=AX.X, op=ALU.add))
            dve.wait_ge(loaded, 32)
            layer_norm(nc, link, dve, m.h[:, :, :], m.x[:, :, :], t, var, std, 1)
            link(nc.vector.tensor_scalar(m.h[:, :, :], m.h[:, :, :], 0.0, None, ALU.max))
            nc.vector.tensor_copy(table[:, :, 0:D], m.h[:, :, :]).then_inc(h_ready, 1)
            dve.wait_ge(attr_in, 32)
            at = attr[:, :].rearrange("p (t c) -> p t c", c=EDIM)
            for hd in range(HEADS):
                link(nc.vector.tensor_scalar(edge.logit[:, :, hd], at[:, :, 0], v[:, hd:hd + 1], None, ALU.mult))
                for c in range(1, EDIM):
                    link(nc.vector.scalar_tensor_tensor(edge.logit[:, :, hd], at[:, :, c], v[:, c * HEADS + hd:c * HEADS + hd + 1],
                                                        edge.logit[:, :, hd], ALU.mult, ALU.add))
            link(nc.vector.memset(edge.logit[:, :, HEADS], 1.0))
            dve.wait_ge(logits_ready, NB)
            link(nc.vector.tensor_copy(m.logit[:, :, :], ps_a[:, 0:NB * WW].rearrange("p (b w) -> p b w", w=WW)))
            nc.vector.memset(table[:, :, D + HEADS:TW], 1.0)
            nc.vector.tensor_copy(table[:, :, D:D + HEADS], m.logit[:, :, 0:HEADS]).then_inc(table_ready, 1)


def add_windows(nc, dve, acc, ps_o, starts, product, added, c, per_bank, layer=0):
    banks = U // per_bank
    regs = window_starts(nc, mybir.EngineType.DVE, starts, c)
    for u in range(U):
        if u % per_bank == 0:
            dve.wait_ge(product, layer * ((CHUNKS + BUFS) * banks) + c * banks + (BUFS * banks + u // per_bank + 1))
        dve.wait_ge(added, layer * (TILES + U) + c * U + (U + u))
        where = acc[..., bass.ds(regs[u], P)] if len(acc.shape) == 2 else acc[:, :, bass.ds(regs[u], P)]
        nc.vector.tensor_tensor(where, where, ps_o(u), ALU.add).then_inc(added, 1)


def phase_gat_max(nc, m, rk, d, edge, acc):
    with ExitStack() as ctx:
        s = Scope(nc, ctx, "gm")
        rows = s.sb("rows", [P, BUFS, U * TW])
        index = s.sb("index", [P, BUFS, U], I32)
        hot = s.sb("hot", [P, BUFS, U, P])
        hot_last = s.sb("hot_last", [P, BUFS, U, P])
        part = s.sb("part", [P, BUFS, U, AW])
        cand = s.sb("cand", [P, 2, PER, STREAMS * AW])
        reset = s.sb("reset", [STREAMS * AW, BUFS, PER * P], BF16)
        zeros = s.sb("zeros", [P, U * D])
        border16 = s.sb("border16", [AW, 1], BF16)
        run = s.sb("run", [STREAMS * AW, 2, PER * P])
        back = s.sb("back", [P, 2, PER, STREAMS * AW])
        border = s.sb("border", [AW, 1])
        ps_c = s.ps("ps_c", [STREAMS * AW, 2, PER * P])
        ps_b = s.ps("ps_b", [P, 512])
        ps_o = s.ps("ps_o", [AW, U, 2, P])
        index_ready = s.sem("index_ready")
        rows_in = [s.sem(f"rows_in{b}") for b in range(BUFS)]
        saved = [s.sem(f"saved{b}") for b in range(BUFS)]
        reset_in = [s.sem(f"reset_in{b}") for b in range(BUFS)]
        hot_ready, cand_ready, cand_t, run_ready = (s.sem(n) for n in ("hot_ready", "cand_ready", "cand_t", "run_ready"))
        back_t, back_ready, product, added = (s.sem(n) for n in ("back_t", "back_ready", "product", "added"))
        part_ready, border_in, chain, zeroed, cleared = (s.sem(n) for n in ("part_ready", "border_in", "chain", "zeroed", "cleared"))
        BANKS = U // PAIR
        block = ctx.enter_context(nc.Block())

        @block.gpsimd
        def _(pool):
            gather_pass(pool, rows, index, d["table0"], TW, index_ready, rows_in)

        @block.sync
        def _(sp):
            sp.dma_start(border16[:, :], d["flags"][1, HALF * P:HALF * P + 1].unsqueeze(0).broadcast_to([AW, 1])).then_inc(border_in, 16)
            sp.wait_ge(zeroed, 1)

            def step(k, j):
                if now := stage(k, j, 0):
                    c, _, b = now
                    sp.wait_ge(run_ready, c + 1)
                    sp.nop(nofuse=True)
                    for st in range(STREAMS):
                        sp.dma_start(reset[st * AW:(st + 1) * AW, b, :], flags_row(d["flags"], 1, c, st, AW)).then_inc(reset_in[b], 16)
                    sp.dma_start(d["filled"][bass.ds(c * (P * U), P * U), :].rearrange("(p u) w -> p (u w)", u=U), zeros[:, :]).then_inc(cleared, 16)
                    sp.dma_start(d["filled8"][bass.ds(c * (P * U), P * U), :].rearrange("(p u) w -> p (u w)", u=U), zeros[:, 0:U * 2 * AW]).then_inc(cleared, 16)
                if now := stage(k, j, 1):
                    c, r, b = now
                    sp.wait_ge(rows_in[b], (r + 1) * (16 * U))
                    sp.nop(nofuse=True)
                    sp.dma_start(d["saved"][bass.ds(c * P, P), :], rows[:, b, :]).then_inc(saved[b], 16)
            loop_steps(sp, step, 1)
            for b in range(BUFS):
                sp.wait_ge(saved[b], 16 * (LOOPS + 1))
            sp.wait_ge(border_in, 16)
            sp.wait_ge(cleared, 32 * CHUNKS)

        @block.scalar
        def _(act):
            for b in range(BUFS):
                act.sem_inc(saved[b], 16)
            act.sem_inc(back_ready, 1)

            def step(k, j):
                if now := stage(k, j, 0):
                    c, r, b = now
                    act.wait_ge(cand_ready, c * 2 + 2)
                    act.wait_ge(saved[b], (r + 1) * 16)
                    nc.scalar.copy(index[:, b, :], m.src[:, bass.ds(c * U, U)]).then_inc(index_ready, 1)
                    act.wait_ge(product, c * BANKS + BANKS)
                    nc.scalar.copy(part[:, b, :, :], edge.logit[:, bass.ds(c * U, U), :]).then_inc(part_ready, 1)
                if now := stage(k, j, 2):
                    c, r, b = now
                    act.wait_ge(back_t, c + 3)
                    act.wait_ge(product, c * BANKS + 3 * BANKS)
                    nc.scalar.copy(back[:, b % 2, :, :], ps_b[:, 0:U * AW].rearrange("p (i a) -> p i a", i=PER)).then_inc(back_ready, 1)
            loop_steps(act, step, 2)

        @block.tensor
        def _(pe):
            pe.sem_inc(product, BUFS * BANKS)
            pe.sem_inc(cand_t, 2)
            pe.sem_inc(back_t, 2)

            def step(k, j):
                if now := stage(k, j, 1):
                    c, r, b = now
                    pe.wait_ge(cand_ready, c * 2 + 2 * BUFS + 2)
                    pe.wait_ge(run_ready, c + BUFS - 1)
                    for i in range(PER):
                        last = nc.tensor.transpose(ps_c[:, b % 2, i * P:(i + 1) * P], cand[:, b % 2, i, :], m.ident[:, :])
                    last.then_inc(cand_t, 1)
                if now := stage(k, j, 2):
                    c, r, b = now
                    pe.wait_ge(run_ready, c + BUFS + 1)
                    pe.wait_ge(back_ready, c + 1)
                    pe.nop(nofuse=True)
                    w = STREAMS * AW
                    for i in range(PER):
                        last = nc.tensor.transpose(ps_b[:, i * w:(i + 1) * w], run[:, b % 2, i * P:(i + 1) * P], m.ident[0:w, 0:w])
                    last.then_inc(back_t, 1)
                    pe.wait_ge(part_ready, c + 1)
                    pe.wait_ge(hot_ready, c * 2 + 2)
                    pe.wait_ge(back_ready, c + 2)
                    for u in range(U):
                        st, i = divmod(u, PER)
                        if u % PAIR == 0:
                            pe.wait_ge(added, c * U + (u + PAIR))
                        nc.tensor.matmul(ps_o[:, u, 0, :], part[:, b, u, :], hot[:, b, u, :], start=True, stop=True)
                        last = nc.tensor.matmul(ps_o[:, u, 1, :], back[:, b % 2, i, st * AW:(st + 1) * AW], hot_last[:, b, u, :],
                                         start=True, stop=True)
                        if u % PAIR == PAIR - 1:
                            last.then_inc(product, 1)
            loop_steps(pe, step, 2)

        @block.vector
        def _(dve):
            link = linker(dve, chain)
            nc.vector.memset(zeros[:, :], 0.0).then_inc(zeroed, 1)
            nc.vector.memset(acc[0:AW, :, :], 0.0).then_inc(added, U)
            nc.vector.memset(run[:, :, :], -BIG).then_inc(run_ready, BUFS)
            dve.sem_inc(cand_ready, 2 * BUFS)

            def step(k, j):
                if now := stage(k, j, 0):
                    c, r, b = now
                    dve.wait_ge(product, c * BANKS + BANKS)
                    one_hot(nc, hot[:, b], m.iota[:, :], rk.local[:, bass.ds(c * U, U)]).then_inc(hot_ready, 1)
                    one_hot(nc, hot_last[:, b], m.iota[:, :], rk.last[:, bass.ds(c * U, U)]).then_inc(hot_ready, 1)
                if now := stage(k, j, 1):
                    c, r, b = now
                    dve.wait_ge(cand_t, c + 3)
                    dve.wait_ge(reset_in[b], (r + 1) * (16 * STREAMS))
                    dve.wait_ge(back_t, c + 1)
                    dve.wait_ge(run_ready, c + BUFS)
                    nc.vector.tensor_tensor_scan(run[:, b % 2, :], reset[:, b, :], ps_c[:, b % 2, :],
                                                 run[:, (b + 1) % 2, PER * P - 1:PER * P], ALU.add, ALU.max).then_inc(run_ready, 1)
                if now := stage(k, j, 2):
                    add_windows(nc, dve, acc[0:AW, :, :], lambda u: ps_o[:, u, :, :], rk.starts, product, added, now[0], PAIR)
                if now := stage(k, j, 0):
                    c, r, b = now
                    dve.wait_ge(rows_in[b], (r + 1) * (16 * U))
                    dve.wait_ge(cand_t, c + 1)
                    tile4 = lambda ap: ap.rearrange("p (s i) a -> p s i a", s=STREAMS)
                    to = cand[:, b % 2, :, :].rearrange("p i (s a) -> p s i a", s=STREAMS)
                    nc.vector.tensor_tensor(to[:, :, :, 0:HEADS],
                                            tile4(rows[:, b, :].rearrange("p (u w) -> p u w", w=TW)[:, :, D:D + HEADS]),
                                            tile4(edge.logit[:, bass.ds(c * U, U), 0:HEADS]), ALU.add).then_inc(cand_ready, 1)
                    dve.wait_ge(part_ready, c + 1)
                    own = edge.logit[:, bass.ds(c * U, U), 0:HEADS]
                    nc.vector.tensor_tensor(own, rows[:, b, :].rearrange("p (u w) -> p u w", w=TW)[:, :, D:D + HEADS], own, ALU.add)
                    nc.vector.tensor_copy(to[:, :, :, HEADS],
                                          rk.dst[:, bass.ds(c * U, U)].rearrange("p (s i) -> p s i", s=STREAMS)).then_inc(cand_ready, 1)
            loop_steps(dve, step, 2)
            dve.wait_ge(border_in, 16)
            dve.wait_ge(run_ready, CHUNKS + BUFS)
            link(nc.vector.tensor_tensor(border[:, :], border16[:, :], run[0:AW, (CHUNKS - 1) % 2, PER * P - 1:PER * P], ALU.add))
            dve.wait_ge(added, TILES + U)
            first = nc.vector.value_load(rk.starts[0:1, PER:PER + 1], min_val=0, max_val=RANKS - P)
            link(nc.vector.tensor_tensor(acc[0:AW, 1, bass.ds(first, 1)], acc[0:AW, 1, bass.ds(first, 1)], border[:, :], ALU.max))


def phase_gat_nodes(nc, m, d, acc):
    with ExitStack() as ctx:
        s = Scope(nc, ctx, "gn")
        table = s.sb("table", [P, RB, 2 * AW])
        slot_f = s.sb("slot_f", [P, RB])
        slot = s.sb("slot", [P, RB], I32)
        number = s.sb("number", [P, RB], I32)
        number_f = s.sb("number_f", [P, RB])
        node = s.sb("node", [P, NB, 2 * AW])
        rank_of = s.sb("rank_of", [P, NB], I32)
        values = s.sb("values", [P, NB, 2 * AW])
        mean = s.sb("mean", [P, NB, HEADS])
        own = s.sb("own", [P, NB, HEADS])
        tmp = s.sb("tmp", [P, NB, HEADS])
        empty = s.sb("empty", [P, NB])
        ps = s.ps("ps", [P, 512])
        before = s.sb("before", [P, P])
        upto_n, pos = s.sb("upto_n", [P, NB]), s.sb("pos", [P, NB])
        none = s.sb("none", [P, NB])
        whole, tile, lane_of, part = (s.sb(n, [P, NB], I32) for n in ("whole", "tile", "lane_of", "part"))
        offset = s.sb("offset", [P, 1])
        cross_i, cross, shared16, shared = s.sb("cross_i", [P, 1], I32), s.sb("cross", [P, 1]), s.sb("shared16", [P, 1], BF16), s.sb("shared", [P, 1])
        ps_before = s.ps("ps_before", [P, 512])
        cross_in, counted, before_ready, starts_ready, starts_out, first_in = (s.sem(n) for n in ("cross_in", "counted", "before_ready", "starts_ready", "starts_out", "first_in"))
        node_out = s.sem("node_out")
        rows_t, table_ready, stored, numbered, slot_ready = (s.sem(n) for n in ("rows_t", "table_ready", "stored", "numbered", "slot_ready"))
        scattered, rank_in, gathered, values_ready, values_out = (s.sem(n) for n in ("scattered", "rank_in", "gathered", "values_ready", "values_out"))
        chain, arg_ready, exp_ready = s.sem("chain"), s.sem("arg_ready"), s.sem("exp_ready")
        block = ctx.enter_context(nc.Block())

        @block.tensor
        def _(pe):
            for r in range(RB):
                for a in range(2):
                    last = nc.tensor.transpose(ps[:, (2 * r + a) * AW:(2 * r + a + 1) * AW], acc[0:AW, a, r * P:(r + 1) * P], m.ident[0:AW, 0:AW])
            last.then_inc(rows_t, 1)
            pe.wait_ge(counted, 1)
            nc.tensor.matmul(ps_before[:, 0:1], before[:, :], upto_n[:, NB - 1:NB], start=True, stop=True).then_inc(before_ready, 1)

        @block.sync
        def _(sp):
            sp.dma_start(cross_i[:, :], d["dst_rows"][1 + HALF * P:2 + HALF * P].unsqueeze(0).broadcast_to([P, 1])).then_inc(cross_in, 16)
            sp.dma_start(shared16[:, :], d["flags"][0, HALF * P:HALF * P + 1].unsqueeze(0).broadcast_to([P, 1])).then_inc(cross_in, 16)
            sp.wait_ge(table_ready, 1)
            sp.dma_start(d["rank8"][0:RANKS, :].rearrange("(r p) w -> p r w", p=P), table[:, :, :]).then_inc(stored, 16)
            sp.wait_ge(scattered, 16 * RB)
            sp.dma_start(rank_of[:, :], d["rank_of"][0:NPAD, :].rearrange("(p b) o -> p (b o)", b=NB)).then_inc(rank_in, 16)
            sp.wait_ge(rank_in, 16)
            sp.wait_ge(values_ready, 1)
            sp.dma_start(d["node8"].rearrange("(p b) w -> p b w", b=NB), values[:, :, :]).then_inc(node_out, 16)
            sp.wait_ge(node_out, 16)
            sp.wait_ge(starts_ready, 1)
            sp.dma_start(d["start_of"].rearrange("(p b) o -> p (b o)", b=NB), m.start_row[:, :]).then_inc(starts_out, 16)
            sp.wait_ge(starts_out, 16)
            sp.wait_ge(cross_in, 32)
            sp.nop(nofuse=True)
            node_at = nc.sync.value_load(cross_i[0:1, 0:1], min_val=0, max_val=NPAD - 1)
            sp.dma_start(m.first[:, :], d["start_of"][bass.ds(node_at, 1), :]).then_inc(first_in, 16)
            sp.wait_ge(first_in, 16)

        @block.gpsimd
        def _(pool):
            nc.gpsimd.iota(m.node_no[:, :], pattern=[[1, NB]], base=0, channel_multiplier=NB, allow_small_or_imprecise_dtypes=True)
            nc.gpsimd.iota(number[:, :], pattern=[[P, RB]], base=0, channel_multiplier=1).then_inc(numbered, 1)
            pool.wait_ge(numbered, 1)
            pool.wait_ge(slot_ready, 1)
            for r in range(RB):
                pool.indirect_dma_start(d["rank_of"], bass.IndirectOffsetOnAxis(slot[:, r:r + 1], 0), number[:, r:r + 1], None).then_inc(scattered, 16)
            pool.wait_ge(rank_in, 16)
            pool.wait_ge(stored, 16)
            for b in range(NB):
                pool.indirect_dma_start(node[:, b, :], None, d["rank8"], bass.IndirectOffsetOnAxis(rank_of[:, b:b + 1], 0)).then_inc(gathered, 16)
            pool.wait_ge(values_ready, 1)
            pool.wait_ge(starts_ready, 1)
            for b in range(NB):
                pool.indirect_dma_start(d["filled8"], bass.IndirectOffsetOnAxis(m.start_pos[:, b:b + 1], 0), values[:, b, :], None).then_inc(values_out, 16)
            pool.wait_ge(values_out, 16 * NB)

        @block.scalar
        def _(act):
            act.wait_ge(arg_ready, 1)
            nc.scalar.activation(m.self_w[:, :, :], tmp[:, :, :], ACT.Exp).then_inc(exp_ready, 1)

        def edge_rows(nc, link, dve):
            count = node[:, :, HEADS]
            link(nc.vector.tensor_scalar(before[:, :], m.iota[:, :], m.lane[:, :], None, ALU.is_gt))
            link(nc.vector.memset(none[:, :], 1.0))
            nc.vector.tensor_tensor_scan(upto_n[:, :], none[:, :], count, 0.0, ALU.mult, ALU.add).then_inc(counted, 1)
            dve.wait_ge(before_ready, 1)
            link(nc.vector.tensor_copy(offset[:, :], ps_before[:, 0:1]))
            link(nc.vector.tensor_scalar(upto_n[:, :], upto_n[:, :], offset[:, :], None, ALU.add))
            link(nc.vector.tensor_scalar(none[:, :], count, 0.0, None, ALU.is_equal))
            link(nc.vector.tensor_scalar(m.has[:, :], count, 0.0, None, ALU.is_gt))
            link(nc.vector.tensor_copy(whole[:, :], m.node_no[:, :]))
            dve.wait_ge(cross_in, 32)
            link(nc.vector.tensor_copy(cross[:, :], cross_i[:, :]))
            link(nc.vector.tensor_copy(shared[:, :], shared16[:, :]))
            link(nc.vector.tensor_scalar(m.join[:, :], m.node_no[:, :], cross[:, :], shared[:, :], ALU.is_equal, ALU.mult))
            for out, back in ((m.end_row, 1.0), (m.start_row, None)):
                if back:
                    link(nc.vector.tensor_scalar(pos[:, :], upto_n[:, :], back, 0.0, ALU.subtract, ALU.max))
                else:
                    link(nc.vector.tensor_tensor(pos[:, :], upto_n[:, :], count, ALU.subtract))
                link(nc.vector.tensor_copy(whole[:, :], pos[:, :]))
                if back:
                    link(nc.vector.tensor_copy(m.end_pos[:, :], whole[:, :]))
                else:
                    link(nc.vector.scalar_tensor_tensor(tile[:, :], m.node_no[:, :], float(ROWS), pos[:, :], ALU.add, ALU.subtract))
                    link(nc.vector.tensor_tensor(tile[:, :], tile[:, :], none[:, :], ALU.mult))
                    link(nc.vector.tensor_tensor(m.start_pos[:, :], tile[:, :], pos[:, :], ALU.add))
                link(nc.vector.tensor_single_scalar(tile[:, :], whole[:, :], 7, ALU.arith_shift_right))
                link(nc.vector.tensor_single_scalar(lane_of[:, :], whole[:, :], P - 1, ALU.bitwise_and))
                link(nc.vector.tensor_scalar(pos[:, :], tile[:, :], float(HALF), None, ALU.is_ge))
                link(nc.vector.scalar_tensor_tensor(tile[:, :], pos[:, :], -float(HALF), tile[:, :], ALU.mult, ALU.add))
                link(nc.vector.tensor_single_scalar(part[:, :], tile[:, :], PER - 1, ALU.bitwise_and))
                link(nc.vector.tensor_single_scalar(tile[:, :], tile[:, :], 2, ALU.arith_shift_right))
                link(nc.vector.scalar_tensor_tensor(pos[:, :], part[:, :], float(STREAMS), pos[:, :], ALU.mult, ALU.add))
                link(nc.vector.scalar_tensor_tensor(pos[:, :], lane_of[:, :], float(U), pos[:, :], ALU.mult, ALU.add))
                link(nc.vector.scalar_tensor_tensor(pos[:, :], tile[:, :], float(U * P), pos[:, :], ALU.mult, ALU.add))
                link(nc.vector.scalar_tensor_tensor(whole[:, :], m.node_no[:, :], float(ROWS), pos[:, :], ALU.add, ALU.subtract))
                link(nc.vector.tensor_tensor(whole[:, :], whole[:, :], none[:, :], ALU.mult))
                link(nc.vector.tensor_tensor(out[:, :], whole[:, :], pos[:, :], ALU.add))
            dve.sem_inc(starts_ready, 1)

        @block.vector
        def _(dve):
            link = linker(dve, chain)
            dve.wait_ge(rows_t, 1)
            link(nc.vector.tensor_copy(table[:, :, :], ps[:, 0:RB * 2 * AW].rearrange("p (r w) -> p r w", r=RB)))
            dve.wait_ge(numbered, 1)
            link(nc.vector.tensor_copy(number_f[:, :], number[:, :]))
            link(nc.vector.tensor_scalar(slot_f[:, :], number_f[:, :], float(TRASH), None, ALU.add))
            link(nc.vector.tensor_scalar(number_f[:, :], table[:, :, HEADS], 0.0, None, ALU.is_equal))
            link(nc.vector.tensor_tensor(slot_f[:, :], slot_f[:, :], number_f[:, :], ALU.mult))
            link(nc.vector.tensor_tensor(slot_f[:, :], slot_f[:, :], table[:, :, 2 * AW - 1], ALU.add))
            nc.vector.tensor_copy(slot[:, :], slot_f[:, :]).then_inc(slot_ready, 1)
            dve.sem_inc(table_ready, 1)
            link(nc.vector.memset(values[:, :, :], 0.0))
            dve.wait_ge(gathered, 16 * NB)
            link(nc.vector.tensor_scalar(empty[:, :], node[:, :, HEADS], 0.0, -BIG, ALU.is_equal, ALU.mult))
            link(nc.vector.tensor_scalar(m.inv_count[:, :], node[:, :, HEADS], 1.0, None, ALU.max))
            link(nc.vector.reciprocal(m.inv_count[:, :], m.inv_count[:, :]))
            link(nc.vector.tensor_tensor(mean[:, :, :], node[:, :, 0:HEADS], bcast(m.inv_count[:, :], HEADS), ALU.mult))
            link(nc.vector.tensor_tensor(own[:, :, :], m.logit[:, :, 0:HEADS], mean[:, :, :], ALU.add))
            link(nc.vector.tensor_tensor(tmp[:, :, :], node[:, :, AW:AW + HEADS], bcast(empty[:, :], HEADS), ALU.add))
            link(nc.vector.tensor_tensor(tmp[:, :, :], tmp[:, :, :], own[:, :, :], ALU.max))
            link(nc.vector.tensor_tensor(tmp[:, :, :], tmp[:, :, :], m.logit[:, :, HEADS:WW], ALU.add))
            link(nc.vector.tensor_tensor(own[:, :, :], own[:, :, :], m.logit[:, :, HEADS:WW], ALU.add))
            link(nc.vector.scalar_tensor_tensor(values[:, :, HEADS:WW], tmp[:, :, :], SLOPE, tmp[:, :, :], ALU.mult, ALU.max))
            link(nc.vector.scalar_tensor_tensor(mean[:, :, :], own[:, :, :], SLOPE, own[:, :, :], ALU.mult, ALU.max))
            link(nc.vector.tensor_copy(values[:, :, 0:HEADS], m.logit[:, :, HEADS:WW]))
            nc.vector.tensor_tensor(tmp[:, :, :], mean[:, :, :], values[:, :, HEADS:WW], ALU.subtract).then_inc(arg_ready, 1)
            dve.sem_inc(values_ready, 1)
            edge_rows(nc, link, dve)


def phase_gat_weights(nc, m, d, edge):
    with ExitStack() as ctx:
        s = Scope(nc, ctx, "gw")
        fill = s.sb("fill", [ROWP, ROWE, 2 * AW])
        keep = s.sb("keep", [ROWP, ROWE], BF16)
        first_dst = s.sb("first_dst", [ROWP, 2], I32)
        entry = s.sb("entry", [ROWP, 2 * AW])
        arg, top = s.sb("arg", [ROWP, ROWE]), s.sb("top", [ROWP, ROWE])
        weight = s.sb("weight", [ROWP, HEADS, ROWE])
        logit = s.sb("logit", [P, ROWT, ROWP])
        tail, whole = s.sb("tail", [ROWP, HEADS]), s.sb("whole", [ROWP, 1])
        tail_t, whole_t, carry_t = s.sb("tail_t", [HEADS, ROWP]), s.sb("whole_t", [HEADS, ROWP]), s.sb("carry_t", [HEADS, ROWP + 1])
        carry = s.sb("carry", [ROWP, HEADS])
        ps_z = s.ps("ps_z", [ROWP, ROWE])
        ps_w = s.ps("ps_w", [P, ROWT, P])
        loaded, first_in, entry_in, logit_ready, logit_t, arg_ready = (s.sem(n) for n in ("loaded", "first_in", "entry_in", "logit_ready", "logit_t", "arg_ready"))
        weight_ready, weight_t, weight_taken, tail_ready, tail_out = (s.sem(n) for n in ("weight_ready", "weight_t", "weight_taken", "tail_ready", "tail_out"))
        carry_ready, carry_out, sums_ready, stored, chain = (s.sem(n) for n in ("carry_ready", "carry_out", "sums_ready", "stored", "chain"))
        A = ROWT // PER
        by_row = lambda a, hd: edge.logit[:, :, hd].rearrange("p (k a s i) -> p a i s k", a=A, s=STREAMS, i=PER)[:, a]
        split = lambda t, a: t.rearrange("p (a i) (s k) -> p a i s k", a=A, s=STREAMS)[:, a]
        block = ctx.enter_context(nc.Block())

        @block.sync
        def _(sp):
            sp.dma_start(first_dst[:, :], d["dst_rows"][1:1 + TILES * P].rearrange("(p e) -> p e", p=ROWP)[:, 0:2]).then_inc(first_in, 16)
            sp.dma_start(keep[:, :], d["flags"][0, :].rearrange("(p e) -> p e", p=ROWP)).then_inc(loaded, 16)
            sp.dma_start(fill[:, :, :], d["filled8"][0:ROWS, :].rearrange("(p e) w -> p e w", p=ROWP)).then_inc(loaded, 16)
            sp.wait_ge(sums_ready, HEADS)
            sp.dma_start(d["filled8"][0:ROWS, :].rearrange("(p e) w -> p e w", p=ROWP), fill[:, :, :]).then_inc(stored, 16)
            sp.wait_ge(stored, 16)

        @block.gpsimd
        def _(pool):
            pool.wait_ge(first_in, 16)
            pool.indirect_dma_start(entry[:, :], None, d["node8"], bass.IndirectOffsetOnAxis(first_dst[:, 0:1], 0)).then_inc(entry_in, 16)

        @block.scalar
        def _(act):
            for hd in range(HEADS):
                if hd >= 1:
                    act.wait_ge(logit_t, hd)
                for a in range(A):
                    nc.scalar.copy(split(logit[:, :, :], a), by_row(a, hd)).then_inc(logit_ready, 1)
                act.wait_ge(arg_ready, hd + 1)
                nc.scalar.activation(weight[:, hd, :], arg[:, :], ACT.Exp).then_inc(weight_ready, 1)
                act.wait_ge(weight_t, hd + 1)
                for a in range(A):
                    nc.scalar.copy(by_row(a, hd), split(ps_w[:, :, 0:ROWP], a)).then_inc(weight_taken, 1)

        @block.tensor
        def _(pe):
            for hd in range(HEADS):
                pe.wait_ge(logit_ready, (hd + 1) * A)
                if hd >= 1:
                    pe.wait_ge(arg_ready, hd)
                for t in range(ROWT):
                    last = nc.tensor.transpose(ps_z[:, t * P:(t + 1) * P], logit[:, t, :], m.ident[:, :])
                last.then_inc(logit_t, 1)
                pe.wait_ge(weight_ready, hd + 1)
                if hd >= 1:
                    pe.wait_ge(weight_taken, hd * A)
                for t in range(ROWT):
                    last = nc.tensor.transpose(ps_w[:, t, 0:ROWP], weight[:, hd, t * P:(t + 1) * P], m.ident[0:ROWP, 0:ROWP])
                last.then_inc(weight_t, 1)
            pe.wait_ge(tail_ready, 2)
            pe.wait_ge(arg_ready, HEADS)
            nc.tensor.matmul(ps_z[0:HEADS, 0:ROWP], tail[:, :], m.ident[0:ROWP, 0:ROWP], start=True, stop=True)
            nc.tensor.matmul(ps_z[0:HEADS, P:P + ROWP], whole[:, 0:1].broadcast_to([ROWP, HEADS]), m.ident[0:ROWP, 0:ROWP], start=True, stop=True).then_inc(tail_out, 1)
            pe.wait_ge(carry_ready, 1)
            nc.tensor.matmul(ps_z[:, 512:512 + HEADS], carry_t[:, 0:ROWP], m.ident[0:HEADS, 0:HEADS], start=True, stop=True).then_inc(carry_out, 1)

        @block.vector
        def _(dve):
            link = linker(dve, chain)
            link(nc.vector.memset(carry_t[:, 0:1], 0.0))
            dve.wait_ge(loaded, 32)
            dve.wait_ge(entry_in, 16)
            nc.vector.tensor_reduce(out=whole[:, :], in_=keep[:, :], axis=AX.X, op=ALU.min).then_inc(tail_ready, 1)
            for hd in range(HEADS):
                if hd >= 1:
                    dve.wait_ge(weight_ready, hd)
                link(nc.vector.tensor_tensor_scan(arg[:, :], keep[:, :], fill[:, :, hd], entry[:, hd:hd + 1], ALU.mult, ALU.add))
                link(nc.vector.tensor_tensor_scan(top[:, :], keep[:, :], fill[:, :, HEADS + hd], entry[:, HEADS + hd:HEADS + hd + 1], ALU.mult, ALU.add))
                dve.wait_ge(logit_t, hd + 1)
                link(nc.vector.tensor_tensor(arg[:, :], arg[:, :], ps_z[:, :], ALU.add))
                link(nc.vector.scalar_tensor_tensor(arg[:, :], arg[:, :], SLOPE, arg[:, :], ALU.mult, ALU.max))
                nc.vector.tensor_tensor(arg[:, :], arg[:, :], top[:, :], ALU.subtract).then_inc(arg_ready, 1)
                dve.wait_ge(arg_ready, hd + 1)
            for hd in range(HEADS):
                dve.wait_ge(weight_ready, hd + 1)
                link(nc.vector.tensor_tensor_scan(top[:, :], keep[:, :], weight[:, hd, :], 0.0, ALU.mult, ALU.add))
                link(nc.vector.tensor_copy(tail[:, hd:hd + 1], top[:, ROWE - 1:ROWE]))
            dve.sem_inc(tail_ready, 1)
            dve.wait_ge(tail_out, 1)
            link(nc.vector.tensor_copy(tail_t[:, :], ps_z[0:HEADS, 0:ROWP]))
            link(nc.vector.tensor_copy(whole_t[:, :], ps_z[0:HEADS, P:P + ROWP]))
            nc.vector.tensor_tensor_scan(carry_t[:, 1:ROWP + 1], whole_t[:, :], tail_t[:, :], 0.0, ALU.mult, ALU.add).then_inc(carry_ready, 1)
            dve.wait_ge(carry_out, 1)
            link(nc.vector.tensor_copy(carry[:, :], ps_z[:, 512:512 + HEADS]))
            for hd in range(HEADS):
                nc.vector.tensor_tensor_scan(fill[:, :, hd], keep[:, :], weight[:, hd, :], carry[:, hd:hd + 1], ALU.mult, ALU.add).then_inc(sums_ready, 1)


def phase_gat_sum(nc, m, d, edge):
    with ExitStack() as ctx:
        s = Scope(nc, ctx, "gs")
        rows = s.sb("rows", [P, BUFS, U * TW])
        keep = s.sb("keep", [P, BUFS, PER * P], BF16)
        scaled = s.sb("scaled", [P, 2, HEADS, U * D])
        run = s.sb("run", [P, 2, HEADS, PER * P])
        back = s.sb("back", [P, BUFS, U, HEADS, D])
        ps_r = s.ps("ps_r", [P, HEADS, PER * P])
        ps_b = s.ps("ps_b", [P, HEADS, PER * P])
        heads = range(HEADS)
        scaled_ready, rows_t, run_ready, back_t, back_ready = ([s.sem(f"{n}{hd}") for hd in heads] for n in ("scaled_ready", "rows_t", "run_ready", "back_t", "back_ready"))
        rows_in, keep_in, stored = ([s.sem(f"{n}{b}") for b in range(BUFS)] for n in ("rows_in", "keep_in", "stored"))
        block = ctx.enter_context(nc.Block())

        @block.sync
        def _(sp):
            def step(k, j):
                if now := stage(k, j, 0):
                    c, r, b = now
                    sp.wait_ge(scaled_ready[HEADS - 1], upto(c, BUFS))
                    sp.nop(nofuse=True)
                    sp.dma_start(rows[:, b, :], d["saved"][bass.ds(c * P, P), :]).then_inc(rows_in[b], 16)
                    sp.wait_ge(run_ready[HEADS - 1], upto(c, BUFS))
                    sp.nop(nofuse=True)
                    load_flags(sp, keep, d, 0, c, b, keep_in)
                if now := stage(k, j, 3):
                    c, r, b = now
                    sp.wait_ge(back_ready[HEADS - 1], upto(c))
                    sp.nop(nofuse=True)
                    sp.dma_start(d["sums_heads"][bass.ds(c * (P * U), P * U), :].rearrange("(p u) w -> p (u w)", u=U),
                                 back[:, b].rearrange("p u h w -> p (u h w)")).then_inc(stored[b], 16)
            loop_steps(sp, step, 3)
            for b in range(BUFS):
                sp.wait_ge(stored[b], 16 * (LOOPS + 1))

        @block.scalar
        def _(act):
            for b in range(BUFS):
                act.sem_inc(stored[b], 16)
            for hd in heads:
                act.sem_inc(back_ready[hd], BUFS)

            def step(k, j):
                if now := stage(k, j, 2):
                    c, r, b = now
                    act.wait_ge(stored[b], (r + 1) * 16)
                    for hd in heads:
                        act.wait_ge(back_t[hd], upto(c))
                        nc.scalar.copy(back[:, b, :, hd, :], ps_b[:, hd, :].rearrange("p (u w) -> p u w", w=D)).then_inc(back_ready[hd], 1)
            loop_steps(act, step, 2)

        @block.tensor
        def _(pe):
            for hd in heads:
                pe.sem_inc(rows_t[hd], BUFS)
                pe.sem_inc(back_t[hd], BUFS)

            def step(k, j):
                if now := stage(k, j, 0):
                    c, r, b = now
                    for hd in heads:
                        pe.wait_ge(scaled_ready[hd], upto(c))
                        pe.wait_ge(run_ready[hd], upto(c, 1))
                        to_channels(nc, ps_r[:, hd, :], scaled[:, b % 2, hd, :], m.ident[:, :]).then_inc(rows_t[hd], 1)
                if now := stage(k, j, 1):
                    c, r, b = now
                    for hd in heads:
                        pe.wait_ge(run_ready[hd], upto(c))
                        pe.wait_ge(back_ready[hd], upto(c, 1))
                        to_channels(nc, ps_b[:, hd, :], run[:, b % 2, hd, :], m.ident[:, :]).then_inc(back_t[hd], 1)
            loop_steps(pe, step, 1)

        @block.vector
        def _(dve):
            for hd in heads:
                nc.vector.memset(run[:, 1, hd, PER * P - 1:PER * P], 0.0).then_inc(run_ready[hd], BUFS)
                dve.sem_inc(scaled_ready[hd], BUFS)

            def step(k, j):
                if now := stage(k, j, 0):
                    c, r, b = now
                    dve.wait_ge(rows_in[b], (r + 1) * 16)
                    for hd in heads:
                        dve.wait_ge(rows_t[hd], upto(c, 2))
                        nc.vector.tensor_tensor(scaled[:, b % 2, hd, :].rearrange("p (i s w) -> p i s w", i=PER, s=STREAMS),
                                                rows[:, b, :].rearrange("p (s i w) -> p i s w", s=STREAMS, i=PER)[:, :, :, 0:D],
                                                edge.logit[:, bass.ds(c * U, U), hd].rearrange("p (s i) -> p i s", s=STREAMS).unsqueeze(3).broadcast_to([P, PER, STREAMS, D]),
                                                ALU.mult).then_inc(scaled_ready[hd], 1)
                if now := stage(k, j, 1):
                    c, r, b = now
                    dve.wait_ge(keep_in[b], (r + 1) * (16 * STREAMS))
                    for hd in heads:
                        dve.wait_ge(rows_t[hd], upto(c))
                        dve.wait_ge(back_t[hd], upto(c, 2))
                        dve.wait_ge(run_ready[hd], upto(c, 1))
                        nc.vector.tensor_tensor_scan(run[:, b % 2, hd, :], keep[:, b, :], ps_r[:, hd, :],
                                                     run[:, (b + 1) % 2, hd, PER * P - 1:PER * P], ALU.mult, ALU.add).then_inc(run_ready[hd], 1)
            loop_steps(dve, step, 1)


def phase_gat_out(nc, m, d):
    with ExitStack() as ctx:
        s = Scope(nc, ctx, "go")
        t = Norm(s)
        sums = s.sb("sums", [P, NB, HEADS * D])
        carried = s.sb("carried", [P, HEADS * D])
        weights = s.sb("weights", [P, NB, 2 * AW])
        den = s.sb("den", [P, NB, HEADS])
        norm = s.sb("norm", [P, NB, HEADS * D])
        y = s.sb("y", [P, NB, D])
        z = s.sb("z", [P, NB, D])
        lin_wt = s.sb("lin_wt", [D, HEADS, D])
        split = s.sb("split", [D, 2, 2 * D])
        w1 = s.sb("w1", [D, HEADS, D])
        w1_01, w1_2 = s.sb("w1_01", [P, D]), s.sb("w1_2", [D, D])
        bias_01, bias_2 = s.sb("bias_01", [P, 1]), s.sb("bias_2", [D, 1])
        fold_01, fold_2 = s.sb("fold_01", [P, D]), s.sb("fold_2", [D, D])
        w2 = s.sb("w2", [D, D])
        vec = s.sb("vec", [P, 6, D])
        bias = s.sb("bias", [P, D])
        left = s.sb("left", [P, 2, P])
        right = s.sb("right", [D, 2, P])
        ps_w = s.ps("ps_w", [P, 3, D])
        ps_l, ps_r = s.ps("ps_l", [P, 2, 512]), s.ps("ps_r", [D, 2, 512])
        ps_y = s.ps("ps_y", [P, 2, 512])
        gathered, loaded, padded, folded, fold_taken = (s.sem(n) for n in ("gathered", "loaded", "padded", "folded", "fold_taken"))
        sums_ready, block_t, block_taken, done, drained = (s.sem(n) for n in ("sums_ready", "block_t", "block_taken", "done", "drained"))
        var, std, chain, y_ready = (s.sem(n) for n in ("var", "std", "chain", "y_ready"))
        sums_h = sums[:, :, :].rearrange("p b (h w) -> p b h w", h=HEADS)
        block = ctx.enter_context(nc.Block())

        @block.gpsimd
        def _(pool):
            for b in range(NB):
                pool.indirect_dma_start(sums[:, b, :], None, d["sums_heads"], bass.IndirectOffsetOnAxis(m.end_row[:, b:b + 1], 0)).then_inc(gathered, 16)
                pool.indirect_dma_start(weights[:, b, :], None, d["filled8"][0:ROWS, :], bass.IndirectOffsetOnAxis(m.end_pos[:, b:b + 1], 0)).then_inc(gathered, 16)
            pool.wait_ge(gathered, 32 * NB)

        @block.sync
        def _(sp):
            sp.dma_start(lin_wt[:, :, :], d["lin_wt"].rearrange("(h c) i -> c h i", h=HEADS)).then_inc(loaded, 16)
            sp.dma_start(w1[:, :, :], d["w1"].rearrange("(h c) i -> c h i", h=HEADS)).then_inc(loaded, 16)
            sp.dma_start(w1_01[:, :], d["w1"][0:P, :]).then_inc(loaded, 16)
            sp.dma_start(w1_2[:, :], d["w1"][P:HEADS * D, :]).then_inc(loaded, 16)
            sp.dma_start(bias_01[:, :], d["gat_bias"][0:P].unsqueeze(1)).then_inc(loaded, 16)
            sp.dma_start(bias_2[:, :], d["gat_bias"][P:HEADS * D].unsqueeze(1)).then_inc(loaded, 16)
            sp.dma_start(w2[:, :], d["w2"]).then_inc(loaded, 16)
            sp.dma_start(carried[:, :], d["sums_heads"][ENDROW:ENDROW + 1, :].broadcast_to([P, HEADS * D])).then_inc(loaded, 16)
            for i, v in enumerate((d["b1"], d["ln1_g"], d["ln1_b"], d["b2"], d["ln2_g"], d["ln2_b"])):
                sp.dma_start(vec[:, i, :], v.unsqueeze(0).broadcast_to([P, D])).then_inc(loaded, 16)
            sp.wait_ge(loaded, 16 * 14)

        @block.tensor
        def _(pe):
            pe.wait_ge(loaded, 16 * 14)
            pe.wait_ge(padded, 1)
            nc.tensor.matmul(ps_w[:, 0, :], split[:, 0, :], w1[:, 0, :], start=True, stop=False)
            nc.tensor.matmul(ps_w[:, 0, :], split[:, 1, :], w1[:, 1, :], start=False, stop=True)
            nc.tensor.matmul(ps_w[0:D, 1, :], lin_wt[:, 2, :], w1[:, 2, :], start=True, stop=True)
            nc.tensor.matmul(ps_w[:, 2, :], bias_01[:, 0:1].broadcast_to([P, P]), w1_01[:, :], start=True, stop=False)
            nc.tensor.matmul(ps_w[:, 2, :], bias_2[:, 0:1].broadcast_to([D, P]), w1_2[:, :], start=False, stop=True).then_inc(folded, 1)
            pe.wait_ge(fold_taken, 2)
            pe.wait_ge(sums_ready, 1)
            for b in range(NB + 1):
                if b < NB:
                    if b >= 2:
                        pe.wait_ge(block_taken, 2 * (b - 1))
                    nc.tensor.transpose(ps_l[:, b % 2, 0:P], norm[:, b, 0:2 * D], m.ident[:, :])
                    nc.tensor.transpose(ps_r[:, b % 2, 0:P], norm[:, b, 2 * D:HEADS * D], m.ident[:, :]).then_inc(block_t, 1)
                if b >= 1:
                    q = b - 1
                    pe.wait_ge(block_taken, 2 * b)
                    if q >= 16 and q % 8 == 0:
                        pe.wait_ge(drained, q // 8 - 1)
                    o = ps_y[:, q // 8 % 2, q % 8 * D:(q % 8 + 1) * D]
                    nc.tensor.matmul(o, left[:, q % 2, :], fold_01[:, :], start=True, stop=False)
                    nc.tensor.matmul(o, right[:, q % 2, :], fold_2[:, :], start=False, stop=True).then_inc(done, 1)
            pe.wait_ge(y_ready, 1)
            for b in range(NB + 1):
                if b < NB:
                    pe.wait_ge(block_taken, 2 * NB + max(b - 1, 0))
                    nc.tensor.transpose(ps_r[:, b % 2, 0:P], y[:, b, :], m.ident[:, :]).then_inc(block_t, 1)
                if b >= 1:
                    q = b - 1
                    pe.wait_ge(block_taken, 2 * NB + b)
                    g = q // 8
                    if q % 8 == 0:
                        pe.wait_ge(drained, 7 + max(g - 1, 0))
                    nc.tensor.matmul(ps_y[:, g % 2, q % 8 * D:(q % 8 + 1) * D], right[:, q % 2, :], w2[:, :], start=True, stop=True).then_inc(done, 1)

        @block.scalar
        def _(act):
            for b in range(NB):
                act.wait_ge(block_t, b + 1)
                if b >= 2:
                    act.wait_ge(done, b - 1)
                nc.scalar.copy(left[:, b % 2, :], ps_l[:, b % 2, 0:P]).then_inc(block_taken, 1)
                nc.scalar.copy(right[:, b % 2, :], ps_r[:, b % 2, 0:P]).then_inc(block_taken, 1)
            root(nc, act, t, var, std, 1)
            for b in range(NB):
                act.wait_ge(block_t, NB + b + 1)
                act.wait_ge(done, NB + max(b - 1, 0))
                nc.scalar.copy(right[:, b % 2, :], ps_r[:, b % 2, 0:P]).then_inc(block_taken, 1)
            root(nc, act, t, var, std, 2)
            root(nc, act, t, var, std, 3)

        @block.vector
        def _(dve):
            link = linker(dve, chain)
            link(nc.vector.memset(split[:, :, :], 0.0))
            dve.wait_ge(loaded, 16 * 14)
            link(nc.vector.tensor_copy(split[:, 0, 0:D], lin_wt[:, 0, :]))
            nc.vector.tensor_copy(split[:, 1, D:2 * D], lin_wt[:, 1, :]).then_inc(padded, 1)
            dve.wait_ge(folded, 1)
            nc.vector.tensor_copy(fold_01[:, :], ps_w[:, 0, :]).then_inc(fold_taken, 1)
            nc.vector.tensor_copy(fold_2[:, :], ps_w[0:D, 1, :]).then_inc(fold_taken, 1)
            link(nc.vector.tensor_tensor(bias[:, :], vec[:, 0, :], ps_w[:, 2, :], ALU.add))
            dve.wait_ge(gathered, 32 * NB)
            link(nc.vector.tensor_tensor(den[:, :, :], weights[:, :, 0:HEADS], bcast(m.has[:, :], HEADS), ALU.mult))
            link(nc.vector.tensor_tensor(den[:, :, :], den[:, :, :], m.self_w[:, :, :], ALU.add))
            link(nc.vector.reciprocal(den[:, :, :], den[:, :, :]))
            for hd in range(HEADS):
                part = sums_h[:, :, hd, :]
                link(nc.vector.tensor_tensor(z[:, :, :], bcast(m.join[:, :], D), carried[:, hd * D:(hd + 1) * D].unsqueeze(1).broadcast_to([P, NB, D]), ALU.mult))
                link(nc.vector.tensor_tensor(part, part, z[:, :, :], ALU.add))
                link(nc.vector.tensor_tensor(z[:, :, :], m.h[:, :, :], bcast(m.self_w[:, :, hd], D), ALU.mult))
                link(nc.vector.tensor_tensor(part, part, z[:, :, :], ALU.add))
                ins = nc.vector.tensor_tensor(norm[:, :, hd * D:(hd + 1) * D], part, bcast(den[:, :, hd], D), ALU.mult)
                if hd < HEADS - 1:
                    link(ins)
                else:
                    ins.then_inc(sums_ready, 1)
            wide = lambda i, n=NB: (vec[:, i, :] if isinstance(i, int) else i).unsqueeze(1).broadcast_to([P, n, D])

            def drain(first, add):
                for g in range(7):
                    lo, hi = g * 8, min(g * 8 + 8, NB)
                    dve.wait_ge(done, first + hi)
                    nc.vector.tensor_tensor(z[:, lo:hi, :], ps_y[:, g % 2, 0:(hi - lo) * D].rearrange("p (b w) -> p b w", w=D),
                                            wide(add, hi - lo), ALU.add).then_inc(drained, 1)

            drain(0, bias[:, :])
            dve.wait_ge(drained, 7)
            link(nc.vector.tensor_tensor(z[:, :, :], z[:, :, :], m.h[:, :, :], ALU.add))
            layer_norm(nc, link, dve, y[:, :, :], z[:, :, :], t, var, std, 1)
            link(nc.vector.tensor_tensor(y[:, :, :], y[:, :, :], wide(1), ALU.mult))
            nc.vector.tensor_tensor(y[:, :, :], y[:, :, :], wide(2), ALU.add).then_inc(y_ready, 1)
            dve.wait_ge(y_ready, 1)
            drain(NB, 3)
            dve.wait_ge(drained, 14)
            link(nc.vector.tensor_tensor(z[:, :, :], z[:, :, :], y[:, :, :], ALU.add))
            layer_norm(nc, link, dve, y[:, :, :], z[:, :, :], t, var, std, 2)
            link(nc.vector.tensor_tensor(y[:, :, :], y[:, :, :], wide(4), ALU.mult))
            link(nc.vector.tensor_tensor(y[:, :, :], y[:, :, :], wide(5), ALU.add))
            link(nc.vector.tensor_tensor(m.x[:, :, :], m.x[:, :, :], y[:, :, :], ALU.add))
            layer_norm(nc, link, dve, m.h[:, :, :], m.x[:, :, :], t, var, std, 3)
            link(nc.vector.tensor_scalar(m.h[:, :, :], m.h[:, :, :], 0.0, None, ALU.max))


LAYERS = 3


def gather_sums(nc, pool, m, d, node, gathered):
    for b in range(NB):
        pool.indirect_dma_start(node[:, b, :], None, d["sums"], bass.IndirectOffsetOnAxis(m.end_row[:, b:b + 1], 0)).then_inc(gathered, 16)


def scatter_starts(nc, pool, m, d, rows, scattered):
    for b in range(NB):
        pool.indirect_dma_start(d["filled"], bass.IndirectOffsetOnAxis(m.start_row[:, b:b + 1], 0), rows[:, b, :], None).then_inc(scattered, 16)


def repeat_start(nc, sp, m, d, scattered, border_out):
    sp.wait_ge(scattered, 16 * NB)
    sp.nop(nofuse=True)
    row = nc.sync.value_load(m.first[0:1, 0:1], min_val=0, max_val=ROWS - 1)
    sp.dma_start(d["filled"][BORDER:BORDER + 1, :], d["filled"][bass.ds(row, 1), :]).then_inc(border_out, 16)
    sp.wait_ge(border_out, 16)


def load_flags(sp, flags, d, kinds, c, b, flags_in):
    for st in range(STREAMS):
        sp.dma_start(flags[st * D:(st + 1) * D, b], flags_row(d["flags"], kinds, c, st, D)).then_inc(flags_in[b], 16)


def to_channels(nc, out, rows, ident):
    for i in range(PER):
        last = nc.tensor.transpose(out[:, i * P:(i + 1) * P], rows[:, i * P:(i + 1) * P], ident)
    return last


def slot(u):
    return u % PER * STREAMS + u // PER


def gather_rows(pool, rows, index, table, index_ready, rows_in, layer=0):
    def step(k, j):
        c, k, b = stage(k, j, 0)
        pool.wait_ge(index_ready, layer * CHUNKS + c + 1)
        pool.nop(nofuse=True)
        for u in range(U):
            pool.indirect_dma_start(rows[:, b, slot(u) * D:(slot(u) + 1) * D], None, table,
                                    bass.IndirectOffsetOnAxis(index[:, b, u:u + 1], 0)).then_inc(rows_in[b], 16)
    loop_steps(pool, step, 0)


def phase_light(nc, m, d):
    with ExitStack() as ctx:
        s = Scope(nc, ctx, "li")
        rows = s.sb("rows", [P, BUFS, U * D])
        index = s.sb("index", [P, BUFS, U], I32)
        keep = s.sb("keep", [P, BUFS, PER * P], BF16)
        run = s.sb("run", [P, 2, PER * P])
        back = s.sb("back", [P, BUFS, U * D])
        node = s.sb("node", [P, NB, D])
        wide = s.sb("wide", [P, NB, D])
        carried = s.sb("carried", [P, D])
        ps_r = s.ps("ps_r", [P, 2, PER * P])
        ps_b = s.ps("ps_b", [P, 2, PER * P])
        index_ready, rows_t, run_ready, back_t, back_ready = (s.sem(n) for n in ("index_ready", "rows_t", "run_ready", "back_t", "back_ready"))
        rows_in, keep_in, stored = ([s.sem(f"{n}{b}") for b in range(BUFS)] for n in ("rows_in", "keep_in", "stored"))
        table_out, all_out, gathered, carried_in, mean_ready, chain = (s.sem(n) for n in ("table_out", "all_out", "gathered", "carried_in", "mean_ready", "chain"))
        block = ctx.enter_context(nc.Block())

        @block.gpsimd
        def _(pool):
            with pool.Fori(0, LAYERS) as n:
                pool.wait_ge(table_out, n * 16 + 16)
                gather_rows(pool, rows, index, d["table"], index_ready, rows_in, n)
                pool.wait_ge(all_out, n + 1)
                pool.nop(nofuse=True)
                gather_sums(nc, pool, m, d, node, gathered)

        @block.sync
        def _(sp):
            sp.dma_start(d["table"].rearrange("(p b) w -> p b w", b=NB), m.h[:, :, :]).then_inc(table_out, 16)
            with sp.Fori(0, LAYERS) as n:
                def step(k, j):
                    if now := stage(k, j, 0):
                        c, r, b = now
                        sp.wait_ge(run_ready, upto(c, BUFS, n))
                        sp.nop(nofuse=True)
                        load_flags(sp, keep, d, 0, c, b, keep_in)
                    if now := stage(k, j, 3):
                        c, r, b = now
                        sp.wait_ge(back_ready, upto(c, 0, n))
                        sp.nop(nofuse=True)
                        sp.dma_start(d["sums"][bass.ds(c * (P * U), P * U), :].rearrange("(p u) w -> p (u w)", u=U), back[:, b, :]).then_inc(stored[b], 16)
                loop_steps(sp, step, 3)
                for b in range(BUFS):
                    sp.wait_ge(stored[b], n * (16 * LOOPS) + 16 * (LOOPS + 1))
                sp.nop(nofuse=True)
                sp.sem_inc(all_out, 1)
                sp.dma_start(carried[:, :], d["sums"][ENDROW:ENDROW + 1, :].broadcast_to([P, D])).then_inc(carried_in, 16)
                sp.wait_ge(mean_ready, n + 1)
                sp.dma_start(d["table"].rearrange("(p b) w -> p b w", b=NB), node[:, :, :]).then_inc(table_out, 16)
            sp.wait_ge(table_out, 16 * (LAYERS + 1))

        @block.scalar
        def _(act):
            act.sem_inc(back_ready, BUFS)
            for b in range(BUFS):
                act.sem_inc(stored[b], 16)
            with act.Fori(0, LAYERS) as n:
                def step(k, j):
                    if now := stage(k, j, 0):
                        c, r, b = now
                        act.wait_ge(rows_t, upto(c, BUFS, n))
                        nc.scalar.copy(index[:, b, :], m.src[:, bass.ds(c * U, U)]).then_inc(index_ready, 1)
                    if now := stage(k, j, 2):
                        c, r, b = now
                        act.wait_ge(back_t, upto(c, 0, n))
                        act.wait_ge(stored[b], n * (16 * LOOPS) + (r + 1) * 16)
                        nc.scalar.copy(back[:, b, :], ps_b[:, b % 2, :]).then_inc(back_ready, 1)
                loop_steps(act, step, 2)

        @block.tensor
        def _(pe):
            pe.sem_inc(rows_t, BUFS)
            pe.sem_inc(back_t, BUFS)
            with pe.Fori(0, LAYERS) as n:
                def step(k, j):
                    if now := stage(k, j, 0):
                        c, r, b = now
                        pe.wait_ge(rows_in[b], n * (16 * U * LOOPS) + (r + 1) * (16 * U))
                        pe.wait_ge(run_ready, upto(c, 2, n))
                        to_channels(nc, ps_r[:, b % 2, :], rows[:, b, :], m.ident[:, :]).then_inc(rows_t, 1)
                    if now := stage(k, j, 1):
                        c, r, b = now
                        pe.wait_ge(run_ready, upto(c, 0, n))
                        pe.wait_ge(back_ready, upto(c, 2, n))
                        to_channels(nc, ps_b[:, b % 2, :], run[:, b % 2, :], m.ident[:, :]).then_inc(back_t, 1)
                loop_steps(pe, step, 1)

        @block.vector
        def _(dve):
            dve.sem_inc(run_ready, BUFS)
            with dve.Fori(0, LAYERS) as n:
                nc.vector.memset(run[:, 1, PER * P - 1:PER * P], 0.0).then_inc(chain, 1)
                dve.wait_ge(chain, n * 3 + 1)

                def step(k, j):
                    c, r, b = stage(k, j, 0)
                    dve.wait_ge(rows_t, upto(c, 0, n))
                    dve.wait_ge(keep_in[b], n * (16 * STREAMS * LOOPS) + (r + 1) * (16 * STREAMS))
                    dve.wait_ge(back_t, upto(c, 2, n))
                    dve.wait_ge(run_ready, upto(c, 1, n))
                    nc.vector.tensor_tensor_scan(run[:, b % 2, :], keep[:, b, :], ps_r[:, b % 2, :],
                                                 run[:, (b + 1) % 2, PER * P - 1:PER * P], ALU.mult, ALU.add).then_inc(run_ready, 1)
                loop_steps(dve, step, 0)
                dve.wait_ge(carried_in, n * 16 + 16)
                dve.wait_ge(gathered, n * (16 * NB) + 16 * NB)
                join_sum(nc, lambda ins, i: (ins.then_inc(chain, 1), dve.wait_ge(chain, n * 3 + (i + 2))), m, node, carried, wide[:, :, :])
                nc.vector.tensor_tensor(node[:, :, :], node[:, :, :], bcast(m.inv_count[:, :], D), ALU.mult).then_inc(mean_ready, 1)
            dve.wait_ge(mean_ready, LAYERS)
            nc.vector.tensor_tensor(m.x[:, :, :], m.x[:, :, :], node[:, :, :], ALU.add)


def join_sum(nc, link, m, node, carried, wide):
    link(nc.vector.tensor_tensor(wide, bcast(m.join[:, :], D), carried[:, :].unsqueeze(1).broadcast_to([P, NB, D]), ALU.mult), 0)
    link(nc.vector.tensor_tensor(node[:, :, :], node[:, :, :], wide, ALU.add), 1)


def phase_edge_tables(nc, m, d):
    with ExitStack() as ctx:
        s = Scope(nc, ctx, "et")
        t = Norm(s)
        w = s.sb("w", [D, 2, D])
        b1 = s.sb("b1", [P, D])
        h_t = s.sb("h_t", [D, 2, P])
        at_dst, at_src = s.sb("at_dst", [P, NB, D]), s.sb("at_src", [P, NB, D])
        ps_t = s.ps("ps_t", [D, 2, 512])
        ps_y = s.ps("ps_y", [P, 2, 4, 2, D])
        loaded, var, std, chain, h_ready, w_ready = (s.sem(n) for n in ("loaded", "var", "std", "chain", "h_ready", "w_ready"))
        transposed, taken, done, src_ready, dst_ready, stored, scattered = (s.sem(n) for n in ("transposed", "taken", "done", "src_ready", "dst_ready", "stored", "scattered"))
        border_out = s.sem("border_out")
        G = -(-NB // 4)
        block = ctx.enter_context(nc.Block())

        @block.sync
        def _(sp):
            sp.dma_start(w[:, :, :], d["w1e"].rearrange("(a i) o -> i a o", a=2)).then_inc(loaded, 16)
            sp.dma_start(b1[:, :], d["b1e"].unsqueeze(0).broadcast_to([P, D])).then_inc(loaded, 16)
            sp.wait_ge(src_ready, G)
            sp.dma_start(d["table"].rearrange("(p b) w -> p b w", b=NB), at_src[:, :, :]).then_inc(stored, 16)
            sp.wait_ge(stored, 16)
            sp.wait_ge(loaded, 32)
            repeat_start(nc, sp, m, d, scattered, border_out)

        @block.gpsimd
        def _(pool):
            pool.wait_ge(dst_ready, G)
            scatter_starts(nc, pool, m, d, at_dst, scattered)

        @block.scalar
        def _(act):
            root(nc, act, t, var, std, 1)
            for b in range(NB):
                act.wait_ge(transposed, b + 1)
                if b >= 2:
                    act.wait_ge(done, b - 1)
                nc.scalar.copy(h_t[:, b % 2, :], ps_t[:, b % 2, 0:P]).then_inc(taken, 1)

        @block.tensor
        def _(pe):
            pe.wait_ge(h_ready, 1)
            pe.wait_ge(w_ready, 1)
            for b in range(NB + 1):
                if b < NB:
                    if b >= 2:
                        pe.wait_ge(taken, b - 1)
                    nc.tensor.transpose(ps_t[:, b % 2, 0:P], m.h[:, b, :], m.ident[:, :]).then_inc(transposed, 1)
                if b >= 1:
                    q = b - 1
                    pe.wait_ge(taken, b)
                    if q >= 8 and q % 4 == 0:
                        pe.wait_ge(src_ready, q // 4 - 1)
                        pe.wait_ge(dst_ready, q // 4 - 1)
                    nc.tensor.matmul(ps_y[:, q // 4 % 2, q % 4, :, :], h_t[:, q % 2, :], w[:, :, :], start=True, stop=True).then_inc(done, 1)

        @block.vector
        def _(dve):
            link = linker(dve, chain)
            dve.wait_ge(loaded, 32)
            nc.vector.tensor_tensor(w[:, 0, :], w[:, 0, :], w[:, 1, :], ALU.subtract).then_inc(w_ready, 1)
            layer_norm(nc, link, dve, m.h[:, :, :], m.x[:, :, :], t, var, std, 1)
            nc.vector.tensor_scalar(m.h[:, :, :], m.h[:, :, :], 0.0, None, ALU.max).then_inc(h_ready, 1)
            for g in range(G):
                lo, hi = g * 4, min(g * 4 + 4, NB)
                dve.wait_ge(done, hi)
                nc.vector.tensor_tensor(at_dst[:, lo:hi, :], ps_y[:, g % 2, 0:hi - lo, 0, :], b1[:, :].unsqueeze(1).broadcast_to([P, hi - lo, D]),
                                        ALU.add).then_inc(dst_ready, 1)
                nc.vector.tensor_copy(at_src[:, lo:hi, :], ps_y[:, g % 2, 0:hi - lo, 1, :]).then_inc(src_ready, 1)


class Pass:

    def __init__(self, s):
        self.rows = s.sb("rows", [P, BUFS, U * D])
        self.index = s.sb("index", [P, BUFS, U], I32)
        self.fill = s.sb("fill", [P, BUFS, U * D])
        self.flags = s.sb("flags", [P, BUFS, 2, PER * P], BF16)
        self.dest = s.sb("dest", [P, 2, PER * P])
        self.run = s.sb("run", [P, 2, PER * P])
        self.back = s.sb("back", [P, BUFS, U * D])
        self.ps_r, self.ps_f, self.ps_m, self.ps_b = (s.ps(n, [P, 2, PER * P]) for n in ("ps_r", "ps_f", "ps_m", "ps_b"))
        self.rows_in, self.fill_in, self.flags_in, self.stored = ([s.sem(f"{n}{b}") for b in range(BUFS)] for n in ("rows_in", "fill_in", "flags_in", "stored"))
        self.index_ready, self.both_t, self.dest_ready, self.run_ready = (s.sem(n) for n in ("index_ready", "both_t", "dest_ready", "run_ready"))
        self.back_t, self.back_ready, self.message = (s.sem(n) for n in ("back_t", "back_ready", "message"))


def pass_sync(sp, d, w):
    def step(k, j):
        if now := stage(k, j, 0):
            c, r, b = now
            sp.wait_ge(w.both_t, upto(c, BUFS))
            sp.nop(nofuse=True)
            sp.dma_start(w.fill[:, b, :], d["filled"][bass.ds(c * (P * U), P * U), :].rearrange("(p u) w -> p (u w)", u=U)).then_inc(w.fill_in[b], 16)
            sp.wait_ge(w.run_ready, upto(c, BUFS))
            sp.nop(nofuse=True)
            load_flags(sp, w.flags, d, slice(0, 2), c, b, w.flags_in)
        if now := stage(k, j, 4):
            c, r, b = now
            sp.wait_ge(w.back_ready, upto(c))
            sp.nop(nofuse=True)
            sp.dma_start(d["sums"][bass.ds(c * (P * U), P * U), :].rearrange("(p u) w -> p (u w)", u=U), w.back[:, b, :]).then_inc(w.stored[b], 16)
    loop_steps(sp, step, 4)
    for b in range(BUFS):
        sp.wait_ge(w.stored[b], 16 * (LOOPS + 1))


def pass_scalar(nc, act, m, w, middle):
    act.sem_inc(w.back_ready, BUFS)
    for b in range(BUFS):
        act.sem_inc(w.stored[b], 16)

    def step(k, j):
        if now := stage(k, j, 0):
            c, r, b = now
            act.wait_ge(w.both_t, upto(c, BUFS))
            nc.scalar.copy(w.index[:, b, :], m.src[:, bass.ds(c * U, U)]).then_inc(w.index_ready, 1)
        if now := stage(k, j, 1):
            middle(*now)
        if now := stage(k, j, 3):
            c, r, b = now
            act.wait_ge(w.back_t, upto(c))
            act.wait_ge(w.stored[b], (r + 1) * 16)
            nc.scalar.copy(w.back[:, b, :], w.ps_b[:, b % 2, :]).then_inc(w.back_ready, 1)
    loop_steps(act, step, 3)


def pass_tensor(nc, pe, m, w, free, middle):
    pe.sem_inc(w.both_t, BUFS)
    pe.sem_inc(w.back_t, BUFS)
    pe.sem_inc(w.message, BUFS)

    def step(k, j):
        if now := stage(k, j, 0):
            c, r, b = now
            pe.wait_ge(w.fill_in[b], (r + 1) * 16)
            free(c)
            to_channels(nc, w.ps_f[:, b % 2, :], w.fill[:, b, :], m.ident[:, :])
            pe.wait_ge(w.rows_in[b], (r + 1) * (16 * U))
            to_channels(nc, w.ps_r[:, b % 2, :], w.rows[:, b, :], m.ident[:, :]).then_inc(w.both_t, 1)
        if now := stage(k, j, 1):
            middle(*now)
        if now := stage(k, j, 2):
            c, r, b = now
            pe.wait_ge(w.run_ready, upto(c))
            pe.wait_ge(w.back_ready, upto(c, 2))
            to_channels(nc, w.ps_b[:, b % 2, :], w.run[:, b % 2, :], m.ident[:, :]).then_inc(w.back_t, 1)
    loop_steps(pe, step, 2)


def spread_dest(nc, dve, w, c, r, b, used):
    dve.wait_ge(w.both_t, upto(c))
    dve.wait_ge(w.flags_in[b], (r + 1) * (16 * STREAMS))
    used(c)
    dve.wait_ge(w.dest_ready, upto(c, 1))
    nc.vector.tensor_tensor_scan(w.dest[:, b % 2, :], w.flags[:, b, 0, :], w.ps_f[:, b % 2, :],
                                 w.dest[:, (b + 1) % 2, PER * P - 1:PER * P], ALU.mult, ALU.add).then_inc(w.dest_ready, 1)
    dve.wait_ge(w.dest_ready, upto(c))


def phase_edge_max(nc, m, d):
    with ExitStack() as ctx:
        s = Scope(nc, ctx, "em")
        w = Pass(s)
        both = s.sb("both", [P, 2, PER * P])
        hidden = s.sb("hidden", [P, 2, PER * P])
        w2 = s.sb("w2", [P, P])
        both_ready, hidden_ready, w_in, w_clear = (s.sem(n) for n in ("both_ready", "hidden_ready", "w_in", "w_clear"))
        block = ctx.enter_context(nc.Block())

        @block.gpsimd
        def _(pool):
            gather_rows(pool, w.rows, w.index, d["table"], w.index_ready, w.rows_in)

        @block.sync
        def _(sp):
            sp.wait_ge(w_clear, 1)
            for st in range(STREAMS):
                sp.dma_start(w2[st * D:(st + 1) * D, st * D:(st + 1) * D], d["w2e"]).then_inc(w_in, 16)
            pass_sync(sp, d, w)

        @block.scalar
        def _(act):
            act.sem_inc(hidden_ready, BUFS)

            def relu(c, r, b):
                act.wait_ge(both_ready, upto(c))
                act.wait_ge(w.message, upto(c, 2))
                nc.scalar.activation(hidden[:, b % 2, :], both[:, b % 2, :], ACT.Relu).then_inc(hidden_ready, 1)
            pass_scalar(nc, act, m, w, relu)

        @block.tensor
        def _(pe):
            pe.wait_ge(w_in, 16 * STREAMS)

            def free(c):
                pe.wait_ge(both_ready, upto(c, 2))

            def messages(c, r, b):
                pe.wait_ge(hidden_ready, upto(c))
                pe.wait_ge(w.run_ready, upto(c, 2))
                nc.tensor.matmul(w.ps_m[:, b % 2, :], w2[:, :], hidden[:, b % 2, :], start=True, stop=True).then_inc(w.message, 1)
            pass_tensor(nc, pe, m, w, free, messages)

        @block.vector
        def _(dve):
            nc.vector.memset(w2[:, :], 0.0).then_inc(w_clear, 1)
            nc.vector.memset(w.dest[:, 1, PER * P - 1:PER * P], 0.0).then_inc(w.dest_ready, BUFS)
            nc.vector.memset(w.run[:, 1, PER * P - 1:PER * P], -BIG).then_inc(w.run_ready, BUFS)
            dve.sem_inc(both_ready, BUFS)

            def used(c):
                dve.wait_ge(both_ready, upto(c, 2))

            def step(k, j):
                if now := stage(k, j, 1):
                    c, r, b = now
                    dve.wait_ge(w.message, upto(c))
                    dve.wait_ge(w.back_t, upto(c, 2))
                    dve.wait_ge(w.run_ready, upto(c, 1))
                    nc.vector.tensor_tensor_scan(w.run[:, b % 2, :], w.flags[:, b, 1, :], w.ps_m[:, b % 2, :],
                                                 w.run[:, (b + 1) % 2, PER * P - 1:PER * P], ALU.add, ALU.max).then_inc(w.run_ready, 1)
                if now := stage(k, j, 0):
                    c, r, b = now
                    spread_dest(nc, dve, w, c, r, b, used)
                    dve.wait_ge(hidden_ready, upto(c, 2))
                    nc.vector.tensor_tensor(both[:, b % 2, :], w.dest[:, b % 2, :], w.ps_r[:, b % 2, :], ALU.add).then_inc(both_ready, 1)
            loop_steps(dve, step, 1)


def phase_edge_out(nc, m, d):
    with ExitStack() as ctx:
        s = Scope(nc, ctx, "eo")
        t = Norm(s)
        node = s.sb("node", [P, NB, D])
        carried = s.sb("carried", [P, D])
        apart = s.sb("apart", [P, NB])
        b2 = s.sb("b2", [P, D])
        stored, gathered, loaded, border_out = (s.sem(n) for n in ("stored", "gathered", "loaded", "border_out"))
        chain, var, std, h_ready, scattered = (s.sem(n) for n in ("chain", "var", "std", "h_ready", "scattered"))
        block = ctx.enter_context(nc.Block())

        @block.scalar
        def _(act):
            root(nc, act, t, var, std, 1)

        @block.sync
        def _(sp):
            sp.dma_start(b2[:, :], d["b2e"].unsqueeze(0).broadcast_to([P, D])).then_inc(loaded, 16)
            sp.dma_start(carried[:, :], d["sums"][ENDROW:ENDROW + 1, :].broadcast_to([P, D])).then_inc(loaded, 16)
            sp.wait_ge(h_ready, 1)
            sp.dma_start(d["table"].rearrange("(p b) w -> p b w", b=NB), m.h[:, :, :]).then_inc(stored, 16)
            sp.wait_ge(stored, 16)
            repeat_start(nc, sp, m, d, scattered, border_out)

        @block.gpsimd
        def _(pool):
            gather_sums(nc, pool, m, d, node, gathered)
            pool.wait_ge(h_ready, 1)
            scatter_starts(nc, pool, m, d, m.h, scattered)

        @block.vector
        def _(dve):
            link = linker(dve, chain)
            link(nc.vector.tensor_scalar(apart[:, :], m.join[:, :], 1.0, BIG, ALU.subtract, ALU.mult))
            dve.wait_ge(loaded, 32)
            link(nc.vector.tensor_tensor(t.square, bcast(apart[:, :], D), carried[:, :].unsqueeze(1).broadcast_to([P, NB, D]), ALU.add))
            dve.wait_ge(gathered, 16 * NB)
            link(nc.vector.tensor_tensor(node[:, :, :], node[:, :, :], t.square, ALU.max))
            link(nc.vector.tensor_tensor(node[:, :, :], node[:, :, :], b2[:, :].unsqueeze(1).broadcast_to([P, NB, D]), ALU.add))
            link(nc.vector.tensor_tensor(node[:, :, :], node[:, :, :], bcast(m.has[:, :], D), ALU.mult))
            link(nc.vector.tensor_tensor(m.x[:, :, :], m.x[:, :, :], node[:, :, :], ALU.add))
            layer_norm(nc, link, dve, m.h[:, :, :], m.x[:, :, :], t, var, std, 1)
            nc.vector.tensor_scalar(m.h[:, :, :], m.h[:, :, :], 0.0, None, ALU.max).then_inc(h_ready, 1)


def phase_dot(nc, m, d):
    with ExitStack() as ctx:
        s = Scope(nc, ctx, "dt")
        w = Pass(s)
        source = s.sb("source", [P, 2, PER * P])
        prod = s.sb("prod", [P, 2, PER * P])
        scaled = s.sb("scaled", [P, 2, PER * P])
        ones = s.sb("ones", [P, P])
        source_ready, prod_ready, scaled_ready, ones_ready, chain = (s.sem(n) for n in ("source_ready", "prod_ready", "scaled_ready", "ones_ready", "chain"))
        block = ctx.enter_context(nc.Block())

        @block.gpsimd
        def _(pool):
            gather_rows(pool, w.rows, w.index, d["table"], w.index_ready, w.rows_in)

        @block.sync
        def _(sp):
            pass_sync(sp, d, w)

        @block.scalar
        def _(act):
            act.sem_inc(source_ready, BUFS)

            def keep_source(c, r, b):
                act.wait_ge(w.both_t, upto(c))
                act.wait_ge(prod_ready, upto(c))
                act.wait_ge(scaled_ready, upto(c, 2))
                nc.scalar.copy(source[:, b % 2, :], w.ps_r[:, b % 2, :]).then_inc(source_ready, 1)
            pass_scalar(nc, act, m, w, keep_source)

        @block.tensor
        def _(pe):
            pe.wait_ge(ones_ready, 1)

            def free(c):
                pe.wait_ge(source_ready, upto(c, 2))
                pe.wait_ge(prod_ready, upto(c, 2))

            def dots(c, r, b):
                pe.wait_ge(prod_ready, upto(c))
                pe.wait_ge(scaled_ready, upto(c, 2))
                nc.tensor.matmul(w.ps_m[:, b % 2, :], ones[:, :], prod[:, b % 2, :], start=True, stop=True).then_inc(w.message, 1)
            pass_tensor(nc, pe, m, w, free, dots)

        @block.vector
        def _(dve):
            link = linker(dve, chain)
            link(nc.vector.memset(ones[:, :], 0.0))
            nc.vector.memset(ones[0:D, 0:D], 1.0)
            nc.vector.memset(ones[D:P, D:P], 1.0).then_inc(ones_ready, 1)
            nc.vector.memset(w.dest[:, 1, PER * P - 1:PER * P], 0.0).then_inc(w.dest_ready, BUFS)
            nc.vector.memset(w.run[:, 1, PER * P - 1:PER * P], 0.0).then_inc(w.run_ready, BUFS)
            dve.sem_inc(prod_ready, BUFS)
            dve.sem_inc(scaled_ready, BUFS)

            def used(c):
                dve.wait_ge(prod_ready, upto(c, 2))

            def step(k, j):
                if now := stage(k, j, 1):
                    c, r, b = now
                    dve.wait_ge(w.message, upto(c))
                    dve.wait_ge(source_ready, upto(c))
                    dve.wait_ge(w.run_ready, upto(c, 2))
                    nc.vector.tensor_tensor(scaled[:, b % 2, :], source[:, b % 2, :], w.ps_m[:, b % 2, :], ALU.mult).then_inc(scaled_ready, 1)
                    dve.wait_ge(scaled_ready, upto(c))
                    dve.wait_ge(w.back_t, upto(c, 2))
                    dve.wait_ge(w.run_ready, upto(c, 1))
                    nc.vector.tensor_tensor_scan(w.run[:, b % 2, :], w.flags[:, b, 0, :], scaled[:, b % 2, :],
                                                 w.run[:, (b + 1) % 2, PER * P - 1:PER * P], ALU.mult, ALU.add).then_inc(w.run_ready, 1)
                if now := stage(k, j, 0):
                    c, r, b = now
                    spread_dest(nc, dve, w, c, r, b, used)
                    dve.wait_ge(w.message, upto(c, 2))
                    nc.vector.tensor_tensor(prod[:, b % 2, :], w.dest[:, b % 2, :], w.ps_r[:, b % 2, :], ALU.mult).then_inc(prod_ready, 1)
            loop_steps(dve, step, 1)


def phase_dot_out(nc, m, d):
    with ExitStack() as ctx:
        s = Scope(nc, ctx, "do")
        node = s.sb("node", [P, NB, D])
        wide = s.sb("wide", [P, NB, D])
        carried = s.sb("carried", [P, D])
        node_t = s.sb("node_t", [D, 2, P])
        fc = s.sb("fc", [D, D])
        ps_t = s.ps("ps_t", [D, 2, 512])
        ps_y = s.ps("ps_y", [P, 2, 512])
        loaded, gathered, summed, transposed, taken, done, x_ready, out_done, chain = (s.sem(n) for n in ("loaded", "gathered", "summed", "transposed", "taken", "done", "x_ready", "out_done", "chain"))
        G = -(-NB // 8)
        block = ctx.enter_context(nc.Block())

        @block.gpsimd
        def _(pool):
            gather_sums(nc, pool, m, d, node, gathered)

        @block.sync
        def _(sp):
            sp.dma_start(fc[:, :], d["fc_t"]).then_inc(loaded, 16)
            sp.dma_start(carried[:, :], d["sums"][ENDROW:ENDROW + 1, :].broadcast_to([P, D])).then_inc(loaded, 16)
            sp.wait_ge(x_ready, G)
            sp.dma_start(d["out"][0:LASTP * NB, :].rearrange("(p b) w -> p b w", b=NB), m.x[0:LASTP, :, :]).then_inc(out_done, 16)
            sp.dma_start(d["out"][LASTP * NB:N, :].rearrange("(p b) w -> p b w", b=LASTB), m.x[LASTP:LASTP + 1, 0:LASTB, :]).then_inc(out_done, 16)
            sp.wait_ge(out_done, 32)

        @block.scalar
        def _(act):
            for b in range(NB):
                act.wait_ge(transposed, b + 1)
                if b >= 2:
                    act.wait_ge(done, b - 1)
                nc.scalar.copy(node_t[:, b % 2, :], ps_t[:, b % 2, 0:P]).then_inc(taken, 1)

        @block.tensor
        def _(pe):
            pe.wait_ge(loaded, 32)
            pe.wait_ge(summed, 1)
            for b in range(NB + 1):
                if b < NB:
                    if b >= 2:
                        pe.wait_ge(taken, b - 1)
                    nc.tensor.transpose(ps_t[:, b % 2, 0:P], node[:, b, :], m.ident[:, :]).then_inc(transposed, 1)
                if b >= 1:
                    q = b - 1
                    pe.wait_ge(taken, b)
                    if q >= 16 and q % 8 == 0:
                        pe.wait_ge(x_ready, q // 8 - 1)
                    nc.tensor.matmul(ps_y[:, q // 8 % 2, q % 8 * D:(q % 8 + 1) * D], node_t[:, q % 2, :], fc[:, :], start=True, stop=True).then_inc(done, 1)

        @block.vector
        def _(dve):
            dve.wait_ge(loaded, 32)
            dve.wait_ge(gathered, 16 * NB)
            join_sum(nc, lambda ins, i: (ins.then_inc(chain, 1), dve.wait_ge(chain, i + 1)), m, node, carried, wide[:, :, :])
            dve.sem_inc(summed, 1)
            for g in range(G):
                lo, hi = g * 8, min(g * 8 + 8, NB)
                dve.wait_ge(done, hi)
                nc.vector.tensor_tensor(m.x[:, lo:hi, :], m.x[:, lo:hi, :], ps_y[:, g % 2, 0:(hi - lo) * D].rearrange("p (b w) -> p b w", w=D), ALU.add).then_inc(x_ready, 1)


def build(nc, d):
    def dram(name, shape, dt=F32):
        return nc.dram_tensor(name, shape, dt, kind="Internal").ap()

    d["starts"] = dram("starts", [TILES], I32)
    d["flags"] = dram("flags", [2, TILES * P], BF16)
    d["table0"] = dram("table0", [NPAD, TW])
    d["table"] = dram("table", [NPAD, D])
    d["saved"] = dram("saved", [CHUNKS * P, U * TW])
    d["rank8"] = dram("rank8", [CROWS, 2 * AW])
    d["sums_heads"] = dram("sums_heads", [ROWS + NPAD, HEADS * D])
    d["filled8"] = dram("filled8", [ROWS + NPAD, 2 * AW])
    d["node8"] = dram("node8", [NPAD, 2 * AW])
    d["sums"] = dram("sums", [ROWS + NPAD, D])
    d["filled"] = dram("filled", [ROWS + NPAD, D])
    d["start_of"] = dram("start_of", [NPAD, 1], I32)
    d["rank_of"] = dram("rank_of", [TRASH + RANKS, 1], I32)
    with ExitStack() as ctx:
        m = Memory(Scope(nc, ctx, "all"))
        with ExitStack() as gat:
            edge = Edges(Scope(nc, gat, "gat"))
            with ExitStack() as by_rank:
                rk = Ranks(Scope(nc, by_rank, "ranks"))
                phase_ranks(nc, m, rk, d)
                phase_table(nc, m, rk, d, edge)
                acc = Scope(nc, by_rank, "sums").sb("acc", [AW, 2, RANKS])
                phase_gat_max(nc, m, rk, d, edge, acc)
                phase_gat_nodes(nc, m, d, acc)
            phase_gat_weights(nc, m, d, edge)
            phase_gat_sum(nc, m, d, edge)
        phase_gat_out(nc, m, d)
        phase_light(nc, m, d)
        phase_edge_tables(nc, m, d)
        phase_edge_max(nc, m, d)
        phase_edge_out(nc, m, d)
        phase_dot(nc, m, d)
        phase_dot_out(nc, m, d)


def kernel(**inputs):
    import concourse.bacc as bacc
    import numpy as np
    from concourse.bass_utils import run_bass_kernel_spmd

    a = {k: np.asarray(v) for k, v in inputs.items()}
    pad = TILES * P - E
    dst = np.concatenate([a["dst"], np.full(pad, N, np.int32)])

    def columns(v):
        t = v.reshape(STREAMS, CHUNKS, PER, P, *v.shape[1:])
        return np.ascontiguousarray(np.moveaxis(t, (3, 1, 0, 2), (0, 1, 2, 3)).reshape(P, -1))

    arrays = {
        "x": a["x"],
        "dst_rows": np.concatenate([np.full(1, -1, np.int32), dst, np.full(1, N + 1, np.int32)]),
        "dst_cols": columns(dst),
        "src_cols": columns(np.concatenate([a["src"], np.zeros(pad, np.int32)])),
        "attr_cols": columns(np.concatenate([a["edge_attr_5"], np.zeros((pad, EDIM), np.float32)])),
        "lin_w": a["L0_gnn_lin_w"], "lin_wt": np.ascontiguousarray(a["L0_gnn_lin_w"].T),
        "att_src": a["L0_gnn_att_src"], "att_dst": a["L0_gnn_att_dst"], "att_edge": a["L0_gnn_att_edge"],
        "lin_edge_w": a["L0_gnn_lin_edge_w"], "gat_bias": a["L0_gnn_gat_bias"],
        "w1": a["L0_gnn_w1"], "b1": a["L0_gnn_b1"], "ln1_g": a["L0_gnn_ln1_g"], "ln1_b": a["L0_gnn_ln1_b"],
        "w2": a["L0_gnn_w2"], "b2": a["L0_gnn_b2"], "ln2_g": a["L0_gnn_ln2_g"], "ln2_b": a["L0_gnn_ln2_b"],
        "w1e": a["L2_gnn_W1"], "b1e": a["L2_gnn_b1"], "w2e": a["L2_gnn_W2"], "b2e": a["L2_gnn_b2"],
        "fc_t": np.ascontiguousarray(a["L3_gnn_fc_weight"].T),
    }
    nc = bacc.Bacc("TRN2", target_bir_lowering=False, num_devices=1)
    d = {}
    for name, v in arrays.items():
        d[name] = nc.dram_tensor(f"in_{name}", v.shape, mybir.dt.from_np(v.dtype), kind="ExternalInput").ap()
    d["out"] = nc.dram_tensor("out", (N, D), F32, kind="ExternalOutput").ap()
    build(nc, d)
    got = run_bass_kernel_spmd(nc, [{f"in_{k}": v for k, v in arrays.items()}], core_ids=[0])
    return got.results[0]["out"]
```

```python
from contextlib import ExitStack

import concourse.bass as bass
from concourse import mybir

F32, BF16, I32 = mybir.dt.float32, mybir.dt.bfloat16, mybir.dt.int32
ALU, ACT, AX = mybir.AluOpType, mybir.ActivationFunctionType, mybir.AxisListType

P = 128
N, E, D = 6250, 200000, 64
HEADS, EDIM = 3, 5
LAYERS = 3
SLOPE, EPS = 0.2, 1e-5
BIG = 1e38

STREAMS, PER = 2, 4
U = STREAMS * PER
BUFS = 4
TILES = -(-E // (P * U * BUFS)) * U * BUFS
CHUNKS = TILES // U
LOOPS = CHUNKS // BUFS
HALF = TILES // STREAMS
ROWP = 98
ROWT = TILES // ROWP
ROWE = ROWT * P

NB = -(-N // P)
LASTP, LASTB = N // NB, N % NB
NPAD = NB * P
SETS = [(lo, min(lo + 8, NB)) for lo in range(0, NB, 8)]
HALVES = [(0, 24), (24, NB)]
GROUP = 56
GROUPS = TILES // GROUP
KEEP, RESET, END, KINDS = 0, 1, 2, 3
ROWS = TILES * P
ENDROW = ((HALF // PER - 1) * P + P - 1) * U + (PER - 1) * STREAMS
BORDER = 1
TW = D + HEADS + 1
AW = HEADS + 1
SW = HEADS * D + 2 * AW
WW = 2 * HEADS


class Norm:

    def __init__(self, stat, square):
        self.stat, self.square = stat, square

    def some(self, lo, hi):
        return Norm(self.stat[:, lo:hi], self.square[:, lo:hi, :])


def norm_of(s):
    return Norm(s.sb("stat", [P, NB])[:, :], s.sb("square", [P, NB, D])[:, :, :])


class Edges:

    def __init__(self, s):
        self.logit = s.sb("logit", [P, TILES, HEADS])


class Memory:

    def __init__(self, s):
        self.src = s.sb("src", [P, TILES], I32)
        self.x = s.sb("x", [P, NB, D])
        self.h = s.sb("h", [P, NB, D])
        self.node_no = s.sb("node_no", [P, NB + 1])
        self.end_row = s.sb("end_row", [P, NB], I32)
        self.start_row = s.sb("start_row", [P, NB], I32)
        self.end_pos = s.sb("end_pos", [P, NB], I32)
        self.start_pos = s.sb("start_pos", [P, NB], I32)
        self.has = s.sb("has", [P, NB])
        self.first = s.sb("first", [1, 1], I32)
        self.join = s.sb("join", [P, NB])
        self.inv_count = s.sb("inv_count", [P, NB])
        self.logit = s.sb("logit", [P, NB, WW])
        self.edge_sum = s.sb("edge_sum", [P, NB, AW])
        self.iota = s.sb("iota", [P, P])
        self.lane = s.sb("lane", [P, 1])
        self.ident = s.sb("ident", [P, P])


def loop_steps(eng, body, skew):
    first = max(1, -(-skew // BUFS))
    for step in range(first * BUFS):
        body(step // BUFS, step % BUFS)
    with eng.Fori(first, LOOPS) as k:
        for j in range(BUFS):
            body(k, j)
    for step in range(CHUNKS, CHUNKS + skew):
        body(step // BUFS, step % BUFS)


def stage(k, j, skew):
    rounds, b = divmod(j - skew, BUFS)
    k = k + rounds if rounds else k
    c = k * BUFS + b
    if isinstance(k, int) and not 0 <= c < CHUNKS:
        return None
    return c, k, b


def upto(c, back=0, layer=0):
    return layer * CHUNKS + c + (BUFS + 1 - back)


def flags_row(flags, kind, c, st, parts):
    part = flags[kind, bass.ds(c * (PER * P) + st * HALF * P, PER * P)]
    return part.unsqueeze(0).broadcast_to([parts, *part.shape])


def gather_pass(pool, rows, index, table, width, index_ready, rows_in, layer=0):
    def step(k, j):
        c, k, b = stage(k, j, 0)
        pool.wait_ge(index_ready, layer * CHUNKS + c + 1)
        pool.nop(nofuse=True)
        for u in range(U):
            pool.indirect_dma_start(rows[:, b, u * width:(u + 1) * width], None, table,
                                    bass.IndirectOffsetOnAxis(index[:, b, u:u + 1], 0)).then_inc(rows_in[b], 16)
    loop_steps(pool, step, 0)


class Scope:

    def __init__(self, nc, ctx, tag):
        self.nc, self.ctx, self.tag, self.sems = nc, ctx, tag, []

    def sb(self, name, shape, dt=F32):
        return self.ctx.enter_context(self.nc.sbuf_tensor(f"{self.tag}_{name}", shape, dt))

    def ps(self, name, shape, dt=F32):
        return self.ctx.enter_context(self.nc.psum_tensor(f"{self.tag}_{name}", shape, dt))

    def sem(self, name):
        if not self.sems:
            self.ctx.callback(self.clear)
        self.sems.append(self.nc.alloc_semaphore(f"{self.tag}_{name}"))
        return self.sems[-1]

    def clear(self):
        self.nc.clear_and_free_semaphores(self.sems)
        self.nc.all_engine_barrier()


def linker(eng, sem):
    count = [0]

    def link(ins):
        count[0] += 1
        ins.then_inc(sem, 1)
        eng.wait_ge(sem, count[0])
        return count[0]

    return link


def bcast(v, n):
    return v.unsqueeze(2).broadcast_to([*v.shape, n])


def layer_norm(nc, link, dve, out, x, t, sem_var, sem_std, turn):
    link(nc.vector.tensor_reduce(out=t.stat, in_=x, axis=AX.X, op=ALU.add))
    link(nc.vector.tensor_scalar(t.stat, t.stat, 1.0 / D, None, ALU.mult))
    link(nc.vector.tensor_tensor(out, x, bcast(t.stat, D), ALU.subtract))
    link(nc.vector.tensor_tensor(t.square, out, out, ALU.mult))
    link(nc.vector.tensor_reduce(out=t.stat, in_=t.square, axis=AX.X, op=ALU.add))
    nc.vector.tensor_scalar(t.stat, t.stat, 1.0 / D, EPS, ALU.mult, ALU.add).then_inc(sem_var, 1)
    dve.wait_ge(sem_std, turn)
    link(nc.vector.reciprocal(t.stat, t.stat))
    link(nc.vector.tensor_tensor(out, out, bcast(t.stat, D), ALU.mult))


def root(nc, act, t, sem_var, sem_std, turn):
    act.wait_ge(sem_var, turn)
    nc.scalar.activation(t.stat, t.stat, ACT.Sqrt).then_inc(sem_std, 1)


def phase_flags(nc, m, d):
    with ExitStack() as ctx:
        s = Scope(nc, ctx, "fl")
        raw = s.sb("raw", [ROWP, 3, ROWE], I32)
        flags = s.sb("flags", [ROWP, KINDS, ROWE], BF16)
        loaded, made, chain, src_in, flags_ready, stored = (s.sem(n) for n in ("loaded", "made", "chain", "src_in", "flags_ready", "stored"))
        block = ctx.enter_context(nc.Block())

        @block.sync
        def _(sp):
            for i in range(3):
                sp.dma_start(raw[:, i, :], d["dst_rows"][i:i + ROWS].rearrange("(p e) -> p e", p=ROWP)).then_inc(loaded, 16)
            sp.dma_start(m.src[:, :], d["src_cols"]).then_inc(src_in, 16)
            for kind in range(KINDS):
                sp.wait_ge(flags_ready, kind + 1)
                sp.dma_start(d["flags"][kind, :].rearrange("(p e) -> p e", p=ROWP), flags[:, kind, :]).then_inc(stored, 16)
            sp.wait_ge(src_in, 16)
            sp.wait_ge(stored, 16 * KINDS)

        @block.gpsimd
        def _(pool):
            nc.gpsimd.iota(m.iota[:, :], pattern=[[1, P]], base=0, channel_multiplier=0,
                           allow_small_or_imprecise_dtypes=True).then_inc(made, 1)
            nc.gpsimd.iota(m.lane[:, :], pattern=[[0, 1]], base=0, channel_multiplier=1,
                           allow_small_or_imprecise_dtypes=True).then_inc(made, 1)
            nc.gpsimd.iota(m.node_no[:, :], pattern=[[1, NB + 1]], base=0, channel_multiplier=NB,
                           allow_small_or_imprecise_dtypes=True).then_inc(made, 1)

        @block.vector
        def _(dve):
            link = linker(dve, chain)
            dve.wait_ge(made, 3)
            link(nc.vector.tensor_scalar(m.ident[:, :], m.iota[:, :], m.lane[:, :], None, ALU.is_equal))
            dve.wait_ge(loaded, 48)
            before, dst, behind = (raw[:, i, :] for i in range(3))
            keep, reset, end = (flags[:, kind, :] for kind in range(KINDS))
            nc.vector.tensor_tensor(keep, before, dst, ALU.is_equal).then_inc(flags_ready, 1)
            link(nc.vector.tensor_tensor(end, behind, dst, ALU.is_equal))
            dve.wait_ge(flags_ready, 1)
            nc.vector.tensor_scalar(reset, keep, 1.0, BIG, ALU.subtract, ALU.mult).then_inc(flags_ready, 1)
            nc.vector.tensor_scalar(end, end, 1.0, BIG, ALU.subtract, ALU.mult).then_inc(flags_ready, 1)


def load_features(nc, sp, m, d, sem):
    sp.dma_start(m.x[0:LASTP, :, :], d["x"][0:LASTP * NB, :].rearrange("(p b) w -> p b w", b=NB)).then_inc(sem, 16)
    sp.dma_start(m.x[LASTP:LASTP + 1, 0:LASTB, :], d["x"][LASTP * NB:N, :].rearrange("(p b) w -> p b w", b=LASTB)).then_inc(sem, 16)


def phase_table(nc, m, d, edge):
    with ExitStack() as ctx:
        s = Scope(nc, ctx, "tb")
        t = norm_of(s)
        lin_w = s.sb("lin_w", [D, HEADS * D])
        att = s.sb("att", [D, 2, HEADS * D])
        prod = s.sb("prod", [D, HEADS * D])
        folded = s.sb("folded", [D, 2 * HEADS])
        edge_w = s.sb("edge_w", [P, EDIM, HEADS * D])
        att_e = s.sb("att_e", [P, HEADS * D])
        v = s.sb("v", [P, EDIM * HEADS])
        attr = s.sb("attr", [P, TILES * EDIM])
        h_t = s.sb("h_t", [D, 2, P])
        table = s.sb("table", [P, NB, TW])
        ps_t = s.ps("ps_t", [D, 2, 512])
        ps_a = s.ps("ps_a", [P, 512])
        loaded, weights_in, attr_in, chain = (s.sem(n) for n in ("loaded", "weights_in", "attr_in", "chain"))
        var, std, h_ready, folded_ready = (s.sem(n) for n in ("var", "std", "h_ready", "folded_ready"))
        transposed, taken, logits_ready, table_ready, stored = (s.sem(n) for n in ("transposed", "taken", "logits_ready", "table_ready", "stored"))
        cleared = s.sem("cleared")
        firsts = s.sb("firsts", [P, GROUPS], I32)
        tiles = s.sb("tiles", [P, NB + 1, GROUP], I32)
        edges = s.sb("edges", [P, NB + 1, P], I32)
        less = s.sb("less", [P, NB + 1, P])
        count, group = s.sb("count", [P, NB + 1]), s.sb("group", [P, NB + 1])
        begin, degree, none, pos = s.sb("begin", [P, NB + 1]), s.sb("degree", [P, NB]), s.sb("none", [P, NB]), s.sb("pos", [P, NB])
        zeros = s.sb("zeros", [P, ROWT * ROWP])
        where = s.sb("where", [P, 2, NB + 1], I32)
        whole, tile, lane_of, part = (s.sb(n, [P, NB], I32) for n in ("whole", "tile", "lane_of", "part"))
        cross_i, cross, shared16, shared = s.sb("cross_i", [P, 1], I32), s.sb("cross", [P, 1]), s.sb("shared16", [P, 1], BF16), s.sb("shared", [P, 1])
        bounds_in, where_ready, found, starts_ready, starts_out, first_in, zero_made, zeroed = (s.sem(n) for n in ("bounds_in", "where_ready", "found", "starts_ready", "starts_out", "first_in", "zero_made", "zeroed"))
        block = ctx.enter_context(nc.Block())

        @block.sync
        def _(sp):
            sp.dma_start(firsts[:, :], d["group_first"].unsqueeze(0).broadcast_to([P, GROUPS])).then_inc(bounds_in, 16)
            sp.dma_start(cross_i[:, :], d["dst_rows"][1 + HALF * P:2 + HALF * P].unsqueeze(0).broadcast_to([P, 1])).then_inc(bounds_in, 16)
            sp.dma_start(shared16[:, :], d["flags"][KEEP, HALF * P:HALF * P + 1].unsqueeze(0).broadcast_to([P, 1])).then_inc(bounds_in, 16)
            sp.wait_ge(cleared, 1)
            load_features(nc, sp, m, d, loaded)
            sp.dma_start(lin_w[:, :], d["lin_w"]).then_inc(weights_in, 16)
            sp.dma_start(att[:, 0, :], d["att_src"].rearrange("h c -> (h c)").unsqueeze(0).broadcast_to([D, HEADS * D])).then_inc(weights_in, 16)
            sp.dma_start(att[:, 1, :], d["att_dst"].rearrange("h c -> (h c)").unsqueeze(0).broadcast_to([D, HEADS * D])).then_inc(weights_in, 16)
            sp.dma_start(edge_w[:, :, :].rearrange("p a b -> p (a b)"), d["lin_edge_w"].rearrange("h c -> (h c)").unsqueeze(0).broadcast_to([P, EDIM * HEADS * D])).then_inc(weights_in, 16)
            sp.dma_start(att_e[:, :], d["att_edge"].rearrange("h c -> (h c)").unsqueeze(0).broadcast_to([P, HEADS * D])).then_inc(weights_in, 16)
            sp.dma_start(attr[:, :], d["attr_cols"]).then_inc(attr_in, 16)
            sp.wait_ge(table_ready, 1)
            sp.dma_start(d["table0"].rearrange("(p b) w -> p b w", b=NB), table[:, :, :]).then_inc(stored, 16)
            sp.wait_ge(stored, 16)
            sp.wait_ge(starts_ready, 1)
            sp.dma_start(d["start_of"].rearrange("(p b) o -> p (b o)", b=NB), m.start_row[:, :]).then_inc(starts_out, 16)
            sp.wait_ge(starts_out, 16)
            sp.wait_ge(bounds_in, 48)
            sp.nop(nofuse=True)
            node_at = nc.sync.value_load(cross_i[0:1, 0:1], min_val=0, max_val=NPAD - 1)
            sp.dma_start(m.first[:, :], d["start_of"][bass.ds(node_at, 1), :]).then_inc(first_in, 16)
            sp.wait_ge(first_in, 16)

        @block.gpsimd
        def _(pool):
            for level, (table, out) in enumerate(((d["tile_first"], tiles), (d["dst_tiles"], edges))):
                pool.wait_ge(where_ready, level + 1)
                for b in range(NB + 1):
                    pool.indirect_dma_start(out[:, b, :], None, table, bass.IndirectOffsetOnAxis(where[:, level, b:b + 1], 0)).then_inc(found, 16)

        @block.scalar
        def _(act):
            act.wait_ge(zero_made, 1)
            width = ROWT * ROWP
            for table, first, n in ((d["sums"], ROWS, NPAD * D // P), (d["sums_heads"], ROWS, NPAD * SW // P), (d["filled4"], 0, ROWS * AW // P)):
                flat = table[first:first + n * P // table.shape[1], :].rearrange("(p r) w -> p (r w)", p=P)
                for o in range(0, n, width):
                    act.dma_start(flat[:, o:min(o + width, n)], zeros[:, 0:min(width, n - o)]).then_inc(zeroed, 16)
            root(nc, act, t, var, std, 1)
            for b in range(NB):
                act.wait_ge(transposed, b + 1)
                if b >= 2:
                    act.wait_ge(logits_ready, b - 1)
                nc.scalar.copy(h_t[:, b % 2, :], ps_t[:, b % 2, 0:P]).then_inc(taken, 1)
            act.wait_ge(zeroed, 16 * (-(-NPAD * D // P // width) - (-NPAD * SW // P // width) - (-ROWS * AW // P // width)))

        @block.tensor
        def _(pe):
            pe.wait_ge(h_ready, 1)
            pe.wait_ge(folded_ready, 1)
            for b in range(NB + 1):
                if b < NB:
                    if b >= 2:
                        pe.wait_ge(taken, b - 1)
                    nc.tensor.transpose(ps_t[:, b % 2, 0:P], m.h[:, b, :], m.ident[:, :]).then_inc(transposed, 1)
                if b >= 1:
                    pe.wait_ge(taken, b)
                    nc.tensor.matmul(ps_a[:, (b - 1) * WW:b * WW], h_t[:, (b - 1) % 2, :], folded[:, :],
                                     start=True, stop=True).then_inc(logits_ready, 1)

        @block.vector
        def _(dve):
            link = linker(dve, chain)
            nc.vector.memset(m.x[:, :, :], 0.0).then_inc(cleared, 1)
            nc.vector.memset(zeros[:, :], 0.0).then_inc(zero_made, 1)
            def smaller(values, n):
                link(nc.vector.tensor_tensor(less[:, :, 0:n], values, m.node_no[:, :].unsqueeze(2).broadcast_to([P, NB + 1, n]), ALU.is_lt))
                link(nc.vector.tensor_reduce(out=count[:, :], in_=less[:, :, 0:n], axis=AX.X, op=ALU.add))

            dve.wait_ge(bounds_in, 48)
            smaller(firsts[:, :].unsqueeze(1).broadcast_to([P, NB + 1, GROUPS]), GROUPS)
            link(nc.vector.tensor_scalar(group[:, :], count[:, :], 1.0, 0.0, ALU.subtract, ALU.max))
            nc.vector.tensor_copy(where[:, 0, :], group[:, :]).then_inc(where_ready, 1)
            dve.wait_ge(weights_in, 80)
            for a in range(2):
                link(nc.vector.tensor_tensor(prod[:, :], lin_w[:, :], att[:, a, :], ALU.mult))
                ins = nc.vector.tensor_reduce(out=folded[:, a * HEADS:(a + 1) * HEADS], in_=prod[:, :].rearrange("p (h c) -> p h c", h=HEADS), axis=AX.X, op=ALU.add)
                if a == 0:
                    link(ins)
                else:
                    ins.then_inc(folded_ready, 1)
            link(nc.vector.tensor_tensor(edge_w[:, :, :], edge_w[:, :, :], att_e[:, :].unsqueeze(1).broadcast_to([P, EDIM, HEADS * D]), ALU.mult))
            link(nc.vector.tensor_reduce(out=v[:, :], in_=edge_w[:, :, :].rearrange("p a (h c) -> p (a h) c", h=HEADS), axis=AX.X, op=ALU.add))
            dve.wait_ge(loaded, 32)
            layer_norm(nc, link, dve, m.h[:, :, :], m.x[:, :, :], t, var, std, 1)
            link(nc.vector.tensor_scalar(m.h[:, :, :], m.h[:, :, :], 0.0, None, ALU.max))
            nc.vector.tensor_copy(table[:, :, 0:D], m.h[:, :, :]).then_inc(h_ready, 1)
            dve.wait_ge(attr_in, 16)
            at = attr[:, :].rearrange("p (t c) -> p t c", c=EDIM)
            for hd in range(HEADS):
                link(nc.vector.tensor_scalar(edge.logit[:, :, hd], at[:, :, 0], v[:, hd:hd + 1], None, ALU.mult))
                for c in range(1, EDIM):
                    link(nc.vector.scalar_tensor_tensor(edge.logit[:, :, hd], at[:, :, c], v[:, c * HEADS + hd:c * HEADS + hd + 1],
                                                        edge.logit[:, :, hd], ALU.mult, ALU.add))
                if hd == 1:
                    dve.wait_ge(found, 16 * (NB + 1))
                    smaller(tiles[:, :, :], GROUP)
                    link(nc.vector.tensor_scalar(count[:, :], count[:, :], 1.0, 0.0, ALU.subtract, ALU.max))
                    link(nc.vector.scalar_tensor_tensor(group[:, :], group[:, :], float(GROUP), count[:, :], ALU.mult, ALU.add))
                    nc.vector.tensor_copy(where[:, 1, :], group[:, :]).then_inc(where_ready, 1)
            dve.wait_ge(logits_ready, NB)
            link(nc.vector.tensor_copy(m.logit[:, :, :], ps_a[:, 0:NB * WW].rearrange("p (b w) -> p b w", w=WW)))
            nc.vector.memset(table[:, :, D + HEADS:TW], 0.0)
            nc.vector.tensor_copy(table[:, :, D:D + HEADS], m.logit[:, :, 0:HEADS]).then_inc(table_ready, 1)
            dve.wait_ge(found, 32 * (NB + 1))
            smaller(edges[:, :, :], P)
            link(nc.vector.scalar_tensor_tensor(begin[:, :], group[:, :], float(P), count[:, :], ALU.mult, ALU.add))
            link(nc.vector.tensor_tensor(degree[:, :], begin[:, 1:NB + 1], begin[:, 0:NB], ALU.subtract))
            link(nc.vector.tensor_scalar(none[:, :], degree[:, :], 0.0, None, ALU.is_equal))
            link(nc.vector.tensor_scalar(m.has[:, :], degree[:, :], 0.0, None, ALU.is_gt))
            link(nc.vector.tensor_scalar(m.inv_count[:, :], degree[:, :], 1.0, None, ALU.max))
            link(nc.vector.reciprocal(m.inv_count[:, :], m.inv_count[:, :]))
            node_no = m.node_no[:, 0:NB]
            link(nc.vector.tensor_copy(cross[:, :], cross_i[:, :]))
            link(nc.vector.tensor_copy(shared[:, :], shared16[:, :]))
            link(nc.vector.tensor_scalar(m.join[:, :], node_no, cross[:, :], shared[:, :], ALU.is_equal, ALU.mult))

            def unless_none(out):
                link(nc.vector.scalar_tensor_tensor(whole[:, :], node_no, float(ROWS), pos[:, :], ALU.add, ALU.subtract))
                link(nc.vector.tensor_tensor(whole[:, :], whole[:, :], none[:, :], ALU.mult))
                link(nc.vector.tensor_tensor(out, whole[:, :], pos[:, :], ALU.add))

            def to_row(out):
                link(nc.vector.tensor_copy(whole[:, :], pos[:, :]))
                link(nc.vector.tensor_single_scalar(tile[:, :], whole[:, :], P.bit_length() - 1, ALU.arith_shift_right))
                link(nc.vector.tensor_single_scalar(lane_of[:, :], whole[:, :], P - 1, ALU.bitwise_and))
                link(nc.vector.tensor_scalar(pos[:, :], tile[:, :], float(HALF), None, ALU.is_ge))
                link(nc.vector.scalar_tensor_tensor(tile[:, :], pos[:, :], -float(HALF), tile[:, :], ALU.mult, ALU.add))
                link(nc.vector.tensor_single_scalar(part[:, :], tile[:, :], PER - 1, ALU.bitwise_and))
                link(nc.vector.tensor_single_scalar(tile[:, :], tile[:, :], PER.bit_length() - 1, ALU.arith_shift_right))
                link(nc.vector.scalar_tensor_tensor(pos[:, :], part[:, :], float(STREAMS), pos[:, :], ALU.mult, ALU.add))
                link(nc.vector.scalar_tensor_tensor(pos[:, :], lane_of[:, :], float(U), pos[:, :], ALU.mult, ALU.add))
                link(nc.vector.scalar_tensor_tensor(pos[:, :], tile[:, :], float(U * P), pos[:, :], ALU.mult, ALU.add))
                unless_none(out)

            link(nc.vector.tensor_scalar(pos[:, :], begin[:, 1:NB + 1], 1.0, 0.0, ALU.subtract, ALU.max))
            link(nc.vector.tensor_copy(m.end_pos[:, :], pos[:, :]))
            to_row(m.end_row[:, :])
            link(nc.vector.tensor_copy(pos[:, :], begin[:, 0:NB]))
            unless_none(m.start_pos[:, :])
            to_row(m.start_row[:, :])
            dve.sem_inc(starts_ready, 1)


def phase_dest(nc, m, d, edge):
    with ExitStack() as ctx:
        s = Scope(nc, ctx, "de")
        fill = s.sb("fill", [ROWP, ROWE, AW])
        sums = s.sb("sums", [ROWP, ROWE, AW])
        value = s.sb("value", [P, NB, AW])
        keep = s.sb("keep", [ROWP, ROWE], BF16)
        first_dst = s.sb("first_dst", [ROWP, 2], I32)
        entry = s.sb("entry", [ROWP, AW])
        spread = s.sb("spread", [ROWP, 2, ROWE])
        logit_r = s.sb("logit_r", [ROWP, HEADS, ROWE])
        logit = s.sb("logit", [P, ROWT, ROWP])
        tail, whole = s.sb("tail", [ROWP, HEADS]), s.sb("whole", [ROWP, 1])
        tail_t, whole_t, carry_t = s.sb("tail_t", [HEADS, ROWP]), s.sb("whole_t", [HEADS, ROWP]), s.sb("carry_t", [HEADS, ROWP + 1])
        carry = s.sb("carry", [ROWP, HEADS])
        ps_z = s.ps("ps_z", [ROWP, ROWE])
        ps_w = s.ps("ps_w", [P, ROWT, P])
        value_ready, node_out, scattered, keep_in, loaded, first_in, entry_in = (s.sem(n) for n in ("value_ready", "node_out", "scattered", "keep_in", "loaded", "first_in", "entry_in"))
        logit_ready, logit_t, logit_taken, spread_ready, spread_t, joined = (s.sem(n) for n in ("logit_ready", "logit_t", "logit_taken", "spread_ready", "spread_t", "joined"))
        tail_ready, tail_out, carry_ready, carry_out, sums_ready, stored, gathered, chain = (s.sem(n) for n in ("tail_ready", "tail_out", "carry_ready", "carry_out", "sums_ready", "stored", "gathered", "chain"))
        A = ROWT // PER
        by_row = lambda a, hd: edge.logit[:, :, hd].rearrange("p (k a s i) -> p a i s k", a=A, s=STREAMS, i=PER)[:, a]
        split = lambda t, a: t.rearrange("p (a i) (s k) -> p a i s k", a=A, s=STREAMS)[:, a]
        rows = lambda table: table[0:ROWS, :].rearrange("(p e) w -> p e w", p=ROWP)
        block = ctx.enter_context(nc.Block())

        @block.sync
        def _(sp):
            sp.dma_start(first_dst[:, :], d["dst_rows"][1:1 + ROWS].rearrange("(p e) -> p e", p=ROWP)[:, 0:2]).then_inc(first_in, 16)
            sp.dma_start(keep[:, :], d["flags"][KEEP, :].rearrange("(p e) -> p e", p=ROWP)).then_inc(keep_in, 16)
            sp.wait_ge(value_ready, 1)
            sp.dma_start(d["node4"].rearrange("(p b) w -> p b w", b=NB), value[:, :, :]).then_inc(node_out, 16)
            sp.wait_ge(sums_ready, HEADS)
            sp.dma_start(rows(d["edge_sums"]), sums[:, :, :]).then_inc(stored, 16)
            sp.wait_ge(scattered, 16 * NB)
            sp.dma_start(fill[:, :, :], rows(d["filled4"])).then_inc(loaded, 16)
            sp.wait_ge(loaded, 16)

        @block.gpsimd
        def _(pool):
            pool.wait_ge(value_ready, 1)
            for b in range(NB):
                pool.indirect_dma_start(d["filled4"], bass.IndirectOffsetOnAxis(m.start_pos[:, b:b + 1], 0), value[:, b, :], None).then_inc(scattered, 16)
            pool.wait_ge(first_in, 16)
            pool.wait_ge(node_out, 16)
            pool.indirect_dma_start(entry[:, :], None, d["node4"], bass.IndirectOffsetOnAxis(first_dst[:, 0:1], 0)).then_inc(entry_in, 16)
            pool.wait_ge(stored, 16)
            for b in range(NB):
                pool.indirect_dma_start(m.edge_sum[:, b, :], None, d["edge_sums"], bass.IndirectOffsetOnAxis(m.end_pos[:, b:b + 1], 0)).then_inc(gathered, 16)
            pool.wait_ge(gathered, 16 * NB)

        @block.scalar
        def _(act):
            for hd in range(HEADS):
                if hd >= 1:
                    act.wait_ge(logit_t, hd)
                for a in range(A):
                    nc.scalar.copy(split(logit[:, :, :], a), by_row(a, hd)).then_inc(logit_ready, 1)
                act.wait_ge(logit_t, hd + 1)
                nc.scalar.copy(logit_r[:, hd, :], ps_z[:, :]).then_inc(logit_taken, 1)

        @block.tensor
        def _(pe):
            for hd in range(HEADS):
                pe.wait_ge(logit_ready, (hd + 1) * A)
                if hd >= 1:
                    pe.wait_ge(logit_taken, hd)
                for t in range(ROWT):
                    last = nc.tensor.transpose(ps_z[:, t * P:(t + 1) * P], logit[:, t, :], m.ident[:, :])
                last.then_inc(logit_t, 1)
            pe.wait_ge(tail_ready, 2)
            pe.wait_ge(logit_taken, HEADS)
            nc.tensor.matmul(ps_z[0:HEADS, 0:ROWP], tail[:, :], m.ident[0:ROWP, 0:ROWP], start=True, stop=True)
            nc.tensor.matmul(ps_z[0:HEADS, P:P + ROWP], whole[:, 0:1].broadcast_to([ROWP, HEADS]), m.ident[0:ROWP, 0:ROWP], start=True, stop=True).then_inc(tail_out, 1)
            pe.wait_ge(carry_ready, 1)
            nc.tensor.matmul(ps_z[:, 512:512 + HEADS], carry_t[:, 0:ROWP], m.ident[0:HEADS, 0:HEADS], start=True, stop=True).then_inc(carry_out, 1)
            for hd in range(HEADS):
                pe.wait_ge(spread_ready, hd + 1)
                if hd >= 1:
                    pe.wait_ge(joined, hd * A)
                for t in range(ROWT):
                    last = nc.tensor.transpose(ps_w[:, t, 0:ROWP], spread[:, hd % 2, t * P:(t + 1) * P], m.ident[0:ROWP, 0:ROWP])
                last.then_inc(spread_t, 1)

        @block.vector
        def _(dve):
            link = linker(dve, chain)
            link(nc.vector.memset(value[:, :, :], 0.0))
            nc.vector.tensor_copy(value[:, :, 0:HEADS], m.logit[:, :, HEADS:WW]).then_inc(value_ready, 1)
            link(nc.vector.memset(carry_t[:, 0:1], 0.0))
            dve.wait_ge(keep_in, 16)
            nc.vector.tensor_reduce(out=whole[:, :], in_=keep[:, :], axis=AX.X, op=ALU.min).then_inc(tail_ready, 1)
            for hd in range(HEADS):
                dve.wait_ge(logit_taken, hd + 1)
                link(nc.vector.tensor_tensor_scan(spread[:, 0, :], keep[:, :], logit_r[:, hd, :], 0.0, ALU.mult, ALU.add))
                link(nc.vector.tensor_copy(tail[:, hd:hd + 1], spread[:, 0, ROWE - 1:ROWE]))
            dve.sem_inc(tail_ready, 1)
            dve.wait_ge(tail_out, 1)
            link(nc.vector.tensor_copy(tail_t[:, :], ps_z[0:HEADS, 0:ROWP]))
            link(nc.vector.tensor_copy(whole_t[:, :], ps_z[0:HEADS, P:P + ROWP]))
            nc.vector.tensor_tensor_scan(carry_t[:, 1:ROWP + 1], whole_t[:, :], tail_t[:, :], 0.0, ALU.mult, ALU.add).then_inc(carry_ready, 1)
            dve.wait_ge(carry_out, 1)
            link(nc.vector.tensor_copy(carry[:, :], ps_z[:, 512:512 + HEADS]))
            link(nc.vector.memset(sums[:, :, HEADS], 0.0))
            for hd in range(HEADS):
                nc.vector.tensor_tensor_scan(sums[:, :, hd], keep[:, :], logit_r[:, hd, :], carry[:, hd:hd + 1], ALU.mult, ALU.add).then_inc(sums_ready, 1)
            dve.wait_ge(loaded, 16)
            dve.wait_ge(entry_in, 16)
            for hd in range(HEADS):
                if hd >= 2:
                    dve.wait_ge(spread_t, hd - 1)
                nc.vector.tensor_tensor_scan(spread[:, hd % 2, :], keep[:, :], fill[:, :, hd], entry[:, hd:hd + 1], ALU.mult, ALU.add).then_inc(spread_ready, 1)
                dve.wait_ge(spread_ready, hd + 1)
            for hd in range(HEADS):
                dve.wait_ge(spread_t, hd + 1)
                for a in range(A):
                    nc.vector.tensor_tensor(by_row(a, hd), by_row(a, hd), split(ps_w[:, :, 0:ROWP], a), ALU.add).then_inc(joined, 1)


def phase_gat(nc, m, d, edge):
    with ExitStack() as ctx:
        s = Scope(nc, ctx, "ga")
        SH = STREAMS * HEADS
        rows = s.sb("rows", [P, BUFS, U * TW])
        index = s.sb("index", [P, BUFS, U], I32)
        keep = s.sb("keep", [P, BUFS, PER * P], BF16)
        flags = s.sb("flags", [SH, BUFS, KINDS, PER * P], BF16)
        total = s.sb("total", [P, 2, PER, SH])
        logit = s.sb("logit", [P, BUFS, PER, SH])
        running = s.sb("running", [SH, 2, PER * P])
        top = s.sb("top", [SH, 2, PER * P])
        fall = s.sb("fall", [SH, BUFS, 1])
        factor = s.sb("factor", [SH, BUFS, 1])
        arg = s.sb("arg", [P, 2, PER, SH])
        weight = s.sb("weight", [P, BUFS, PER, SH])
        top_e = s.sb("top_e", [P, BUFS, PER * SH])
        scaled = s.sb("scaled", [P, 2, HEADS, U * D])
        factor_w = s.sb("factor_w", [P, 2, HEADS])
        entry = s.sb("entry", [P, 2, HEADS])
        entry_d = s.sb("entry_d", [SH, 2, 1])
        run = s.sb("run", [P, 2, HEADS, PER * P])
        run_d = s.sb("run_d", [SH, 2, PER * P])
        back = s.sb("back", [P, BUFS, U, SW])
        pick = s.sb("pick", [SH, HEADS, P])
        zeros = s.sb("zeros", [P, U * D])
        ps_z = s.ps("ps_z", [SH, PER * P])
        ps_t = s.ps("ps_t", [P, 512])
        ps_r = s.ps("ps_r", [P, 2, PER * P])
        ps_d = s.ps("ps_d", [SH, PER * P])
        ps_b = s.ps("ps_b", [P, 2, PER * P])
        ps_e = s.ps("ps_e", [P, 512])
        names = ("index_ready", "logit_ready", "logit_t", "running_ready", "top_ready", "fall_ready", "factor_ready", "top_t", "factor_t", "arg_ready", "weight_ready", "top_taken")
        index_ready, logit_ready, logit_t, running_ready, top_ready, fall_ready, factor_ready, top_t, factor_t, arg_ready, weight_ready, top_taken = (s.sem(n) for n in names)
        names = ("scaled_ready", "rows_t", "weight_t", "entry_ready", "run_ready", "run_d_ready", "back_t", "back_d_t", "back_ready", "back_d_ready", "total_ready", "factor_in", "pick_ready", "zeroed", "cleared", "chain")
        scaled_ready, rows_t, weight_t, entry_ready, run_ready, run_d_ready, back_t, back_d_t, back_ready, back_d_ready, total_ready, factor_in, pick_ready, zeroed, cleared, chain = (s.sem(n) for n in names)
        rows_in, keep_in, flags_in, stored = ([s.sem(f"{n}{b}") for b in range(BUFS)] for n in ("rows_in", "keep_in", "flags_in", "stored"))
        last = PER * P - 1

        def items(c, hd, back=0):
            return c * HEADS + (HEADS * BUFS + hd + 1 - back)
        block = ctx.enter_context(nc.Block())

        @block.gpsimd
        def _(pool):
            gather_pass(pool, rows, index, d["table0"], TW, index_ready, rows_in)

        @block.sync
        def _(sp):
            sp.wait_ge(zeroed, 1)

            def step(k, j):
                if now := stage(k, j, 0):
                    c, r, b = now
                    sp.wait_ge(run_d_ready, upto(c, BUFS))
                    sp.nop(nofuse=True)
                    load_flags(sp, keep, d, KEEP, c, b, keep_in)
                    for st in range(STREAMS):
                        sp.dma_start(flags[st * HEADS:(st + 1) * HEADS, b], flags_row(d["flags"], slice(0, KINDS), c, st, HEADS)).then_inc(flags_in[b], 16)
                    sp.dma_start(d["filled"][bass.ds(c * (P * U), P * U), :].rearrange("(p u) w -> p (u w)", u=U), zeros[:, :]).then_inc(cleared, 16)
                if now := stage(k, j, 5):
                    c, r, b = now
                    sp.wait_ge(back_d_ready, upto(c))
                    sp.nop(nofuse=True)
                    sp.dma_start(d["sums_heads"][bass.ds(c * (P * U), P * U), :].rearrange("(p u) w -> p (u w)", u=U),
                                 back[:, b].rearrange("p u w -> p (u w)")).then_inc(stored[b], 16)
            loop_steps(sp, step, 5)
            for b in range(BUFS):
                sp.wait_ge(stored[b], 16 * (LOOPS + 1))
            sp.wait_ge(cleared, 16 * CHUNKS)

        @block.scalar
        def _(act):
            for b in range(BUFS):
                act.sem_inc(stored[b], 16)
            act.sem_inc(factor_ready, BUFS)
            act.sem_inc(weight_ready, BUFS)
            act.sem_inc(back_ready, HEADS * BUFS)
            act.sem_inc(back_d_ready, BUFS)

            def step(k, j):
                if now := stage(k, j, 0):
                    c, r, b = now
                    act.wait_ge(scaled_ready, items(c, HEADS - 1, HEADS * BUFS))
                    nc.scalar.copy(index[:, b, :], m.src[:, bass.ds(c * U, U)]).then_inc(index_ready, 1)
                if now := stage(k, j, 5):
                    c, r, b = now
                    act.wait_ge(stored[b], (r + 1) * 16)
                    for hd in range(HEADS):
                        act.wait_ge(back_t, items(c, hd))
                        nc.scalar.copy(back[:, b, :, hd * D:(hd + 1) * D], ps_b[:, (b * HEADS + hd) % 2, :].rearrange("p (u w) -> p u w", w=D)).then_inc(back_ready, 1)
                    act.wait_ge(top_taken, upto(c))
                    nc.scalar.copy(back[:, b, :, HEADS * D + HEADS:HEADS * D + 2 * HEADS], top_e[:, b, :].rearrange("p (u w) -> p u w", w=HEADS))
                    act.wait_ge(back_d_t, upto(c))
                    nc.scalar.copy(back[:, b, :, HEADS * D:HEADS * D + HEADS], ps_e[:, 0:U * HEADS].rearrange("p (u w) -> p u w", w=HEADS)).then_inc(back_d_ready, 1)
                if now := stage(k, j, 2):
                    c, r, b = now
                    act.wait_ge(fall_ready, upto(c))
                    act.wait_ge(entry_ready, upto(c, BUFS))
                    nc.scalar.activation(factor[:, b, :], fall[:, b, :], ACT.Exp).then_inc(factor_ready, 1)
                if now := stage(k, j, 3):
                    c, r, b = now
                    act.wait_ge(arg_ready, upto(c))
                    act.wait_ge(weight_t, upto(c, BUFS))
                    nc.scalar.activation(weight[:, b, :, :], arg[:, b % 2, :, :], ACT.Exp).then_inc(weight_ready, 1)
            loop_steps(act, step, 5)

        @block.tensor
        def _(pe):
            for sem in (logit_t, top_t, factor_t, weight_t, back_d_t):
                pe.sem_inc(sem, BUFS)
            pe.sem_inc(rows_t, HEADS * BUFS)
            pe.sem_inc(back_t, HEADS * BUFS)
            pe.wait_ge(pick_ready, 1)

            def step(k, j):
                if now := stage(k, j, 4):
                    c, r, b = now
                    for hd in range(HEADS):
                        pe.wait_ge(run_ready, items(c, hd))
                        pe.wait_ge(back_ready, items(c, hd, 2))
                        to_channels(nc, ps_b[:, (b * HEADS + hd) % 2, :], run[:, b % 2, hd, :], m.ident[:, :]).then_inc(back_t, 1)
                    pe.wait_ge(run_d_ready, upto(c))
                    pe.wait_ge(back_d_ready, upto(c, 1))
                    pe.nop(nofuse=True)
                    for i in range(PER):
                        ins = nc.tensor.transpose(ps_e[:, i * SH:(i + 1) * SH], run_d[:, b % 2, i * P:(i + 1) * P], m.ident[0:SH, 0:SH])
                    ins.then_inc(back_d_t, 1)
                if now := stage(k, j, 1):
                    c, r, b = now
                    pe.wait_ge(top_ready, upto(c))
                    pe.wait_ge(top_taken, upto(c, 1))
                    pe.nop(nofuse=True)
                    for i in range(PER):
                        ins = nc.tensor.transpose(ps_t[:, i * SH:(i + 1) * SH], top[:, b % 2, i * P:(i + 1) * P], m.ident[0:SH, 0:SH])
                    ins.then_inc(top_t, 1)
                    pe.wait_ge(factor_ready, upto(c))
                    for hd in range(HEADS):
                        ins = nc.tensor.matmul(ps_t[:, U * HEADS + hd:U * HEADS + hd + 1], pick[:, hd, :], factor[:, b, :], start=True, stop=True)
                    ins.then_inc(factor_t, 1)
                if now := stage(k, j, 0):
                    c, r, b = now
                    pe.wait_ge(logit_ready, upto(c))
                    pe.wait_ge(running_ready, upto(c, 1))
                    for i in range(PER):
                        ins = nc.tensor.transpose(ps_z[:, i * P:(i + 1) * P], logit[:, b, i, :], m.ident[:, :])
                    ins.then_inc(logit_t, 1)
                if now := stage(k, j, 3):
                    c, r, b = now
                    for hd in range(HEADS):
                        pe.wait_ge(scaled_ready, items(c, hd))
                        pe.wait_ge(run_ready, items(c, hd, 2))
                        to_channels(nc, ps_r[:, (b * HEADS + hd) % 2, :], scaled[:, b % 2, hd, :], m.ident[:, :]).then_inc(rows_t, 1)
                    pe.wait_ge(weight_ready, upto(c))
                    pe.wait_ge(run_d_ready, upto(c, 1))
                    for i in range(PER):
                        ins = nc.tensor.transpose(ps_d[:, i * P:(i + 1) * P], weight[:, b, i, :], m.ident[:, :])
                    ins.then_inc(weight_t, 1)
            loop_steps(pe, step, 4)

        @block.vector
        def _(dve):
            link = linker(dve, chain)
            nc.vector.memset(zeros[:, :], 0.0).then_inc(zeroed, 1)
            for hd in range(HEADS):
                for st in range(STREAMS):
                    link(nc.vector.tensor_copy(pick[:, hd, st * D:(st + 1) * D], m.ident[0:SH, st * HEADS + hd:st * HEADS + hd + 1].broadcast_to([SH, D])))
            dve.sem_inc(pick_ready, 1)
            link(nc.vector.memset(back[:, :, :, HEADS * D:SW], 0.0))
            link(nc.vector.memset(running[:, 1, last:last + 1], -BIG))
            link(nc.vector.memset(run[:, 1, :, last:last + 1], 0.0))
            link(nc.vector.memset(run_d[:, 1, last:last + 1], 0.0))
            for sem in (logit_ready, running_ready, top_ready, fall_ready, arg_ready, factor_in, top_taken, entry_ready, run_d_ready):
                dve.sem_inc(sem, BUFS)
            dve.sem_inc(scaled_ready, HEADS * BUFS)
            dve.sem_inc(run_ready, HEADS * BUFS)

            def step(k, j):
                if now := stage(k, j, 3):
                    c, r, b = now
                    dve.wait_ge(weight_ready, upto(c))
                    for hd in range(HEADS):
                        dve.wait_ge(rows_t, items(c, hd, 2 * HEADS))
                        nc.vector.tensor_tensor(scaled[:, b % 2, hd, :].rearrange("p (i s w) -> p i s w", i=PER, s=STREAMS),
                                                rows[:, b, :].rearrange("p (s i w) -> p i s w", s=STREAMS, i=PER)[:, :, :, 0:D],
                                                weight[:, b, :, :].rearrange("p i (s a) -> p i s a", s=STREAMS)[:, :, :, hd].unsqueeze(3).broadcast_to([P, PER, STREAMS, D]),
                                                ALU.mult).then_inc(scaled_ready, 1)
                if now := stage(k, j, 4):
                    c, r, b = now
                    dve.wait_ge(keep_in[b], (r + 1) * (16 * STREAMS))
                    dve.wait_ge(run_ready, items(c, -1))
                    dve.wait_ge(run_d_ready, upto(c, 1))
                    dve.wait_ge(factor_in, upto(c))
                    nc.vector.tensor_tensor(entry[:, b % 2, :], run[:, (b + 1) % 2, :, last], factor_w[:, b % 2, :], ALU.mult)
                    nc.vector.tensor_tensor(entry_d[:, b % 2, :], run_d[:, (b + 1) % 2, last:last + 1], factor[:, b, :], ALU.mult).then_inc(entry_ready, 1)
                    dve.wait_ge(entry_ready, upto(c))
                    for hd in range(HEADS):
                        dve.wait_ge(rows_t, items(c, hd))
                        dve.wait_ge(back_t, items(c, hd, 2 * HEADS))
                        nc.vector.tensor_tensor_scan(run[:, b % 2, hd, :], keep[:, b, :], ps_r[:, (b * HEADS + hd) % 2, :],
                                                     entry[:, b % 2, hd:hd + 1], ALU.mult, ALU.add).then_inc(run_ready, 1)
                    dve.wait_ge(weight_t, upto(c))
                    dve.wait_ge(back_d_t, upto(c, 2))
                    nc.vector.tensor_tensor_scan(run_d[:, b % 2, :], flags[:, b, KEEP, :], ps_d[:, :],
                                                 entry_d[:, b % 2, :], ALU.mult, ALU.add).then_inc(run_d_ready, 1)
                if now := stage(k, j, 1):
                    c, r, b = now
                    dve.wait_ge(logit_t, upto(c))
                    dve.wait_ge(flags_in[b], (r + 1) * (16 * STREAMS))
                    dve.wait_ge(running_ready, upto(c, 1))
                    nc.vector.tensor_tensor_scan(running[:, b % 2, :], flags[:, b, RESET, :], ps_z[:, :],
                                                 running[:, (b + 1) % 2, last:last + 1], ALU.add, ALU.max).then_inc(running_ready, 1)
                    dve.wait_ge(running_ready, upto(c))
                    dve.wait_ge(top_t, upto(c, 2))
                    nc.vector.tensor_tensor_scan(top[:, b % 2, ::-1], flags[:, b, END, ::-1], running[:, b % 2, ::-1],
                                                 -BIG, ALU.add, ALU.max).then_inc(top_ready, 1)
                    dve.wait_ge(top_ready, upto(c))
                    dve.wait_ge(factor_ready, upto(c, BUFS))
                    nc.vector.tensor_scalar(fall[:, b, :], running[:, (b + 1) % 2, last:last + 1], top[:, b % 2, 0:1], 0.0, ALU.subtract, ALU.min).then_inc(fall_ready, 1)
                if now := stage(k, j, 2):
                    c, r, b = now
                    dve.wait_ge(factor_t, upto(c))
                    dve.wait_ge(weight_ready, upto(c, 2))
                    nc.vector.tensor_tensor(arg[:, b % 2, :, :], logit[:, b, :, :], ps_t[:, 0:U * HEADS].rearrange("p (i a) -> p i a", i=PER), ALU.subtract).then_inc(arg_ready, 1)
                    dve.wait_ge(entry_ready, upto(c, 2))
                    nc.vector.tensor_copy(factor_w[:, b % 2, :], ps_t[:, U * HEADS:U * HEADS + HEADS]).then_inc(factor_in, 1)
                    dve.wait_ge(back_d_ready, upto(c, BUFS))
                    nc.vector.tensor_copy(top_e[:, b, :], ps_t[:, 0:U * HEADS]).then_inc(top_taken, 1)
                if now := stage(k, j, 0):
                    c, r, b = now
                    dve.wait_ge(rows_in[b], (r + 1) * (16 * U))
                    dve.wait_ge(logit_t, upto(c, BUFS))
                    dve.wait_ge(arg_ready, upto(c, BUFS))
                    for st in range(STREAMS):
                        ins = nc.vector.tensor_tensor(total[:, b % 2, :, st * HEADS:(st + 1) * HEADS],
                                                      rows[:, b, :].rearrange("p (s i w) -> p s i w", s=STREAMS, i=PER)[:, st, :, D:D + HEADS],
                                                      edge.logit[:, bass.ds(c * U + st * PER, PER), :], ALU.add)
                    ins.then_inc(total_ready, 1)
                    dve.wait_ge(total_ready, c + 1)
                    nc.vector.scalar_tensor_tensor(logit[:, b, :, :], total[:, b % 2, :, :], SLOPE, total[:, b % 2, :, :], ALU.mult, ALU.max).then_inc(logit_ready, 1)
            loop_steps(dve, step, 4)


def phase_gat_out(nc, m, d):
    with ExitStack() as ctx:
        s = Scope(nc, ctx, "go")
        t = norm_of(s)
        sums = s.sb("sums", [P, NB, SW])
        carried = s.sb("carried", [P, SW])
        den = s.sb("den", [P, NB, HEADS])
        mean, own, top = (s.sb(n, [P, NB, HEADS]) for n in ("mean", "own", "top"))
        fall = s.sb("fall", [P, 3, NB, HEADS])
        weighed = s.sb("weighed", [P, NB, HEADS])
        norm = s.sb("norm", [P, NB, HEADS * D])
        y = s.sb("y", [P, NB, D])
        z = s.sb("z", [P, NB, D])
        lin_wt = s.sb("lin_wt", [D, HEADS, D])
        split = s.sb("split", [D, 2, 2 * D])
        w1 = s.sb("w1", [D, HEADS, D])
        w1_01, w1_2 = s.sb("w1_01", [P, D]), s.sb("w1_2", [D, D])
        bias_01, bias_2 = s.sb("bias_01", [P, 1]), s.sb("bias_2", [D, 1])
        fold_01, fold_2 = s.sb("fold_01", [P, D]), s.sb("fold_2", [D, D])
        w2 = s.sb("w2", [D, D])
        vec = s.sb("vec", [P, 6, D])
        bias = s.sb("bias", [P, D])
        left = s.sb("left", [P, 2, P])
        right = s.sb("right", [D, 2, P])
        ps_w = s.ps("ps_w", [P, 3, D])
        ps_l, ps_r = s.ps("ps_l", [P, 2, 512]), s.ps("ps_r", [D, 2, 512])
        ps_y = s.ps("ps_y", [P, 2, 512])
        gathered = [s.sem(f"gathered{g}") for g in range(len(HALVES))]
        loaded, padded, folded, fold_taken = (s.sem(n) for n in ("loaded", "padded", "folded", "fold_taken"))
        apart = s.sb("apart", [P, NB])
        fall_ready, factor_ready = s.sem("fall_ready"), s.sem("factor_ready")
        sums_ready, block_t, block_taken, done, drained = (s.sem(n) for n in ("sums_ready", "block_t", "block_taken", "done", "drained"))
        var, std, chain, y_ready = (s.sem(n) for n in ("var", "std", "chain", "y_ready"))
        sums_h = sums[:, :, 0:HEADS * D].rearrange("p b (h w) -> p b h w", h=HEADS)
        starts = {lo: g + 1 for g, (lo, hi) in enumerate(HALVES)}
        block = ctx.enter_context(nc.Block())

        @block.gpsimd
        def _(pool):
            for (lo, hi), sem in zip(HALVES, gathered):
                for b in range(lo, hi):
                    pool.indirect_dma_start(sums[:, b, :], None, d["sums_heads"], bass.IndirectOffsetOnAxis(m.end_row[:, b:b + 1], 0)).then_inc(sem, 16)

        @block.sync
        def _(sp):
            sp.dma_start(lin_wt[:, :, :], d["lin_wt"].rearrange("(h c) i -> c h i", h=HEADS)).then_inc(loaded, 16)
            sp.dma_start(w1[:, :, :], d["w1"].rearrange("(h c) i -> c h i", h=HEADS)).then_inc(loaded, 16)
            sp.dma_start(w1_01[:, :], d["w1"][0:P, :]).then_inc(loaded, 16)
            sp.dma_start(w1_2[:, :], d["w1"][P:HEADS * D, :]).then_inc(loaded, 16)
            sp.dma_start(bias_01[:, :], d["gat_bias"][0:P].unsqueeze(1)).then_inc(loaded, 16)
            sp.dma_start(bias_2[:, :], d["gat_bias"][P:HEADS * D].unsqueeze(1)).then_inc(loaded, 16)
            sp.dma_start(w2[:, :], d["w2"]).then_inc(loaded, 16)
            sp.dma_start(carried[:, :], d["sums_heads"][ENDROW:ENDROW + 1, :].broadcast_to([P, SW])).then_inc(loaded, 16)
            for i, v in enumerate((d["b1"], d["ln1_g"], d["ln1_b"], d["b2"], d["ln2_g"], d["ln2_b"])):
                sp.dma_start(vec[:, i, :], v.unsqueeze(0).broadcast_to([P, D])).then_inc(loaded, 16)
            sp.wait_ge(loaded, 16 * 14)

        @block.tensor
        def _(pe):
            pe.wait_ge(loaded, 16 * 14)
            pe.wait_ge(padded, 1)
            nc.tensor.matmul(ps_w[:, 0, :], split[:, 0, :], w1[:, 0, :], start=True, stop=False)
            nc.tensor.matmul(ps_w[:, 0, :], split[:, 1, :], w1[:, 1, :], start=False, stop=True)
            nc.tensor.matmul(ps_w[0:D, 1, :], lin_wt[:, 2, :], w1[:, 2, :], start=True, stop=True)
            nc.tensor.matmul(ps_w[:, 2, :], bias_01[:, 0:1].broadcast_to([P, P]), w1_01[:, :], start=True, stop=False)
            nc.tensor.matmul(ps_w[:, 2, :], bias_2[:, 0:1].broadcast_to([D, P]), w1_2[:, :], start=False, stop=True).then_inc(folded, 1)
            pe.wait_ge(fold_taken, 2)
            for b in range(NB + 1):
                if b < NB:
                    if b in starts:
                        pe.wait_ge(sums_ready, starts[b])
                    if b >= 2:
                        pe.wait_ge(block_taken, 2 * (b - 1))
                    nc.tensor.transpose(ps_l[:, b % 2, 0:P], norm[:, b, 0:2 * D], m.ident[:, :])
                    nc.tensor.transpose(ps_r[:, b % 2, 0:P], norm[:, b, 2 * D:HEADS * D], m.ident[:, :]).then_inc(block_t, 1)
                if b >= 1:
                    q = b - 1
                    pe.wait_ge(block_taken, 2 * b)
                    if q >= 16 and q % 8 == 0:
                        pe.wait_ge(drained, q // 8 - 1)
                    o = ps_y[:, q // 8 % 2, q % 8 * D:(q % 8 + 1) * D]
                    nc.tensor.matmul(o, left[:, q % 2, :], fold_01[:, :], start=True, stop=False)
                    nc.tensor.matmul(o, right[:, q % 2, :], fold_2[:, :], start=False, stop=True).then_inc(done, 1)
            for b in range(NB + 1):
                if b < NB:
                    if b in starts:
                        pe.wait_ge(y_ready, starts[b])
                    pe.wait_ge(block_taken, 2 * NB + max(b - 1, 0))
                    nc.tensor.transpose(ps_r[:, b % 2, 0:P], y[:, b, :], m.ident[:, :]).then_inc(block_t, 1)
                if b >= 1:
                    q = b - 1
                    pe.wait_ge(block_taken, 2 * NB + b)
                    g = q // 8
                    if q % 8 == 0:
                        pe.wait_ge(drained, 7 + max(g - 1, 0))
                    nc.tensor.matmul(ps_y[:, g % 2, q % 8 * D:(q % 8 + 1) * D], right[:, q % 2, :], w2[:, :], start=True, stop=True).then_inc(done, 1)

        @block.scalar
        def _(act):
            for g, (lo, hi) in enumerate(HALVES):
                act.wait_ge(fall_ready, g + 1)
                nc.scalar.activation(fall[:, :, lo:hi, :], fall[:, :, lo:hi, :], ACT.Exp).then_inc(factor_ready, 1)
            for b in range(NB):
                act.wait_ge(block_t, b + 1)
                if b >= 2:
                    act.wait_ge(done, b - 1)
                nc.scalar.copy(left[:, b % 2, :], ps_l[:, b % 2, 0:P]).then_inc(block_taken, 1)
                nc.scalar.copy(right[:, b % 2, :], ps_r[:, b % 2, 0:P]).then_inc(block_taken, 1)
            for g, (lo, hi) in enumerate(HALVES):
                root(nc, act, t.some(lo, hi), var, std, g + 1)
            for b in range(NB):
                act.wait_ge(block_t, NB + b + 1)
                act.wait_ge(done, NB + max(b - 1, 0))
                nc.scalar.copy(right[:, b % 2, :], ps_r[:, b % 2, 0:P]).then_inc(block_taken, 1)
            root(nc, act, t, var, std, 3)
            root(nc, act, t, var, std, 4)

        @block.vector
        def _(dve):
            link = linker(dve, chain)
            link(nc.vector.memset(split[:, :, :], 0.0))
            dve.wait_ge(loaded, 16 * 14)
            link(nc.vector.tensor_copy(split[:, 0, 0:D], lin_wt[:, 0, :]))
            nc.vector.tensor_copy(split[:, 1, D:2 * D], lin_wt[:, 1, :]).then_inc(padded, 1)
            dve.wait_ge(folded, 1)
            nc.vector.tensor_copy(fold_01[:, :], ps_w[:, 0, :]).then_inc(fold_taken, 1)
            nc.vector.tensor_copy(fold_2[:, :], ps_w[0:D, 1, :]).then_inc(fold_taken, 1)
            link(nc.vector.tensor_tensor(bias[:, :], vec[:, 0, :], ps_w[:, 2, :], ALU.add))
            for g, (lo, hi) in enumerate(HALVES):
                n = hi - lo
                of = lambda v: v[:, lo:hi]
                first = lambda o, w: carried[:, o:o + w].unsqueeze(1).broadcast_to([P, n, w])
                falls = [fall[:, part, lo:hi, :] for part in range(3)]
                link(nc.vector.tensor_tensor(of(mean), m.edge_sum[:, lo:hi, 0:HEADS], bcast(of(m.inv_count), HEADS), ALU.mult))
                link(nc.vector.tensor_tensor(of(mean), of(mean), bcast(of(m.has), HEADS), ALU.mult))
                link(nc.vector.tensor_tensor(of(own), m.logit[:, lo:hi, 0:HEADS], of(mean), ALU.add))
                link(nc.vector.tensor_tensor(of(own), of(own), m.logit[:, lo:hi, HEADS:WW], ALU.add))
                link(nc.vector.scalar_tensor_tensor(falls[2], of(own), SLOPE, of(own), ALU.mult, ALU.max))
                link(nc.vector.tensor_scalar(of(apart), of(m.join), 1.0, BIG, ALU.subtract, ALU.mult))
                link(nc.vector.tensor_tensor(falls[0], bcast(of(apart), HEADS), first(HEADS * D + HEADS, HEADS), ALU.add))
                link(nc.vector.tensor_scalar(of(apart), of(m.has), 1.0, BIG, ALU.subtract, ALU.mult))
                dve.wait_ge(gathered[g], 16 * n)
                link(nc.vector.tensor_tensor(falls[1], bcast(of(apart), HEADS), sums[:, lo:hi, HEADS * D + HEADS:HEADS * D + 2 * HEADS], ALU.add))
                link(nc.vector.tensor_tensor(of(top), falls[0], falls[1], ALU.max))
                link(nc.vector.tensor_tensor(of(top), of(top), falls[2], ALU.max))
                for part in range(3):
                    link(nc.vector.tensor_tensor(falls[part], falls[part], of(top), ALU.subtract))
                dve.sem_inc(fall_ready, 1)
                dve.wait_ge(factor_ready, g + 1)
                link(nc.vector.tensor_tensor(of(den), falls[0], first(HEADS * D, HEADS), ALU.mult))
                link(nc.vector.tensor_tensor(of(weighed), falls[1], sums[:, lo:hi, HEADS * D:HEADS * D + HEADS], ALU.mult))
                link(nc.vector.tensor_tensor(of(den), of(den), of(weighed), ALU.add))
                link(nc.vector.tensor_tensor(of(den), of(den), falls[2], ALU.add))
                link(nc.vector.reciprocal(of(den), of(den)))
                for part in range(3):
                    link(nc.vector.tensor_tensor(falls[part], falls[part], of(den), ALU.mult))
                for hd in range(HEADS):
                    part, share = sums_h[:, lo:hi, hd, :], z[:, lo:hi, :]
                    link(nc.vector.tensor_tensor(part, part, bcast(falls[1][:, :, hd], D), ALU.mult))
                    link(nc.vector.tensor_tensor(share, bcast(falls[0][:, :, hd], D), first(hd * D, D), ALU.mult))
                    link(nc.vector.tensor_tensor(part, part, share, ALU.add))
                    link(nc.vector.tensor_tensor(share, m.h[:, lo:hi, :], bcast(falls[2][:, :, hd], D), ALU.mult))
                    link(nc.vector.tensor_tensor(norm[:, lo:hi, hd * D:(hd + 1) * D], part, share, ALU.add))
                dve.sem_inc(sums_ready, 1)
            wide = lambda i, n=NB: (vec[:, i, :] if isinstance(i, int) else i).unsqueeze(1).broadcast_to([P, n, D])

            def drain(first, add):
                for g in range(7):
                    lo, hi = g * 8, min(g * 8 + 8, NB)
                    dve.wait_ge(done, first + hi)
                    nc.vector.tensor_tensor(z[:, lo:hi, :], ps_y[:, g % 2, 0:(hi - lo) * D].rearrange("p (b w) -> p b w", w=D),
                                            wide(add, hi - lo), ALU.add).then_inc(drained, 1)

            drain(0, bias[:, :])
            dve.wait_ge(drained, 7)
            for g, (lo, hi) in enumerate(HALVES):
                of = lambda v: v[:, lo:hi, :]
                link(nc.vector.tensor_tensor(of(z), of(z), of(m.h), ALU.add))
                layer_norm(nc, link, dve, of(y), of(z), t.some(lo, hi), var, std, g + 1)
                link(nc.vector.tensor_tensor(of(y), of(y), wide(1, hi - lo), ALU.mult))
                link(nc.vector.tensor_tensor(of(y), of(y), wide(2, hi - lo), ALU.add))
                dve.sem_inc(y_ready, 1)
            drain(NB, 3)
            dve.wait_ge(drained, 14)
            link(nc.vector.tensor_tensor(z[:, :, :], z[:, :, :], y[:, :, :], ALU.add))
            layer_norm(nc, link, dve, y[:, :, :], z[:, :, :], t, var, std, 3)
            link(nc.vector.tensor_tensor(y[:, :, :], y[:, :, :], wide(4), ALU.mult))
            link(nc.vector.tensor_tensor(y[:, :, :], y[:, :, :], wide(5), ALU.add))
            link(nc.vector.tensor_tensor(m.x[:, :, :], m.x[:, :, :], y[:, :, :], ALU.add))
            layer_norm(nc, link, dve, m.h[:, :, :], m.x[:, :, :], t, var, std, 4)
            link(nc.vector.tensor_scalar(m.h[:, :, :], m.h[:, :, :], 0.0, None, ALU.max))


def gather_sums(pool, m, d, node, gathered, sets):
    for (lo, hi), sem in zip(sets, gathered):
        for b in range(lo, hi):
            pool.indirect_dma_start(node[:, b, :], None, d["sums"], bass.IndirectOffsetOnAxis(m.end_row[:, b:b + 1], 0)).then_inc(sem, 16)


def scatter_starts(pool, m, d, rows, scattered, ready, sets):
    for g, (lo, hi) in enumerate(sets):
        pool.wait_ge(ready, g + 1)
        for b in range(lo, hi):
            pool.indirect_dma_start(d["filled"], bass.IndirectOffsetOnAxis(m.start_row[:, b:b + 1], 0), rows[:, b, :], None).then_inc(scattered, 16)


def repeat_start(nc, sp, m, d, scattered, border_out):
    sp.wait_ge(scattered, 16 * NB)
    sp.nop(nofuse=True)
    row = nc.sync.value_load(m.first[0:1, 0:1], min_val=0, max_val=ROWS - 1)
    sp.dma_start(d["filled"][BORDER:BORDER + 1, :], d["filled"][bass.ds(row, 1), :]).then_inc(border_out, 16)
    sp.wait_ge(border_out, 16)


def load_flags(sp, flags, d, kinds, c, b, flags_in):
    for st in range(STREAMS):
        sp.dma_start(flags[st * D:(st + 1) * D, b], flags_row(d["flags"], kinds, c, st, D)).then_inc(flags_in[b], 16)


def to_channels(nc, out, rows, ident):
    for i in range(PER):
        last = nc.tensor.transpose(out[:, i * P:(i + 1) * P], rows[:, i * P:(i + 1) * P], ident)
    return last


def slot(u):
    return u % PER * STREAMS + u // PER


def gather_rows(pool, rows, index, table, index_ready, rows_in, layer=0):
    def step(k, j):
        c, k, b = stage(k, j, 0)
        pool.wait_ge(index_ready, layer * CHUNKS + c + 1)
        pool.nop(nofuse=True)
        for u in range(U):
            pool.indirect_dma_start(rows[:, b, slot(u) * D:(slot(u) + 1) * D], None, table,
                                    bass.IndirectOffsetOnAxis(index[:, b, u:u + 1], 0)).then_inc(rows_in[b], 16)
    loop_steps(pool, step, 0)


def phase_light(nc, m, d):
    with ExitStack() as ctx:
        s = Scope(nc, ctx, "li")
        rows = s.sb("rows", [P, BUFS, U * D])
        index = s.sb("index", [P, BUFS, U], I32)
        keep = s.sb("keep", [P, BUFS, PER * P], BF16)
        run = s.sb("run", [P, 2, PER * P])
        back = s.sb("back", [P, BUFS, U * D])
        node = s.sb("node", [P, NB, D])
        wide = s.sb("wide", [P, NB, D])
        carried = s.sb("carried", [P, D])
        ps_r = s.ps("ps_r", [P, 2, PER * P])
        ps_b = s.ps("ps_b", [P, 2, PER * P])
        index_ready, rows_t, run_ready, back_t, back_ready = (s.sem(n) for n in ("index_ready", "rows_t", "run_ready", "back_t", "back_ready"))
        rows_in, keep_in, stored = ([s.sem(f"{n}{b}") for b in range(BUFS)] for n in ("rows_in", "keep_in", "stored"))
        table_out, all_out, carried_in, mean_ready, chain = (s.sem(n) for n in ("table_out", "all_out", "carried_in", "mean_ready", "chain"))
        gathered = [s.sem(f"gathered{g}") for g in range(len(SETS))]
        block = ctx.enter_context(nc.Block())

        @block.gpsimd
        def _(pool):
            with pool.Fori(0, LAYERS) as n:
                pool.wait_ge(table_out, n * (16 * len(SETS)) + 16)
                gather_rows(pool, rows, index, d["table"], index_ready, rows_in, n)
                pool.wait_ge(all_out, n + 1)
                pool.nop(nofuse=True)
                gather_sums(pool, m, d, node, gathered, SETS)

        @block.sync
        def _(sp):
            sp.dma_start(d["table"].rearrange("(p b) w -> p b w", b=NB), m.h[:, :, :]).then_inc(table_out, 16)
            with sp.Fori(0, LAYERS) as n:
                def step(k, j):
                    if now := stage(k, j, 0):
                        c, r, b = now
                        sp.wait_ge(run_ready, upto(c, BUFS, n))
                        sp.nop(nofuse=True)
                        load_flags(sp, keep, d, 0, c, b, keep_in)
                    if now := stage(k, j, 3):
                        c, r, b = now
                        sp.wait_ge(back_ready, upto(c, 0, n))
                        sp.nop(nofuse=True)
                        sp.dma_start(d["sums"][bass.ds(c * (P * U), P * U), :].rearrange("(p u) w -> p (u w)", u=U), back[:, b, :]).then_inc(stored[b], 16)
                loop_steps(sp, step, 3)
                for b in range(BUFS):
                    sp.wait_ge(stored[b], n * (16 * LOOPS) + 16 * (LOOPS + 1))
                sp.nop(nofuse=True)
                sp.sem_inc(all_out, 1)
                sp.dma_start(carried[:, :], d["sums"][ENDROW:ENDROW + 1, :].broadcast_to([P, D])).then_inc(carried_in, 16)
                for g, (lo, hi) in enumerate(SETS):
                    sp.wait_ge(mean_ready, n * len(SETS) + (g + 1))
                    sp.nop(nofuse=True)
                    sp.dma_start(d["table"].rearrange("(p b) w -> p b w", b=NB)[:, lo:hi, :], node[:, lo:hi, :]).then_inc(table_out, 16)
            sp.wait_ge(table_out, 16 * (LAYERS * len(SETS) + 1))

        @block.scalar
        def _(act):
            act.sem_inc(back_ready, BUFS)
            for b in range(BUFS):
                act.sem_inc(stored[b], 16)
            with act.Fori(0, LAYERS) as n:
                def step(k, j):
                    if now := stage(k, j, 0):
                        c, r, b = now
                        act.wait_ge(rows_t, upto(c, BUFS, n))
                        nc.scalar.copy(index[:, b, :], m.src[:, bass.ds(c * U, U)]).then_inc(index_ready, 1)
                    if now := stage(k, j, 2):
                        c, r, b = now
                        act.wait_ge(back_t, upto(c, 0, n))
                        act.wait_ge(stored[b], n * (16 * LOOPS) + (r + 1) * 16)
                        nc.scalar.copy(back[:, b, :], ps_b[:, b % 2, :]).then_inc(back_ready, 1)
                loop_steps(act, step, 2)

        @block.tensor
        def _(pe):
            pe.sem_inc(rows_t, BUFS)
            pe.sem_inc(back_t, BUFS)
            with pe.Fori(0, LAYERS) as n:
                def step(k, j):
                    if now := stage(k, j, 0):
                        c, r, b = now
                        pe.wait_ge(rows_in[b], n * (16 * U * LOOPS) + (r + 1) * (16 * U))
                        pe.wait_ge(run_ready, upto(c, 2, n))
                        to_channels(nc, ps_r[:, b % 2, :], rows[:, b, :], m.ident[:, :]).then_inc(rows_t, 1)
                    if now := stage(k, j, 1):
                        c, r, b = now
                        pe.wait_ge(run_ready, upto(c, 0, n))
                        pe.wait_ge(back_ready, upto(c, 2, n))
                        to_channels(nc, ps_b[:, b % 2, :], run[:, b % 2, :], m.ident[:, :]).then_inc(back_t, 1)
                loop_steps(pe, step, 1)

        @block.vector
        def _(dve):
            dve.sem_inc(run_ready, BUFS)
            with dve.Fori(0, LAYERS) as n:
                nc.vector.memset(run[:, 1, PER * P - 1:PER * P], 0.0).then_inc(chain, 1)
                dve.wait_ge(chain, n * (2 * len(SETS) + 1) + 1)

                def step(k, j):
                    c, r, b = stage(k, j, 0)
                    dve.wait_ge(rows_t, upto(c, 0, n))
                    dve.wait_ge(keep_in[b], n * (16 * STREAMS * LOOPS) + (r + 1) * (16 * STREAMS))
                    dve.wait_ge(back_t, upto(c, 2, n))
                    dve.wait_ge(run_ready, upto(c, 1, n))
                    nc.vector.tensor_tensor_scan(run[:, b % 2, :], keep[:, b, :], ps_r[:, b % 2, :],
                                                 run[:, (b + 1) % 2, PER * P - 1:PER * P], ALU.mult, ALU.add).then_inc(run_ready, 1)
                loop_steps(dve, step, 0)
                dve.wait_ge(carried_in, n * 16 + 16)
                for g, (lo, hi) in enumerate(SETS):
                    dve.wait_ge(gathered[g], n * (16 * (hi - lo)) + 16 * (hi - lo))
                    join_sum(nc, lambda ins, i: (ins.then_inc(chain, 1), dve.wait_ge(chain, n * (2 * len(SETS) + 1) + (2 * g + i + 2))), m, node, carried, wide, lo, hi)
                    nc.vector.tensor_tensor(node[:, lo:hi, :], node[:, lo:hi, :], bcast(m.inv_count[:, lo:hi], D), ALU.mult).then_inc(mean_ready, 1)
            dve.wait_ge(mean_ready, LAYERS * len(SETS))
            nc.vector.tensor_tensor(m.x[:, :, :], m.x[:, :, :], node[:, :, :], ALU.add)


def join_sum(nc, link, m, node, carried, wide, lo, hi):
    link(nc.vector.tensor_tensor(wide[:, lo:hi, :], bcast(m.join[:, lo:hi], D), carried[:, :].unsqueeze(1).broadcast_to([P, hi - lo, D]), ALU.mult), 0)
    link(nc.vector.tensor_tensor(node[:, lo:hi, :], node[:, lo:hi, :], wide[:, lo:hi, :], ALU.add), 1)


def phase_edge_tables(nc, m, d):
    with ExitStack() as ctx:
        s = Scope(nc, ctx, "et")
        t = norm_of(s)
        w = s.sb("w", [D, 2, D])
        b1 = s.sb("b1", [P, D])
        h_t = s.sb("h_t", [D, 2, P])
        at_dst, at_src = s.sb("at_dst", [P, NB, D]), s.sb("at_src", [P, NB, D])
        ps_t = s.ps("ps_t", [D, 2, 512])
        ps_y = s.ps("ps_y", [P, 2, 4, 2, D])
        loaded, var, std, chain, h_ready, w_ready = (s.sem(n) for n in ("loaded", "var", "std", "chain", "h_ready", "w_ready"))
        transposed, taken, done, src_ready, dst_ready, stored, scattered = (s.sem(n) for n in ("transposed", "taken", "done", "src_ready", "dst_ready", "stored", "scattered"))
        border_out = s.sem("border_out")
        G = -(-NB // 4)
        block = ctx.enter_context(nc.Block())

        @block.sync
        def _(sp):
            sp.dma_start(w[:, :, :], d["w1e"].rearrange("(a i) o -> i a o", a=2)).then_inc(loaded, 16)
            sp.dma_start(b1[:, :], d["b1e"].unsqueeze(0).broadcast_to([P, D])).then_inc(loaded, 16)
            sp.wait_ge(src_ready, G)
            sp.dma_start(d["table"].rearrange("(p b) w -> p b w", b=NB), at_src[:, :, :]).then_inc(stored, 16)
            sp.wait_ge(stored, 16)
            sp.wait_ge(loaded, 32)
            repeat_start(nc, sp, m, d, scattered, border_out)

        @block.gpsimd
        def _(pool):
            scatter_starts(pool, m, d, at_dst, scattered, dst_ready, [(lo, min(lo + 4, NB)) for lo in range(0, NB, 4)])

        @block.scalar
        def _(act):
            root(nc, act, t, var, std, 1)
            for b in range(NB):
                act.wait_ge(transposed, b + 1)
                if b >= 2:
                    act.wait_ge(done, b - 1)
                nc.scalar.copy(h_t[:, b % 2, :], ps_t[:, b % 2, 0:P]).then_inc(taken, 1)

        @block.tensor
        def _(pe):
            pe.wait_ge(h_ready, 1)
            pe.wait_ge(w_ready, 1)
            for b in range(NB + 1):
                if b < NB:
                    if b >= 2:
                        pe.wait_ge(taken, b - 1)
                    nc.tensor.transpose(ps_t[:, b % 2, 0:P], m.h[:, b, :], m.ident[:, :]).then_inc(transposed, 1)
                if b >= 1:
                    q = b - 1
                    pe.wait_ge(taken, b)
                    if q >= 8 and q % 4 == 0:
                        pe.wait_ge(src_ready, q // 4 - 1)
                        pe.wait_ge(dst_ready, q // 4 - 1)
                    nc.tensor.matmul(ps_y[:, q // 4 % 2, q % 4, :, :], h_t[:, q % 2, :], w[:, :, :], start=True, stop=True).then_inc(done, 1)

        @block.vector
        def _(dve):
            link = linker(dve, chain)
            dve.wait_ge(loaded, 32)
            nc.vector.tensor_tensor(w[:, 0, :], w[:, 0, :], w[:, 1, :], ALU.subtract).then_inc(w_ready, 1)
            layer_norm(nc, link, dve, m.h[:, :, :], m.x[:, :, :], t, var, std, 1)
            nc.vector.tensor_scalar(m.h[:, :, :], m.h[:, :, :], 0.0, None, ALU.max).then_inc(h_ready, 1)
            for g in range(G):
                lo, hi = g * 4, min(g * 4 + 4, NB)
                dve.wait_ge(done, hi)
                nc.vector.tensor_tensor(at_dst[:, lo:hi, :], ps_y[:, g % 2, 0:hi - lo, 0, :], b1[:, :].unsqueeze(1).broadcast_to([P, hi - lo, D]),
                                        ALU.add).then_inc(dst_ready, 1)
                nc.vector.tensor_copy(at_src[:, lo:hi, :], ps_y[:, g % 2, 0:hi - lo, 1, :]).then_inc(src_ready, 1)


class Pass:

    def __init__(self, s):
        self.rows = s.sb("rows", [P, BUFS, U * D])
        self.index = s.sb("index", [P, BUFS, U], I32)
        self.fill = s.sb("fill", [P, BUFS, U * D])
        self.flags = s.sb("flags", [P, BUFS, 2, PER * P], BF16)
        self.dest = s.sb("dest", [P, 2, PER * P])
        self.run = s.sb("run", [P, 2, PER * P])
        self.back = s.sb("back", [P, BUFS, U * D])
        self.ps_r, self.ps_f, self.ps_m, self.ps_b = (s.ps(n, [P, 2, PER * P]) for n in ("ps_r", "ps_f", "ps_m", "ps_b"))
        self.rows_in, self.fill_in, self.flags_in, self.stored = ([s.sem(f"{n}{b}") for b in range(BUFS)] for n in ("rows_in", "fill_in", "flags_in", "stored"))
        self.index_ready, self.both_t, self.dest_ready, self.run_ready = (s.sem(n) for n in ("index_ready", "both_t", "dest_ready", "run_ready"))
        self.back_t, self.back_ready, self.message = (s.sem(n) for n in ("back_t", "back_ready", "message"))


def pass_sync(sp, d, w):
    def step(k, j):
        if now := stage(k, j, 0):
            c, r, b = now
            sp.wait_ge(w.both_t, upto(c, BUFS))
            sp.nop(nofuse=True)
            sp.dma_start(w.fill[:, b, :], d["filled"][bass.ds(c * (P * U), P * U), :].rearrange("(p u) w -> p (u w)", u=U)).then_inc(w.fill_in[b], 16)
            sp.wait_ge(w.run_ready, upto(c, BUFS))
            sp.nop(nofuse=True)
            load_flags(sp, w.flags, d, slice(0, 2), c, b, w.flags_in)
        if now := stage(k, j, 4):
            c, r, b = now
            sp.wait_ge(w.back_ready, upto(c))
            sp.nop(nofuse=True)
            sp.dma_start(d["sums"][bass.ds(c * (P * U), P * U), :].rearrange("(p u) w -> p (u w)", u=U), w.back[:, b, :]).then_inc(w.stored[b], 16)
    loop_steps(sp, step, 4)
    for b in range(BUFS):
        sp.wait_ge(w.stored[b], 16 * (LOOPS + 1))


def pass_scalar(nc, act, m, w, middle):
    act.sem_inc(w.back_ready, BUFS)
    for b in range(BUFS):
        act.sem_inc(w.stored[b], 16)

    def step(k, j):
        if now := stage(k, j, 0):
            c, r, b = now
            act.wait_ge(w.both_t, upto(c, BUFS))
            nc.scalar.copy(w.index[:, b, :], m.src[:, bass.ds(c * U, U)]).then_inc(w.index_ready, 1)
        if now := stage(k, j, 2):
            middle(*now)
        if now := stage(k, j, 4):
            c, r, b = now
            act.wait_ge(w.back_t, upto(c))
            act.wait_ge(w.stored[b], (r + 1) * 16)
            nc.scalar.copy(w.back[:, b, :], w.ps_b[:, b % 2, :]).then_inc(w.back_ready, 1)
    loop_steps(act, step, 4)


def pass_tensor(nc, pe, m, w, free, middle):
    pe.sem_inc(w.both_t, BUFS)
    pe.sem_inc(w.back_t, BUFS)
    pe.sem_inc(w.message, BUFS)

    def step(k, j):
        if now := stage(k, j, 0):
            c, r, b = now
            pe.wait_ge(w.fill_in[b], (r + 1) * 16)
            free(c)
            to_channels(nc, w.ps_f[:, b % 2, :], w.fill[:, b, :], m.ident[:, :])
            pe.wait_ge(w.rows_in[b], (r + 1) * (16 * U))
            to_channels(nc, w.ps_r[:, b % 2, :], w.rows[:, b, :], m.ident[:, :]).then_inc(w.both_t, 1)
        if now := stage(k, j, 1):
            middle(*now)
        if now := stage(k, j, 2):
            c, r, b = now
            pe.wait_ge(w.run_ready, upto(c))
            pe.wait_ge(w.back_ready, upto(c, 2))
            to_channels(nc, w.ps_b[:, b % 2, :], w.run[:, b % 2, :], m.ident[:, :]).then_inc(w.back_t, 1)
    loop_steps(pe, step, 2)


def spread_dest(nc, dve, w, c, r, b, used):
    dve.wait_ge(w.both_t, upto(c))
    dve.wait_ge(w.flags_in[b], (r + 1) * (16 * STREAMS))
    used(c)
    dve.wait_ge(w.dest_ready, upto(c, 1))
    nc.vector.tensor_tensor_scan(w.dest[:, b % 2, :], w.flags[:, b, 0, :], w.ps_f[:, b % 2, :],
                                 w.dest[:, (b + 1) % 2, PER * P - 1:PER * P], ALU.mult, ALU.add).then_inc(w.dest_ready, 1)
    dve.wait_ge(w.dest_ready, upto(c))


def phase_edge_max(nc, m, d):
    with ExitStack() as ctx:
        s = Scope(nc, ctx, "em")
        w = Pass(s)
        both = s.sb("both", [P, 2, PER * P])
        hidden = s.sb("hidden", [P, 2, PER * P])
        w2 = s.sb("w2", [P, P])
        both_ready, hidden_ready, w_in, w_clear = (s.sem(n) for n in ("both_ready", "hidden_ready", "w_in", "w_clear"))
        block = ctx.enter_context(nc.Block())

        @block.gpsimd
        def _(pool):
            gather_rows(pool, w.rows, w.index, d["table"], w.index_ready, w.rows_in)

        @block.sync
        def _(sp):
            sp.wait_ge(w_clear, 1)
            for st in range(STREAMS):
                sp.dma_start(w2[st * D:(st + 1) * D, st * D:(st + 1) * D], d["w2e"]).then_inc(w_in, 16)
            pass_sync(sp, d, w)

        @block.scalar
        def _(act):
            act.sem_inc(hidden_ready, BUFS)

            def relu(c, r, b):
                act.wait_ge(both_ready, upto(c))
                act.wait_ge(w.message, upto(c, 2))
                nc.scalar.activation(hidden[:, b % 2, :], both[:, b % 2, :], ACT.Relu).then_inc(hidden_ready, 1)
            pass_scalar(nc, act, m, w, relu)

        @block.tensor
        def _(pe):
            pe.wait_ge(w_in, 16 * STREAMS)

            def free(c):
                pe.wait_ge(both_ready, upto(c, 2))

            def messages(c, r, b):
                pe.wait_ge(hidden_ready, upto(c))
                pe.wait_ge(w.run_ready, upto(c, 2))
                nc.tensor.matmul(w.ps_m[:, b % 2, :], w2[:, :], hidden[:, b % 2, :], start=True, stop=True).then_inc(w.message, 1)
            pass_tensor(nc, pe, m, w, free, messages)

        @block.vector
        def _(dve):
            nc.vector.memset(w2[:, :], 0.0).then_inc(w_clear, 1)
            nc.vector.memset(w.dest[:, 1, PER * P - 1:PER * P], 0.0).then_inc(w.dest_ready, BUFS)
            nc.vector.memset(w.run[:, 1, PER * P - 1:PER * P], -BIG).then_inc(w.run_ready, BUFS)
            dve.sem_inc(both_ready, BUFS)

            def used(c):
                dve.wait_ge(both_ready, upto(c, 2))

            def step(k, j):
                if now := stage(k, j, 1):
                    c, r, b = now
                    dve.wait_ge(w.message, upto(c))
                    dve.wait_ge(w.back_t, upto(c, 2))
                    dve.wait_ge(w.run_ready, upto(c, 1))
                    nc.vector.tensor_tensor_scan(w.run[:, b % 2, :], w.flags[:, b, 1, :], w.ps_m[:, b % 2, :],
                                                 w.run[:, (b + 1) % 2, PER * P - 1:PER * P], ALU.add, ALU.max).then_inc(w.run_ready, 1)
                if now := stage(k, j, 0):
                    c, r, b = now
                    spread_dest(nc, dve, w, c, r, b, used)
                    dve.wait_ge(hidden_ready, upto(c, 2))
                    nc.vector.tensor_tensor(both[:, b % 2, :], w.dest[:, b % 2, :], w.ps_r[:, b % 2, :], ALU.add).then_inc(both_ready, 1)
            loop_steps(dve, step, 1)


def phase_edge_out(nc, m, d):
    with ExitStack() as ctx:
        s = Scope(nc, ctx, "eo")
        t = norm_of(s)
        node = s.sb("node", [P, NB, D])
        carried = s.sb("carried", [P, D])
        apart = s.sb("apart", [P, NB])
        b2 = s.sb("b2", [P, D])
        gathered = [s.sem(f"gathered{g}") for g in range(len(HALVES))]
        stored, loaded, border_out = (s.sem(n) for n in ("stored", "loaded", "border_out"))
        chain, var, std, h_ready, scattered = (s.sem(n) for n in ("chain", "var", "std", "h_ready", "scattered"))
        block = ctx.enter_context(nc.Block())

        @block.scalar
        def _(act):
            for g, (lo, hi) in enumerate(HALVES):
                root(nc, act, t.some(lo, hi), var, std, g + 1)

        @block.sync
        def _(sp):
            sp.dma_start(b2[:, :], d["b2e"].unsqueeze(0).broadcast_to([P, D])).then_inc(loaded, 16)
            sp.dma_start(carried[:, :], d["sums"][ENDROW:ENDROW + 1, :].broadcast_to([P, D])).then_inc(loaded, 16)
            sp.wait_ge(h_ready, len(HALVES))
            sp.dma_start(d["table"].rearrange("(p b) w -> p b w", b=NB), m.h[:, :, :]).then_inc(stored, 16)
            sp.wait_ge(stored, 16)
            repeat_start(nc, sp, m, d, scattered, border_out)

        @block.gpsimd
        def _(pool):
            gather_sums(pool, m, d, node, gathered, HALVES)
            scatter_starts(pool, m, d, m.h, scattered, h_ready, HALVES)

        @block.vector
        def _(dve):
            link = linker(dve, chain)
            link(nc.vector.tensor_scalar(apart[:, :], m.join[:, :], 1.0, BIG, ALU.subtract, ALU.mult))
            dve.wait_ge(loaded, 32)
            for g, (lo, hi) in enumerate(HALVES):
                part, maxima, x, h = t.some(lo, hi), node[:, lo:hi, :], m.x[:, lo:hi, :], m.h[:, lo:hi, :]
                wide = lambda v: v.unsqueeze(1).broadcast_to([P, hi - lo, D])
                link(nc.vector.tensor_tensor(part.square, bcast(apart[:, lo:hi], D), wide(carried[:, :]), ALU.add))
                dve.wait_ge(gathered[g], 16 * (hi - lo))
                link(nc.vector.tensor_tensor(maxima, maxima, part.square, ALU.max))
                link(nc.vector.tensor_tensor(maxima, maxima, wide(b2[:, :]), ALU.add))
                link(nc.vector.tensor_tensor(maxima, maxima, bcast(m.has[:, lo:hi], D), ALU.mult))
                link(nc.vector.tensor_tensor(x, x, maxima, ALU.add))
                layer_norm(nc, link, dve, h, x, part, var, std, g + 1)
                nc.vector.tensor_scalar(h, h, 0.0, None, ALU.max).then_inc(h_ready, 1)


def phase_dot(nc, m, d):
    with ExitStack() as ctx:
        s = Scope(nc, ctx, "dt")
        w = Pass(s)
        source = s.sb("source", [P, 2, PER * P])
        prod = s.sb("prod", [P, 2, PER * P])
        scaled = s.sb("scaled", [P, 2, PER * P])
        ones = s.sb("ones", [P, P])
        source_ready, prod_ready, scaled_ready, ones_ready, chain = (s.sem(n) for n in ("source_ready", "prod_ready", "scaled_ready", "ones_ready", "chain"))
        block = ctx.enter_context(nc.Block())

        @block.gpsimd
        def _(pool):
            gather_rows(pool, w.rows, w.index, d["table"], w.index_ready, w.rows_in)

        @block.sync
        def _(sp):
            pass_sync(sp, d, w)

        @block.scalar
        def _(act):
            act.sem_inc(source_ready, BUFS)

            def keep_source(c, r, b):
                act.wait_ge(w.both_t, upto(c))
                act.wait_ge(prod_ready, upto(c))
                act.wait_ge(scaled_ready, upto(c, 2))
                nc.scalar.copy(source[:, b % 2, :], w.ps_r[:, b % 2, :]).then_inc(source_ready, 1)
            pass_scalar(nc, act, m, w, keep_source)

        @block.tensor
        def _(pe):
            pe.wait_ge(ones_ready, 1)

            def free(c):
                pe.wait_ge(source_ready, upto(c, 2))
                pe.wait_ge(prod_ready, upto(c, 2))

            def dots(c, r, b):
                pe.wait_ge(prod_ready, upto(c))
                pe.wait_ge(scaled_ready, upto(c, 2))
                nc.tensor.matmul(w.ps_m[:, b % 2, :], ones[:, :], prod[:, b % 2, :], start=True, stop=True).then_inc(w.message, 1)
            pass_tensor(nc, pe, m, w, free, dots)

        @block.vector
        def _(dve):
            link = linker(dve, chain)
            link(nc.vector.memset(ones[:, :], 0.0))
            nc.vector.memset(ones[0:D, 0:D], 1.0)
            nc.vector.memset(ones[D:P, D:P], 1.0).then_inc(ones_ready, 1)
            nc.vector.memset(w.dest[:, 1, PER * P - 1:PER * P], 0.0).then_inc(w.dest_ready, BUFS)
            nc.vector.memset(w.run[:, 1, PER * P - 1:PER * P], 0.0).then_inc(w.run_ready, BUFS)
            dve.sem_inc(prod_ready, BUFS)
            dve.sem_inc(scaled_ready, BUFS)

            def used(c):
                dve.wait_ge(prod_ready, upto(c, 2))

            def step(k, j):
                if now := stage(k, j, 1):
                    c, r, b = now
                    dve.wait_ge(w.message, upto(c))
                    dve.wait_ge(source_ready, upto(c))
                    dve.wait_ge(w.run_ready, upto(c, 2))
                    nc.vector.tensor_tensor(scaled[:, b % 2, :], source[:, b % 2, :], w.ps_m[:, b % 2, :], ALU.mult).then_inc(scaled_ready, 1)
                    dve.wait_ge(scaled_ready, upto(c))
                    dve.wait_ge(w.back_t, upto(c, 2))
                    dve.wait_ge(w.run_ready, upto(c, 1))
                    nc.vector.tensor_tensor_scan(w.run[:, b % 2, :], w.flags[:, b, 0, :], scaled[:, b % 2, :],
                                                 w.run[:, (b + 1) % 2, PER * P - 1:PER * P], ALU.mult, ALU.add).then_inc(w.run_ready, 1)
                if now := stage(k, j, 0):
                    c, r, b = now
                    spread_dest(nc, dve, w, c, r, b, used)
                    dve.wait_ge(w.message, upto(c, 2))
                    nc.vector.tensor_tensor(prod[:, b % 2, :], w.dest[:, b % 2, :], w.ps_r[:, b % 2, :], ALU.mult).then_inc(prod_ready, 1)
            loop_steps(dve, step, 1)


def phase_dot_out(nc, m, d):
    with ExitStack() as ctx:
        s = Scope(nc, ctx, "do")
        node = s.sb("node", [P, NB, D])
        wide = s.sb("wide", [P, NB, D])
        carried = s.sb("carried", [P, D])
        node_t = s.sb("node_t", [D, 2, P])
        fc = s.sb("fc", [D, D])
        ps_t = s.ps("ps_t", [D, 2, 512])
        ps_y = s.ps("ps_y", [P, 2, 512])
        loaded, summed, transposed, taken, done, x_ready, out_done, chain = (s.sem(n) for n in ("loaded", "summed", "transposed", "taken", "done", "x_ready", "out_done", "chain"))
        G = len(SETS)
        gathered = [s.sem(f"gathered{g}") for g in range(G)]
        block = ctx.enter_context(nc.Block())

        @block.gpsimd
        def _(pool):
            gather_sums(pool, m, d, node, gathered, SETS)

        @block.sync
        def _(sp):
            sp.dma_start(fc[:, :], d["fc_t"]).then_inc(loaded, 16)
            sp.dma_start(carried[:, :], d["sums"][ENDROW:ENDROW + 1, :].broadcast_to([P, D])).then_inc(loaded, 16)
            sp.wait_ge(x_ready, G)
            sp.dma_start(d["out"][0:LASTP * NB, :].rearrange("(p b) w -> p b w", b=NB), m.x[0:LASTP, :, :]).then_inc(out_done, 16)
            sp.dma_start(d["out"][LASTP * NB:N, :].rearrange("(p b) w -> p b w", b=LASTB), m.x[LASTP:LASTP + 1, 0:LASTB, :]).then_inc(out_done, 16)
            sp.wait_ge(out_done, 32)

        @block.scalar
        def _(act):
            for b in range(NB):
                act.wait_ge(transposed, b + 1)
                if b >= 2:
                    act.wait_ge(done, b - 1)
                nc.scalar.copy(node_t[:, b % 2, :], ps_t[:, b % 2, 0:P]).then_inc(taken, 1)

        @block.tensor
        def _(pe):
            pe.wait_ge(loaded, 32)
            for b in range(NB + 1):
                if b < NB:
                    if b % 8 == 0:
                        pe.wait_ge(summed, b // 8 + 1)
                    if b >= 2:
                        pe.wait_ge(taken, b - 1)
                    nc.tensor.transpose(ps_t[:, b % 2, 0:P], node[:, b, :], m.ident[:, :]).then_inc(transposed, 1)
                if b >= 1:
                    q = b - 1
                    pe.wait_ge(taken, b)
                    if q >= 16 and q % 8 == 0:
                        pe.wait_ge(x_ready, q // 8 - 1)
                    nc.tensor.matmul(ps_y[:, q // 8 % 2, q % 8 * D:(q % 8 + 1) * D], node_t[:, q % 2, :], fc[:, :], start=True, stop=True).then_inc(done, 1)

        @block.vector
        def _(dve):
            dve.wait_ge(loaded, 32)
            for g in range(G + 1):
                if g < G:
                    lo, hi = SETS[g]
                    dve.wait_ge(gathered[g], 16 * (hi - lo))
                    join_sum(nc, lambda ins, i: (ins.then_inc(chain, 1), dve.wait_ge(chain, 2 * g + i + 1)), m, node, carried, wide, lo, hi)
                    dve.sem_inc(summed, 1)
                if g >= 1:
                    lo, hi = SETS[g - 1]
                    dve.wait_ge(done, hi)
                    nc.vector.tensor_tensor(m.x[:, lo:hi, :], m.x[:, lo:hi, :], ps_y[:, (g - 1) % 2, 0:(hi - lo) * D].rearrange("p (b w) -> p b w", w=D), ALU.add).then_inc(x_ready, 1)


def build(nc, d):
    def dram(name, shape, dt=F32):
        return nc.dram_tensor(name, shape, dt, kind="Internal").ap()

    d["flags"] = dram("flags", [KINDS, ROWS], BF16)
    d["table0"] = dram("table0", [NPAD, TW])
    d["table"] = dram("table", [NPAD, D])
    d["sums_heads"] = dram("sums_heads", [ROWS + NPAD, SW])
    d["filled4"] = dram("filled4", [ROWS + NPAD, AW])
    d["node4"] = dram("node4", [NPAD, AW])
    d["edge_sums"] = dram("edge_sums", [ROWS, AW])
    d["sums"] = dram("sums", [ROWS + NPAD, D])
    d["filled"] = dram("filled", [ROWS + NPAD, D])
    d["start_of"] = dram("start_of", [NPAD, 1], I32)
    with ExitStack() as ctx:
        m = Memory(Scope(nc, ctx, "all"))
        with ExitStack() as gat:
            edge = Edges(Scope(nc, gat, "gat"))
            phase_flags(nc, m, d)
            phase_table(nc, m, d, edge)
            phase_dest(nc, m, d, edge)
            phase_gat(nc, m, d, edge)
        phase_gat_out(nc, m, d)
        phase_light(nc, m, d)
        phase_edge_tables(nc, m, d)
        phase_edge_max(nc, m, d)
        phase_edge_out(nc, m, d)
        phase_dot(nc, m, d)
        phase_dot_out(nc, m, d)


def kernel(**inputs):
    import concourse.bacc as bacc
    import numpy as np
    from concourse.bass_utils import run_bass_kernel_spmd

    a = {k: np.asarray(v) for k, v in inputs.items()}
    pad = TILES * P - E
    dst = np.concatenate([a["dst"], np.full(pad, N, np.int32)])

    def columns(v):
        t = v.reshape(STREAMS, CHUNKS, PER, P, *v.shape[1:])
        return np.ascontiguousarray(np.moveaxis(t, (3, 1, 0, 2), (0, 1, 2, 3)).reshape(P, -1))

    arrays = {
        "x": a["x"],
        "dst_rows": np.concatenate([np.full(1, -1, np.int32), dst, np.full(1, N + 1, np.int32)]),
        "dst_tiles": dst.reshape(TILES, P),
        "tile_first": np.ascontiguousarray(dst[::P].reshape(GROUPS, GROUP)),
        "group_first": np.ascontiguousarray(dst[::P * GROUP]),
        "src_cols": columns(np.concatenate([a["src"], np.zeros(pad, np.int32)])),
        "attr_cols": columns(np.concatenate([a["edge_attr_5"], np.zeros((pad, EDIM), np.float32)])),
        "lin_w": a["L0_gnn_lin_w"], "lin_wt": np.ascontiguousarray(a["L0_gnn_lin_w"].T),
        "att_src": a["L0_gnn_att_src"], "att_dst": a["L0_gnn_att_dst"], "att_edge": a["L0_gnn_att_edge"],
        "lin_edge_w": a["L0_gnn_lin_edge_w"], "gat_bias": a["L0_gnn_gat_bias"],
        "w1": a["L0_gnn_w1"], "b1": a["L0_gnn_b1"], "ln1_g": a["L0_gnn_ln1_g"], "ln1_b": a["L0_gnn_ln1_b"],
        "w2": a["L0_gnn_w2"], "b2": a["L0_gnn_b2"], "ln2_g": a["L0_gnn_ln2_g"], "ln2_b": a["L0_gnn_ln2_b"],
        "w1e": a["L2_gnn_W1"], "b1e": a["L2_gnn_b1"], "w2e": a["L2_gnn_W2"], "b2e": a["L2_gnn_b2"],
        "fc_t": np.ascontiguousarray(a["L3_gnn_fc_weight"].T),
    }
    nc = bacc.Bacc("TRN2", target_bir_lowering=False, num_devices=1)
    d = {}
    for name, v in arrays.items():
        d[name] = nc.dram_tensor(f"in_{name}", v.shape, mybir.dt.from_np(v.dtype), kind="ExternalInput").ap()
    d["out"] = nc.dram_tensor("out", (N, D), F32, kind="ExternalOutput").ap()
    build(nc, d)
    got = run_bass_kernel_spmd(nc, [{f"in_{k}": v for k, v in arrays.items()}], core_ids=[0])
    return got.results[0]["out"]
```
